# Optimizing a Trainium2 kernel written in Bass

```python
import numpy as np
import jax
import jax.numpy as jnp

def _softmax(x, axis=-1):
    return jax.nn.softmax(x, axis=axis)

def _gelu(x):
    return jax.nn.gelu(x, approximate=True)

def _silu(x):
    return jax.nn.silu(x)

def _sigmoid(x):
    return jax.nn.sigmoid(x)

def _layernorm(x, axis=-1, eps=1e-05):
    m = jnp.mean(x, axis=axis, keepdims=True)
    v = jnp.var(x, axis=axis, keepdims=True)
    return (x - m) / jnp.sqrt(v + eps)

def _scatter_add(tgt, idx, src, axis=0):
    return tgt.at[idx].add(src)

def _segment_sum(src, seg, n):
    return jax.ops.segment_sum(src, seg, n)
kernel_name = 'mk_vit_tower_d2_tok_img256_r4_307121'

def setup_inputs(seed: int=0):
    np.random.seed(seed)
    _w = jnp.asarray

    def _rec_inputs():
        import jax
        import jax.numpy as jnp
        _rk = jax.random.key(seed)
        x = 9.04603e-05 + 1.00016 * jax.random.normal(jax.random.fold_in(_rk, 1), (8, 1, 224, 224), jnp.float32)
        return x
    x = _rec_inputs()

    def _L0_tok_setup():
        import jax, jax.numpy as jnp
        import numpy as np
        WS = 7
        H = W = 56
        C = 64
        NH = 8
        HD = C // NH
        SCALE = HD ** (-0.5)
        SHIFT = WS // 2
        N = WS * WS

        def _rel_pos_index():
            coords = np.stack(np.meshgrid(np.arange(WS), np.arange(WS), indexing='ij'))
            cf = coords.reshape(2, -1)
            rel = (cf[:, :, None] - cf[:, None, :]).transpose(1, 2, 0).copy()
            rel[..., 0] += WS - 1
            rel[..., 1] += WS - 1
            rel[..., 0] *= 2 * WS - 1
            return jnp.array(rel.sum(-1))

        def _attn_mask():
            img = np.zeros((H, W), np.int32)
            cnt = 0
            for h in (slice(0, -WS), slice(-WS, -SHIFT), slice(-SHIFT, None)):
                for w in (slice(0, -WS), slice(-WS, -SHIFT), slice(-SHIFT, None)):
                    cnt += 1
                    img[h, w] = cnt
            mw = img.reshape(H // WS, WS, W // WS, WS).transpose(0, 2, 1, 3).reshape(-1, N)
            diff = mw[:, None, :] - mw[:, :, None]
            return jnp.array(np.where(diff != 0, -100.0, 0.0).astype(np.float32))

        def _layernorm(x, g, b):
            m = x.mean(-1, keepdims=True)
            v = ((x - m) ** 2).mean(-1, keepdims=True)
            return (x - m) * jax.lax.rsqrt(v + 1e-05) * g + b

        def _window_partition(x):
            B = x.shape[0]
            x = x.reshape(B, H // WS, WS, W // WS, WS, C).transpose(0, 1, 3, 2, 4, 5)
            return x.reshape(-1, N, C)

        def _window_reverse(xw, B):
            x = xw.reshape(B, H // WS, W // WS, WS, WS, C).transpose(0, 1, 3, 2, 4, 5)
            return x.reshape(B, H, W, C)

        def _swin_block(x, p, shift, rpi, amask):
            B = x.shape[0]
            shortcut = x
            h = _layernorm(x, p['n1g'], p['n1b']).reshape(B, H, W, C)
            if shift > 0:
                h = jnp.roll(h, (-shift, -shift), axis=(1, 2))
            xw = _window_partition(h)
            B_ = xw.shape[0]
            qkv = (xw @ p['qkv_w'].T + p['qkv_b']).reshape(B_, N, 3, NH, HD).transpose(2, 0, 3, 1, 4)
            q, k, v = (qkv[0], qkv[1], qkv[2])
            attn = jnp.einsum('bhnd,bhmd->bhnm', q * SCALE, k)
            attn = attn + p['rpb'][rpi].transpose(2, 0, 1)[None]
            if shift > 0:
                nW = amask.shape[0]
                attn = attn.reshape(B_ // nW, nW, NH, N, N) + amask[None, :, None]
                attn = attn.reshape(B_, NH, N, N)
            attn = jax.nn.softmax(attn, axis=-1)
            o = jnp.einsum('bhnm,bhmd->bhnd', attn, v).transpose(0, 2, 1, 3).reshape(B_, N, C)
            o = o @ p['proj_w'].T + p['proj_b']
            h = _window_reverse(o, B)
            if shift > 0:
                h = jnp.roll(h, (shift, shift), axis=(1, 2))
            x = shortcut + h.reshape(B, H * W, C)
            y = _layernorm(x, p['n2g'], p['n2b'])
            y = jax.nn.gelu(y @ p['w1'].T + p['b1'], approximate=False)
            return x + y @ p['w2'].T + p['b2']
        key = jax.random.key(seed)
        ks = jax.random.split(key, 8)
        s = 0.02
        return {'x': jax.random.normal(ks[0], (16, 1, 224, 224), jnp.float32), 'pe_w': jax.random.normal(ks[1], (C, 1, 4, 4), jnp.float32) * s, 'pe_b': jnp.zeros((C,), jnp.float32), 'pe_ng': jnp.ones((C,), jnp.float32), 'pe_nb': jnp.zeros((C,), jnp.float32), 'n1g': jnp.ones((2, C), jnp.float32), 'n1b': jnp.zeros((2, C), jnp.float32), 'qkv_w': jax.random.normal(ks[2], (2, 3 * C, C), jnp.float32) * s, 'qkv_b': jnp.zeros((2, 3 * C), jnp.float32), 'rpb': jax.random.normal(ks[3], (2, (2 * WS - 1) ** 2, NH), jnp.float32) * s, 'proj_w': jax.random.normal(ks[4], (2, C, C), jnp.float32) * s, 'proj_b': jnp.zeros((2, C), jnp.float32), 'n2g': jnp.ones((2, C), jnp.float32), 'n2b': jnp.zeros((2, C), jnp.float32), 'w1': jax.random.normal(ks[5], (2, 4 * C, C), jnp.float32) * s, 'b1': jnp.zeros((2, 4 * C), jnp.float32), 'w2': jax.random.normal(ks[6], (2, C, 4 * C), jnp.float32) * s, 'b2': jnp.zeros((2, C), jnp.float32)}
    _L0_tok_all = _L0_tok_setup()
    _L0_tok_in = {k: v for k, v in _L0_tok_all.items() if k in ('pe_w', 'pe_b', 'pe_ng', 'pe_nb', 'n1g', 'n1b', 'qkv_w', 'qkv_b', 'rpb', 'proj_w', 'proj_b', 'n2g', 'n2b', 'w1', 'b1', 'w2', 'b2')}
    del _L0_tok_all

    def _L0_attn_setup():
        import jax, jax.numpy as jnp
        import numpy as np
        B, S, D = (4, 1024, 64)
        key = jax.random.key(seed)
        k1, k2, k3, k4 = jax.random.split(key, 4)
        inputs = jax.random.normal(k1, (B, S, D), dtype=jnp.float32)
        Wq = jax.random.normal(k2, (D, D), dtype=jnp.float32) * 0.05
        Wk = jax.random.normal(k3, (D, D), dtype=jnp.float32) * 0.05
        Wv = jax.random.normal(k4, (D, D), dtype=jnp.float32) * 0.05
        return {'inputs': inputs, 'Wq': Wq, 'Wk': Wk, 'Wv': Wv}
    _L0_attn_all = _L0_attn_setup()
    _L0_attn_in = {k: v for k, v in _L0_attn_all.items() if k in ('Wq', 'Wk', 'Wv')}
    del _L0_attn_all

    def _L0_ffn_setup():
        import math
        import jax, jax.numpy as jnp
        import numpy as np
        CAPACITY_FACTOR = 1.25
        key = jax.random.key(seed)
        ks = jax.random.split(key, 5)
        B, L, D, F, E = (8, 2048, 64, 256, 8)
        h = jax.random.normal(ks[0], (B, L, D), dtype=jnp.float32)
        gate_w = jax.random.normal(ks[1], (D, E), dtype=jnp.float32) * 0.02
        gate_b = jnp.zeros((E,), dtype=jnp.float32)
        w1 = jax.random.normal(ks[2], (E, D, F), dtype=jnp.float32) * (1.0 / math.sqrt(D))
        b1 = jnp.zeros((E, F), dtype=jnp.float32)
        w2 = jax.random.normal(ks[3], (E, F, D), dtype=jnp.float32) * (1.0 / math.sqrt(F))
        b2 = jnp.zeros((E, D), dtype=jnp.float32)
        return {'h': h, 'gate_w': gate_w, 'gate_b': gate_b, 'w1': w1, 'b1': b1, 'w2': w2, 'b2': b2}
    _L0_ffn_all = _L0_ffn_setup()
    _L0_ffn_in = {k: v for k, v in _L0_ffn_all.items() if k in ('gate_w', 'gate_b', 'w1', 'b1', 'w2', 'b2')}
    del _L0_ffn_all

    def _L1_attn_setup():
        import jax, jax.numpy as jnp
        import numpy as np
        B, T, C, HR = (8, 1024, 64, 4)
        N_LAYER, LAYER_ID = (12, 3)
        HID = HR * C

        def _fancy_decay_first():
            r01 = LAYER_ID / (N_LAYER - 1)
            h = np.arange(C, dtype=np.float32)
            decay = -5.0 + 8.0 * (h / (C - 1)) ** (0.7 + 1.3 * r01)
            zig = (np.arange(1, C + 1) % 3 - 1).astype(np.float32) * 0.5
            first = np.float32(np.log(0.3)) + zig
            return (jnp.asarray(decay, jnp.float32), jnp.asarray(first, jnp.float32))

        def _ln(x, g, b):
            m = jnp.mean(x, axis=-1, keepdims=True)
            v = jnp.var(x, axis=-1, keepdims=True)
            return (x - m) * jax.lax.rsqrt(v + 1e-05) * g + b

        def _wkv(w, u, k, v):
            Bb, Tt, Cc = k.shape
            kT = jnp.swapaxes(k, 0, 1)
            vT = jnp.swapaxes(v, 0, 1)

            def step(carry, kv):
                p, q, o = carry
                kt, vt = kv
                no = jnp.maximum(o, u + kt)
                A = jnp.exp(o - no)
                E = jnp.exp(u + kt - no)
                y = (A * p + E * vt) / (A * q + E)
                no2 = jnp.maximum(w + o, kt)
                A2 = jnp.exp(w + o - no2)
                E2 = jnp.exp(kt - no2)
                return ((A2 * p + E2 * vt, A2 * q + E2, no2), y)
            init = (jnp.zeros((Bb, Cc), k.dtype), jnp.zeros((Bb, Cc), k.dtype), jnp.full((Bb, Cc), -1e+38, k.dtype))
            _, yT = jax.lax.scan(step, init, (kT, vT))
            return jnp.swapaxes(yT, 0, 1)
        key = jax.random.key(seed)
        ks = jax.random.split(key, 12)
        s = 0.02
        decay, first = _fancy_decay_first()
        return {'x': jax.random.normal(ks[0], (B, T, C), jnp.float32), 'Wk': jax.random.normal(ks[1], (C, C), jnp.float32) * s, 'Wv': jax.random.normal(ks[2], (C, C), jnp.float32) * s, 'Wr': jax.random.normal(ks[3], (C, C), jnp.float32) * s, 'Wo': jax.random.normal(ks[4], (C, C), jnp.float32) * s, 'Wk_ffn': jax.random.normal(ks[5], (C, HID), jnp.float32) * s, 'Wv_ffn': jax.random.normal(ks[6], (HID, C), jnp.float32) * s, 'Wr_ffn': jax.random.normal(ks[7], (C, C), jnp.float32) * s, 'g1': 1.0 + 0.1 * jax.random.normal(ks[8], (C,), jnp.float32), 'b1': 0.1 * jax.random.normal(ks[9], (C,), jnp.float32), 'g2': 1.0 + 0.1 * jax.random.normal(ks[10], (C,), jnp.float32), 'b2': 0.1 * jax.random.normal(ks[11], (C,), jnp.float32), 'spatial_decay': decay, 'spatial_first': first}
    _L1_attn_all = _L1_attn_setup()
    _L1_attn_in = {k: v for k, v in _L1_attn_all.items() if k in ('Wk', 'Wv', 'Wr', 'Wo', 'Wk_ffn', 'Wv_ffn', 'Wr_ffn', 'g1', 'b1', 'g2', 'b2', 'spatial_decay', 'spatial_first')}
    del _L1_attn_all

    def _L1_ffn_setup():
        import jax, jax.numpy as jnp
        import numpy as np
        B, T, IN_DIM = (64, 64, 64)
        HID, OUT_DIM = (128, 64)
        N_LAYERS, N_EXPERTS, N_SHARED = (2, 16, 1)
        key = jax.random.key(seed)
        ks = jax.random.split(key, 10)
        s = 0.02
        x = jax.random.normal(ks[0], (B, T, IN_DIM), dtype=jnp.float32)
        route_id = jax.random.randint(ks[1], (B,), 0, N_EXPERTS)
        Wi = jax.random.normal(ks[2], (HID, IN_DIM), dtype=jnp.float32) * s
        bi = jnp.zeros((HID,), dtype=jnp.float32)
        Wr = jax.random.normal(ks[3], (N_LAYERS, N_EXPERTS, HID, HID), dtype=jnp.float32) * s
        br = jax.random.normal(ks[4], (N_LAYERS, N_EXPERTS, HID), dtype=jnp.float32) * s
        Ws = jax.random.normal(ks[5], (N_LAYERS, N_SHARED, HID, HID), dtype=jnp.float32) * s
        bs = jax.random.normal(ks[6], (N_LAYERS, N_SHARED, HID), dtype=jnp.float32) * s
        Wo = jax.random.normal(ks[7], (OUT_DIM, HID), dtype=jnp.float32) * s
        bo = jnp.zeros((OUT_DIM,), dtype=jnp.float32)
        return {'x': x, 'route_id': route_id, 'Wi': Wi, 'bi': bi, 'Wr': Wr, 'br': br, 'Ws': Ws, 'bs': bs, 'Wo': Wo, 'bo': bo}
    _L1_ffn_all = _L1_ffn_setup()
    _L1_ffn_in = {k: v for k, v in _L1_ffn_all.items() if k in ('route_id', 'Wi', 'bi', 'Wr', 'br', 'Ws', 'bs', 'Wo', 'bo')}
    del _L1_ffn_all
    return {'x': x, 'L0_tok_pe_w': _L0_tok_in['pe_w'], 'L0_tok_pe_b': _L0_tok_in['pe_b'], 'L0_tok_pe_ng': _L0_tok_in['pe_ng'], 'L0_tok_pe_nb': _L0_tok_in['pe_nb'], 'L0_tok_n1g': _L0_tok_in['n1g'], 'L0_tok_n1b': _L0_tok_in['n1b'], 'L0_tok_qkv_w': _L0_tok_in['qkv_w'], 'L0_tok_qkv_b': _L0_tok_in['qkv_b'], 'L0_tok_rpb': _L0_tok_in['rpb'], 'L0_tok_proj_w': _L0_tok_in['proj_w'], 'L0_tok_proj_b': _L0_tok_in['proj_b'], 'L0_tok_n2g': _L0_tok_in['n2g'], 'L0_tok_n2b': _L0_tok_in['n2b'], 'L0_tok_w1': _L0_tok_in['w1'], 'L0_tok_b1': _L0_tok_in['b1'], 'L0_tok_w2': _L0_tok_in['w2'], 'L0_tok_b2': _L0_tok_in['b2'], 'L0_attn_Wq': _L0_attn_in['Wq'], 'L0_attn_Wk': _L0_attn_in['Wk'], 'L0_attn_Wv': _L0_attn_in['Wv'], 'L0_ffn_gate_w': _L0_ffn_in['gate_w'], 'L0_ffn_gate_b': _L0_ffn_in['gate_b'], 'L0_ffn_w1': _L0_ffn_in['w1'], 'L0_ffn_b1': _L0_ffn_in['b1'], 'L0_ffn_w2': _L0_ffn_in['w2'], 'L0_ffn_b2': _L0_ffn_in['b2'], 'L1_attn_Wk': _L1_attn_in['Wk'], 'L1_attn_Wv': _L1_attn_in['Wv'], 'L1_attn_Wr': _L1_attn_in['Wr'], 'L1_attn_Wo': _L1_attn_in['Wo'], 'L1_attn_Wk_ffn': _L1_attn_in['Wk_ffn'], 'L1_attn_Wv_ffn': _L1_attn_in['Wv_ffn'], 'L1_attn_Wr_ffn': _L1_attn_in['Wr_ffn'], 'L1_attn_g1': _L1_attn_in['g1'], 'L1_attn_b1': _L1_attn_in['b1'], 'L1_attn_g2': _L1_attn_in['g2'], 'L1_attn_b2': _L1_attn_in['b2'], 'L1_attn_spatial_decay': _L1_attn_in['spatial_decay'], 'L1_attn_spatial_first': _L1_attn_in['spatial_first'], 'L1_ffn_route_id': _L1_ffn_in['route_id'], 'L1_ffn_Wi': _L1_ffn_in['Wi'], 'L1_ffn_bi': _L1_ffn_in['bi'], 'L1_ffn_Wr': _L1_ffn_in['Wr'], 'L1_ffn_br': _L1_ffn_in['br'], 'L1_ffn_Ws': _L1_ffn_in['Ws'], 'L1_ffn_bs': _L1_ffn_in['bs'], 'L1_ffn_Wo': _L1_ffn_in['Wo'], 'L1_ffn_bo': _L1_ffn_in['bo']}

def reference(x, L0_tok_pe_w, L0_tok_pe_b, L0_tok_pe_ng, L0_tok_pe_nb, L0_tok_n1g, L0_tok_n1b, L0_tok_qkv_w, L0_tok_qkv_b, L0_tok_rpb, L0_tok_proj_w, L0_tok_proj_b, L0_tok_n2g, L0_tok_n2b, L0_tok_w1, L0_tok_b1, L0_tok_w2, L0_tok_b2, L0_attn_Wq, L0_attn_Wk, L0_attn_Wv, L0_ffn_gate_w, L0_ffn_gate_b, L0_ffn_w1, L0_ffn_b1, L0_ffn_w2, L0_ffn_b2, L1_attn_Wk, L1_attn_Wv, L1_attn_Wr, L1_attn_Wo, L1_attn_Wk_ffn, L1_attn_Wv_ffn, L1_attn_Wr_ffn, L1_attn_g1, L1_attn_b1, L1_attn_g2, L1_attn_b2, L1_attn_spatial_decay, L1_attn_spatial_first, L1_ffn_route_id, L1_ffn_Wi, L1_ffn_bi, L1_ffn_Wr, L1_ffn_br, L1_ffn_Ws, L1_ffn_bs, L1_ffn_Wo, L1_ffn_bo):
    import jax
    import jax.numpy as jnp

    def _L0_tok_ref(x, pe_w, pe_b, pe_ng, pe_nb, n1g, n1b, qkv_w, qkv_b, rpb, proj_w, proj_b, n2g, n2b, w1, b1, w2, b2):
        import jax, jax.numpy as jnp
        import numpy as np
        WS = 7
        H = W = 56
        C = 64
        NH = 8
        HD = C // NH
        SCALE = HD ** (-0.5)
        SHIFT = WS // 2
        N = WS * WS

        def _rel_pos_index():
            coords = np.stack(np.meshgrid(np.arange(WS), np.arange(WS), indexing='ij'))
            cf = coords.reshape(2, -1)
            rel = (cf[:, :, None] - cf[:, None, :]).transpose(1, 2, 0).copy()
            rel[..., 0] += WS - 1
            rel[..., 1] += WS - 1
            rel[..., 0] *= 2 * WS - 1
            return jnp.array(rel.sum(-1))

        def _attn_mask():
            img = np.zeros((H, W), np.int32)
            cnt = 0
            for h in (slice(0, -WS), slice(-WS, -SHIFT), slice(-SHIFT, None)):
                for w in (slice(0, -WS), slice(-WS, -SHIFT), slice(-SHIFT, None)):
                    cnt += 1
                    img[h, w] = cnt
            mw = img.reshape(H // WS, WS, W // WS, WS).transpose(0, 2, 1, 3).reshape(-1, N)
            diff = mw[:, None, :] - mw[:, :, None]
            return jnp.array(np.where(diff != 0, -100.0, 0.0).astype(np.float32))

        def _layernorm(x, g, b):
            m = x.mean(-1, keepdims=True)
            v = ((x - m) ** 2).mean(-1, keepdims=True)
            return (x - m) * jax.lax.rsqrt(v + 1e-05) * g + b

        def _window_partition(x):
            B = x.shape[0]
            x = x.reshape(B, H // WS, WS, W // WS, WS, C).transpose(0, 1, 3, 2, 4, 5)
            return x.reshape(-1, N, C)

        def _window_reverse(xw, B):
            x = xw.reshape(B, H // WS, W // WS, WS, WS, C).transpose(0, 1, 3, 2, 4, 5)
            return x.reshape(B, H, W, C)

        def _swin_block(x, p, shift, rpi, amask):
            B = x.shape[0]
            shortcut = x
            h = _layernorm(x, p['n1g'], p['n1b']).reshape(B, H, W, C)
            if shift > 0:
                h = jnp.roll(h, (-shift, -shift), axis=(1, 2))
            xw = _window_partition(h)
            B_ = xw.shape[0]
            qkv = (xw @ p['qkv_w'].T + p['qkv_b']).reshape(B_, N, 3, NH, HD).transpose(2, 0, 3, 1, 4)
            q, k, v = (qkv[0], qkv[1], qkv[2])
            attn = jnp.einsum('bhnd,bhmd->bhnm', q * SCALE, k)
            attn = attn + p['rpb'][rpi].transpose(2, 0, 1)[None]
            if shift > 0:
                nW = amask.shape[0]
                attn = attn.reshape(B_ // nW, nW, NH, N, N) + amask[None, :, None]
                attn = attn.reshape(B_, NH, N, N)
            attn = jax.nn.softmax(attn, axis=-1)
            o = jnp.einsum('bhnm,bhmd->bhnd', attn, v).transpose(0, 2, 1, 3).reshape(B_, N, C)
            o = o @ p['proj_w'].T + p['proj_b']
            h = _window_reverse(o, B)
            if shift > 0:
                h = jnp.roll(h, (shift, shift), axis=(1, 2))
            x = shortcut + h.reshape(B, H * W, C)
            y = _layernorm(x, p['n2g'], p['n2b'])
            y = jax.nn.gelu(y @ p['w1'].T + p['b1'], approximate=False)
            return x + y @ p['w2'].T + p['b2']
        B = x.shape[0]
        h = jax.lax.conv_general_dilated(x, pe_w, (4, 4), 'VALID', dimension_numbers=('NCHW', 'OIHW', 'NCHW'))
        h = h + pe_b[None, :, None, None]
        t = h.reshape(B, C, H * W).transpose(0, 2, 1)
        t = _layernorm(t, pe_ng, pe_nb)
        rpi = _rel_pos_index()
        amask = _attn_mask()
        for i, shift in enumerate((0, SHIFT)):
            p = {'n1g': n1g[i], 'n1b': n1b[i], 'qkv_w': qkv_w[i], 'qkv_b': qkv_b[i], 'rpb': rpb[i], 'proj_w': proj_w[i], 'proj_b': proj_b[i], 'n2g': n2g[i], 'n2b': n2b[i], 'w1': w1[i], 'b1': b1[i], 'w2': w2[i], 'b2': b2[i]}
            t = _swin_block(t, p, shift, rpi, amask)
        return t

    def _L0_attn_ref(inputs, Wq, Wk, Wv):
        import jax, jax.numpy as jnp
        import numpy as np
        B, S, D = (4, 1024, 64)
        d = inputs.shape[-1]
        Q = jnp.einsum('bsd,de->bse', inputs, Wq)
        K = jnp.einsum('bsd,de->bse', inputs, Wk)
        V = jnp.einsum('bsd,de->bse', inputs, Wv)
        scale = 1.0 / jnp.sqrt(jnp.asarray(d, dtype=inputs.dtype))
        scores = jnp.einsum('bqe,bke->bqk', Q, K) * scale
        attn = jax.nn.softmax(scores, axis=-1)
        return jnp.einsum('bqk,bke->bqe', attn, V)

    def _L0_ffn_ref(h, gate_w, gate_b, w1, b1, w2, b2):
        import math
        import jax, jax.numpy as jnp
        import numpy as np
        CAPACITY_FACTOR = 1.25
        B, L, D = h.shape
        E = gate_w.shape[1]
        T = B * L
        C = max(1, math.ceil(CAPACITY_FACTOR * T / E))
        x = h.reshape(T, D)
        logits = x @ gate_w + gate_b
        probs = jax.nn.softmax(logits, axis=-1)
        idx = jnp.argmax(probs, axis=-1)
        prb = jnp.take_along_axis(probs, idx[:, None], axis=1)[:, 0]
        one_hot = jax.nn.one_hot(idx, E, dtype=jnp.float32)
        pos = (jnp.cumsum(one_hot, axis=0) * one_hot).sum(-1).astype(jnp.int32) - 1
        kept = pos < C
        pos_safe = jnp.where(kept, pos, C)
        buf = jnp.zeros((E, C, D), dtype=h.dtype).at[idx, pos_safe].set(x, mode='drop')
        hmid = jax.nn.relu(jnp.einsum('ecd,edf->ecf', buf, w1) + b1[:, None, :])
        ybuf = jnp.einsum('ecf,efd->ecd', hmid, w2) + b2[:, None, :]
        pos_g = jnp.minimum(pos, C - 1)
        y_tok = ybuf[idx, pos_g] * (prb * kept)[:, None]
        y = y_tok.reshape(B, L, D)
        y = jnp.nan_to_num(y, nan=0.0, posinf=10000.0, neginf=-10000.0)
        return y

    def _L1_attn_ref(x, Wk, Wv, Wr, Wo, Wk_ffn, Wv_ffn, Wr_ffn, g1, b1, g2, b2, spatial_decay, spatial_first):
        import jax, jax.numpy as jnp
        import numpy as np
        B, T, C, HR = (8, 1024, 64, 4)
        N_LAYER, LAYER_ID = (12, 3)
        HID = HR * C

        def _fancy_decay_first():
            r01 = LAYER_ID / (N_LAYER - 1)
            h = np.arange(C, dtype=np.float32)
            decay = -5.0 + 8.0 * (h / (C - 1)) ** (0.7 + 1.3 * r01)
            zig = (np.arange(1, C + 1) % 3 - 1).astype(np.float32) * 0.5
            first = np.float32(np.log(0.3)) + zig
            return (jnp.asarray(decay, jnp.float32), jnp.asarray(first, jnp.float32))

        def _ln(x, g, b):
            m = jnp.mean(x, axis=-1, keepdims=True)
            v = jnp.var(x, axis=-1, keepdims=True)
            return (x - m) * jax.lax.rsqrt(v + 1e-05) * g + b

        def _wkv(w, u, k, v):
            Bb, Tt, Cc = k.shape
            kT = jnp.swapaxes(k, 0, 1)
            vT = jnp.swapaxes(v, 0, 1)

            def step(carry, kv):
                p, q, o = carry
                kt, vt = kv
                no = jnp.maximum(o, u + kt)
                A = jnp.exp(o - no)
                E = jnp.exp(u + kt - no)
                y = (A * p + E * vt) / (A * q + E)
                no2 = jnp.maximum(w + o, kt)
                A2 = jnp.exp(w + o - no2)
                E2 = jnp.exp(kt - no2)
                return ((A2 * p + E2 * vt, A2 * q + E2, no2), y)
            init = (jnp.zeros((Bb, Cc), k.dtype), jnp.zeros((Bb, Cc), k.dtype), jnp.full((Bb, Cc), -1e+38, k.dtype))
            _, yT = jax.lax.scan(step, init, (kT, vT))
            return jnp.swapaxes(yT, 0, 1)
        Tlen = x.shape[1]
        h = _ln(x, g1, b1)
        k = h @ Wk
        v = h @ Wv
        sr = jax.nn.sigmoid(h @ Wr)
        y = _wkv(spatial_decay / Tlen, spatial_first / Tlen, k, v)
        x = x + sr * y @ Wo
        h2 = _ln(x, g2, b2)
        kk = jnp.square(jax.nn.relu(h2 @ Wk_ffn))
        x = x + jax.nn.sigmoid(h2 @ Wr_ffn) * (kk @ Wv_ffn)
        return x

    def _L1_ffn_ref(x, route_id, Wi, bi, Wr, br, Ws, bs, Wo, bo):
        import jax, jax.numpy as jnp
        import numpy as np
        B, T, IN_DIM = (64, 64, 64)
        HID, OUT_DIM = (128, 64)
        N_LAYERS, N_EXPERTS, N_SHARED = (2, 16, 1)
        flat = x.reshape(-1, x.shape[-1])
        n_tok = flat.shape[0]
        route = jnp.repeat(route_id, n_tok // route_id.shape[0])
        h = jax.nn.relu(flat @ Wi.T + bi)
        n_layers, n_experts = (Wr.shape[0], Wr.shape[1])
        for l in range(n_layers):
            shared = (jnp.einsum('nd,shd->snh', h, Ws[l]) + bs[l][:, None, :]).mean(axis=0)
            routed = jnp.zeros_like(h)
            for e in range(n_experts):
                ye = h @ Wr[l, e].T + br[l, e]
                routed = routed + jnp.where((route == e)[:, None], ye, 0.0)
            h = jax.nn.relu(shared + routed + h)
        out = h @ Wo.T + bo
        return out.reshape(*x.shape[:-1], out.shape[-1])
    h = _L0_tok_ref(x, L0_tok_pe_w, L0_tok_pe_b, L0_tok_pe_ng, L0_tok_pe_nb, L0_tok_n1g, L0_tok_n1b, L0_tok_qkv_w, L0_tok_qkv_b, L0_tok_rpb, L0_tok_proj_w, L0_tok_proj_b, L0_tok_n2g, L0_tok_n2b, L0_tok_w1, L0_tok_b1, L0_tok_w2, L0_tok_b2)
    h = h + _L0_attn_ref(_layernorm(h, axis=-1), L0_attn_Wq, L0_attn_Wk, L0_attn_Wv)
    h = h + _L0_ffn_ref(_layernorm(h, axis=-1), L0_ffn_gate_w, L0_ffn_gate_b, L0_ffn_w1, L0_ffn_b1, L0_ffn_w2, L0_ffn_b2)
    h = h + _L1_attn_ref(_layernorm(h, axis=-1), L1_attn_Wk, L1_attn_Wv, L1_attn_Wr, L1_attn_Wo, L1_attn_Wk_ffn, L1_attn_Wv_ffn, L1_attn_Wr_ffn, L1_attn_g1, L1_attn_b1, L1_attn_g2, L1_attn_b2, L1_attn_spatial_decay, L1_attn_spatial_first)
    h = h + _L1_ffn_ref(_layernorm(h, axis=-1), L1_ffn_route_id, L1_ffn_Wi, L1_ffn_bi, L1_ffn_Wr, L1_ffn_br, L1_ffn_Ws, L1_ffn_bs, L1_ffn_Wo, L1_ffn_bo)
    return h

_drawn_inputs = setup_inputs


def setup_inputs(seed=0):
    import zlib

    import numpy as np

    out = dict(_drawn_inputs(seed))
    spreads = {'L0_tok_pe_b': (0.0, 0.1),
     'L0_tok_pe_ng': (1.0, 0.2),
     'L0_tok_pe_nb': (0.0, 0.1),
     'L0_tok_n1g': (1.0, 0.6),
     'L0_tok_n1b': (0.0, 0.8),
     'L0_tok_qkv_b': (0.0, 0.42),
     'L0_tok_proj_b': (0.0, 0.1),
     'L0_tok_n2g': (1.0, 0.6),
     'L0_tok_n2b': (0.0, 0.8),
     'L0_tok_b1': (0.0, 0.396),
     'L0_tok_b2': (0.0, 0.1),
     'L0_ffn_gate_b': (0.0, 0.1),
     'L0_ffn_b1': (0.0, 0.8),
     'L0_ffn_b2': (0.0, 0.8),
     'L1_ffn_bi': (0.0, 2.0),
     'L1_ffn_bo': (0.0, 0.8)}
    factors = {'L0_tok_rpb': 64.0,
     'L0_attn_Wq': 7.193,
     'L0_attn_Wk': 8.0,
     'L1_attn_Wk': 8.0,
     'L1_attn_Wv': 8.0,
     'L1_attn_Wr': 8.0,
     'L1_attn_Wo': 8.0,
     'L1_attn_Wk_ffn': 8.0,
     'L1_attn_Wv_ffn': 8.0,
     'L1_attn_Wr_ffn': 8.0,
     'L1_attn_g1': 8.0,
     'L1_attn_b1': 8.0,
     'L1_attn_g2': 8.0,
     'L1_attn_b2': 8.0,
     'L1_attn_spatial_decay': 8.0,
     'L1_attn_spatial_first': 64.0,
     'L1_ffn_Wi': 40.054,
     'L1_ffn_Wr': 44.749,
     'L1_ffn_br': 64.0,
     'L1_ffn_Ws': 39.215,
     'L1_ffn_bs': 64.0,
     'L1_ffn_Wo': 13.135}
    for name, (base, spread) in spreads.items():
        noise = np.random.default_rng([zlib.crc32(name.encode()), seed]).standard_normal(out[name].shape)
        drawn = base * np.exp(spread * noise) if base else spread * noise
        out[name] = jnp.asarray(drawn.astype(out[name].dtype))
    for name, factor in factors.items():
        out[name] = (out[name] * factor).astype(out[name].dtype)
    return out
```

```python
import numpy as np

C = 64
IMGS, SIDE = 8, 56
HALF_IMGS = IMGS // 2
TOK = SIDE * SIDE
COLS = HALF_IMGS * TOK
WS = 7
WIN = WS * WS
STRIP = WS * SIDE
STRIPS = SIDE // WS
CHUNKS = COLS // STRIP
NW = SIDE // WS
HEADS, HD = 8, 8
SHIFT = WS // 2
HID = 256
EPS = 1e-5
UN = 4
LNT = 98
KT = STRIP // LNT
EXPERTS = 8
CAP = 3920
QT = 112
QTILES = TOK // QT
KG = 4
KPG = QTILES // KG
ROUTES = 16
ROUTE_LAYERS = 2
RH = 128
STOP = 99

def table(*items):
    at, out = 0, {}
    for name, width in items:
        out[name] = (at, width)
        at += width
    out["_"] = (0, at)
    return out


BASE = table(("ident", 128), ("center", 128), ("mean", 128), ("eps", 1), ("pe_w", 128), ("pe_b", 1),
             ("pe_g", 1), ("pe_nb", 1), ("n1g", 2), ("n1b", 2), ("n2g", 2), ("n2b", 2),
             ("rg1", 1), ("rb1", 1), ("rg2", 1), ("rb2", 1))
SWIN = table(("wq", 128), ("wk", 128), ("wv", 64), ("wp", 128), ("bq", 1), ("bk", 1), ("bv", 1), ("bp", 1),
             ("headmask", HEADS))
MLP = table(("w1", 4 * 128), ("w2", 4 * 128), ("b1", 4), ("b2", 1))
ATT = table(("wq", 128), ("wk", 128), ("wv", 128))
GATE = table(("gw", 128), ("gb", 128), ("tri", LNT), ("ones", LNT))
MOE = table(("w1", EXPERTS * 512), ("w2", EXPERTS * 512), ("b1", EXPERTS * 4), ("b2", 128),
            ("sel", EXPERTS * 128))
RWKV = table(("wk", 128), ("wv", 128), ("wr", 128), ("wo", 128), ("decay", 1), ("first", 1))
RWKV_FFN = table(("wr", 128), ("w1", 512), ("w2", 512))
ROUTED = table(("wi", 2 * RH), ("bi", 1), ("wr", ROUTE_LAYERS * ROUTES * RH), ("br", ROUTE_LAYERS * ROUTES),
               ("ws", ROUTE_LAYERS * RH), ("bs", ROUTE_LAYERS), ("wo", C), ("bo", 1))


def build(nc, dram, out):
    from contextlib import ExitStack, contextmanager

    import concourse.bass as bass
    from concourse import mybir

    F32 = mybir.dt.float32
    BF16 = mybir.dt.bfloat16
    I32 = mybir.dt.int32
    ALU = mybir.AluOpType
    ACT = mybir.ActivationFunctionType
    AX = mybir.AxisListType.X
    pick = bass.ds

    def strip_by_row(ap):
        return ap.rearrange("p (a b k) -> p a b k", a=WS, b=NW)

    def strip_by_window(ap):
        return ap.rearrange("p (a b k) -> p b a k", a=WS, b=NW)

    @contextmanager
    def phase():
        with nc.cleanup_on_exit(), ExitStack() as ctx:
            yield ctx

    def load(ctx, name, cols):
        width = cols["_"][1]
        tile = ctx.enter_context(nc.sbuf_tensor(f"c_{name}", [128, width], F32))

        def part(key, a=0, n=None, p0=0, p1=128):
            at, w = cols[key]
            n = w - a if n is None else n
            return tile[p0:p1, at + a:at + a + n]
        return tile, part

    def warm_up(pe, bank, base):
        for _ in range(9):
            pe.matmul(bank[:, 0:256], base("center"), base("ident", 0, 256), start=True, stop=True)

    def layernorm(name, src, dst, base, gamma=None, beta=None):
        affine = gamma is not None
        with phase() as ctx:
            sb = lambda n, s, d=F32: ctx.enter_context(nc.sbuf_tensor(f"{name}_{n}", s, d))
            sem = lambda n: nc.alloc_semaphore(f"{name}_{n}")
            xs = sb("xs", [128, UN, STRIP])
            r = sb("r", [128, UN, STRIP])
            t = sb("t", [128, UN, STRIP]) if affine else None
            A = ctx.enter_context(nc.psum_tensor(f"{name}_A", [128, UN, 512], F32))
            V = ctx.enter_context(nc.psum_tensor(f"{name}_V", [128, UN, 512], F32))
            centered, copied, squared, averaged, logged, inverted, scaled, done = (
                sem(n) for n in ("centered", "copied", "squared", "averaged", "logged", "inverted", "scaled", "done"))
            block = ctx.enter_context(nc.Block())

            def cols(c):
                return pick(c * STRIP, STRIP)

            def after(eng, s, c):
                eng.wait_ge(s, c + 1)

            def passed(eng, s, c):
                eng.wait_ge(s, c + 1 + UN)

            def pipeline(eng, *stages):
                def turn(c0, first=False, tail=False):
                    for u in range(max(lag for lag, _ in stages) if tail else UN):
                        for lag, stage in stages:
                            v = u - lag
                            if (v >= 0 and not tail) or (v < 0 and not first):
                                stage(c0 + v, v % UN)
                turn(0, first=True)
                with eng.Fori(1, CHUNKS // UN) as it:
                    turn(it * UN)
                turn(CHUNKS, tail=True)

            @block.tensor
            def _(pe):
                def center(c, u):
                    after(pe, copied, c)
                    pe.matmul(A[:, u, 0:STRIP], base("center"), src[:, cols(c)], start=True, stop=True)\
                      .then_inc(centered, 1)

                def average(c, u):
                    after(pe, logged, c)
                    pe.wait_ge(squared, c + 1)
                    pe.matmul(V[:, u, 0:STRIP], base("mean"), r[:, u, :], start=True, stop=True).then_inc(averaged, 1)

                warm_up(pe, A[:, 0, :], base)
                pipeline(pe, (0, center), (1, average))

            @block.scalar
            def _(act):
                act.preload_act_table_set("natural_log_exp_and_others")

                def square(c, u):
                    after(act, scaled, c)
                    passed(act, copied, c)
                    act.activation(r[:, u, :], xs[:, u, :], ACT.Square).then_inc(squared, 1)

                def log(c, u):
                    act.wait_ge(averaged, c + 1)
                    act.activation(r[:, u, :], V[:, u, 0:STRIP], ACT.Ln, bias=base("eps")).then_inc(logged, 1)

                def invert(c, u):
                    passed(act, logged, c)
                    act.activation(r[:, u, :], r[:, u, :], ACT.Exp, scale=-0.5).then_inc(inverted, 1)

                pipeline(act, (0, square), (1, log), (1, invert))

            @block.vector
            def _(dve):
                def copy(c, u):
                    dve.wait_ge(centered, c + 1)
                    after(dve, scaled, c)
                    dve.tensor_copy(xs[:, u, :], A[:, u, 0:STRIP]).then_inc(copied, 1)

                def scale(c, u):
                    dve.wait_ge(inverted, c + 1)
                    if affine:
                        after(dve, done, c)
                    dve.tensor_tensor(t[:, u, :] if affine else dst[:, cols(c)], xs[:, u, :], r[:, u, :],
                                      ALU.mult).then_inc(scaled, 1)

                def transform(c, u):
                    passed(dve, scaled, c)
                    dve.tensor_scalar(dst[:, cols(c)], t[:, u, :], gamma, beta, ALU.mult, ALU.add).then_inc(done, 1)

                for s in (copied, scaled, logged, done):
                    dve.sem_inc(s, UN)
                if affine:
                    pipeline(dve, (0, copy), (2, scale), (2, transform))
                else:
                    pipeline(dve, (0, copy), (2, scale))

    def patch_embed(patches, dst, base):
        with phase() as ctx:
            P = ctx.enter_context(nc.psum_tensor("pe_P", [128, UN, 512], F32))
            made = nc.alloc_semaphore("pe_made")
            done = nc.alloc_semaphore("pe_done")
            block = ctx.enter_context(nc.Block())

            @block.tensor
            def _(pe):
                with pe.Fori(0, CHUNKS // UN) as it:
                    for u in range(UN):
                        pe.wait_ge(done, it * UN + u + 1)
                        pe.matmul(P[:, u, 0:STRIP], base("pe_w", p1=32),
                                  patches[0:32, pick(it * (UN * STRIP) + u * STRIP, STRIP)],
                                  start=True, stop=True).then_inc(made, 1)

            @block.vector
            def _(dve):
                dve.sem_inc(done, UN)
                with dve.Fori(0, CHUNKS // UN) as it:
                    for u in range(UN):
                        dve.wait_ge(made, it * UN + u + 1)
                        dve.tensor_scalar(dst[:, pick(it * (UN * STRIP) + u * STRIP, STRIP)], P[:, u, 0:STRIP],
                                          base("pe_b"), None, ALU.add).then_inc(done, 1)

    def roll(name, src, dst, shift):
        s = src[:, :].rearrange("p (i y x) -> p i y x", i=HALF_IMGS, y=SIDE)
        d = dst[:, :].rearrange("p (i y x) -> p i y x", i=HALF_IMGS, y=SIDE)
        cut = SIDE - shift
        spans = ((0, cut, shift), (cut, SIDE, -cut))
        with phase() as ctx:
            block = ctx.enter_context(nc.Block())

            def copies(eng, images):
                for i in images:
                    for y0, y1, dy in spans:
                        for x0, x1, dx in spans:
                            yield d[:, i, y0:y1, x0:x1], s[:, i, y0 + dy:y1 + dy, x0 + dx:x1 + dx]

            @block.vector
            def _(dve):
                for o, i in copies(dve, (0, 1, 2)):
                    dve.tensor_copy(o, i)

            @block.scalar
            def _(act):
                for o, i in copies(act, (3,)):
                    act.activation(o, i, ACT.Copy)

    def window_attention(b, res, y, base):
        name = f"wa{b}"
        with phase() as ctx:
            sb = lambda n, s, d=F32: ctx.enter_context(nc.sbuf_tensor(f"{name}_{n}", s, d))
            ps = lambda n, s: ctx.enter_context(nc.psum_tensor(f"{name}_{n}", s, F32))
            sem = lambda n: nc.alloc_semaphore(f"{name}_{n}")
            ctile, part = load(ctx, name, SWIN)
            yw = sb("yw", [128, NW, 128])
            kexp = sb("kexp", [128, 2, HEADS, STRIP])
            qbd = sb("qbd", [128, 2, NW, 128])
            vexp = sb("vexp", [128, 2, 2, NW, 4, C])
            bias = sb("bias", [128, 4, HEADS * WIN])
            biask = sb("biask", [128, HEADS])
            scores = sb("scores", [128, 4, HEADS * WIN])
            probs = sb("probs", [128, 4, HEADS, C])
            probsT = sb("probsT", [128, 2, 512])
            stat = sb("stat", [128, 4, 3, HEADS])
            osb = sb("osb", [128, STRIP])
            landed_o = sb("landed_o", [128, STRIP])
            KP, QP, OP, VP = ps("KP", [128, 512]), ps("QP", [128, 512]), ps("OP", [128, 512]), ps("VP", [128, 512])
            S = ps("S", [128, 2, 512])
            T = ps("T", [128, 2, 512])
            (loaded, masks_loaded, zeroed, staged, k_made, q_made, va_made, vb_made, kexp_made, qbd_made, vexp_made, scored,
             biased, maxed, shifted, exped, summed, inverted, normed, turned, turned_out, pv_made, o_out,
             projected, added, kb_made, residual_done) = (
                sem(n) for n in ("loaded", "masks_loaded", "zeroed", "staged", "k_made", "q_made", "va_made", "vb_made", "kexp_made",
                                 "qbd_made", "vexp_made", "scored", "biased", "maxed", "shifted", "exped", "summed",
                                 "inverted", "normed", "turned", "turned_out", "pv_made", "o_out", "projected",
                                 "added", "kb_made", "residual_done"))
            block = ctx.enter_context(nc.Block())
            NB = CHUNKS // 2
            LAG_E, LAG_N, LAG_T, LAG_V = 1, 2, 4, 5
            SCALE = HD ** -0.5

            def chunk_cols(c):
                return pick(c * STRIP, STRIP)

            @block.sync
            def _(sp):
                sp.dma_start(ctile[:, :], dram["swin"][b]).then_inc(loaded, 16)
                sp.dma_start(bias[:, 0, :], dram["rpb"][b]).then_inc(loaded, 16)
                if b:
                    sp.dma_start(kexp[:, 0, 0:3, :], dram["masks"][:, :, :]).then_inc(masks_loaded, 16)

            @block.tensor
            def _(pe):
                pe.wait_ge(loaded, 32)
                pe.wait_ge(zeroed, 4)

                def keys_queries(c):
                    toks = yw[:, :, 0:WIN]
                    pe.wait_ge(staged, 2 * c + 2)
                    if not isinstance(c, int) or c:
                        pe.wait_ge(kexp_made, c)
                    pe.matmul(KP[:, 0:STRIP], part("wk"), toks, start=True, stop=True).then_inc(k_made, 1)
                    pe.wait_ge(qbd_made, c + 1)
                    if not isinstance(c, int) or c > 1:
                        pe.wait_ge(added, c - 1)
                    pe.matmul(QP[:, 0:STRIP], part("wq"), toks, start=True, stop=True).then_inc(q_made, 1)

                def values(c, h):
                    pe.wait_ge(vexp_made, 2 * c + 1 + h)
                    for w in range(NW):
                        mm = pe.matmul(VP[:, w * C:(w + 1) * C], yw[h * C:(h + 1) * C, w, :],
                                       part("wv", p0=h * C, p1=(h + 1) * C), start=True, stop=True)
                    mm.then_inc((va_made, vb_made)[h], 1)

                def score(c, par, w):
                    if w == 0:
                        pe.wait_ge(kexp_made, c + 1)
                        pe.wait_ge(qbd_made, c + 2)
                    pe.wait_ge(biased, c * NW + w + 1)
                    pe.matmul(S[:, w % 2, 0:STRIP], qbd[:, par, w, :],
                              kexp[:, par, :, w * WIN:(w + 1) * WIN], start=True, stop=True).then_inc(scored, 1)

                def turn(c, w):
                    n = c * NW + w
                    pe.wait_ge(normed, n + 1)
                    pe.wait_ge(turned_out, n + 1)
                    for k in range(4):
                        mm = pe.transpose(T[:, w % 2, k * 128:(k + 1) * 128],
                                          probs[:, w % 4, 2 * k:2 * k + 2, :].rearrange("p h k -> p (h k)"), base("ident"))
                    mm.then_inc(turned, 1)

                def weigh(c, par, w):
                    n = c * NW + w
                    if w == 0:
                        pe.wait_ge(vexp_made, 2 * c + 3)
                        pe.wait_ge(o_out, c + 1)
                    pe.wait_ge(turned_out, n + 3)
                    for h in range(2):
                        for k in range(4):
                            mm = pe.matmul(OP[h * C:(h + 1) * C, w * WIN:(w + 1) * WIN], vexp[:, par, h, w, k, :],
                                           probsT[:, w % 2, k * 128 + h * C:k * 128 + h * C + WIN],
                                           start=(k == 0), stop=(k == 3))
                    mm.then_inc(pv_made, 1)

                def project(c):
                    pe.wait_ge(o_out, c + 2)
                    pe.wait_ge(qbd_made, min(c + 4, CHUNKS + 1) if isinstance(c, int) else c + 4)
                    pe.matmul(QP[:, 0:STRIP], part("wp"), osb[:, :], start=True, stop=True).then_inc(projected, 1)

                def slot(c, par, w, first=False, tail=False):
                    if not tail:
                        score(c, par, w)
                    for lag, kind in ((LAG_T, 0), (LAG_V, 1)):
                        v = w - lag
                        cc, pp = (c, par) if v >= 0 else (c - 1, 1 - par)
                        if first and v < 0:
                            continue
                        if tail and v >= 0:
                            continue
                        if kind == 0:
                            turn(cc, v % NW)
                        else:
                            weigh(cc, pp, v % NW)
                    if w == LAG_V and not first:
                        project(c - 1)

                def body(c0, first=False, last=False):
                    for par in range(2):
                        c = c0 + par
                        for w in range(NW):
                            slot(c, par, w, first=first and par == 0)
                            if not (last and par == 1):
                                if w == 2:
                                    keys_queries(c + 1)
                                if w == 4:
                                    values(c + 1, 0)
                                if w == 6:
                                    values(c + 1, 1)

                warm_up(pe, OP, base)
                keys_queries(0)
                values(0, 0)
                values(0, 1)
                warm_up(pe, OP, base)
                body(0, first=True)
                with pe.Fori(1, NB - 1) as m:
                    body(m * 2)
                body((NB - 1) * 2, last=True)
                for w in range(LAG_V + 3):
                    slot(CHUNKS, 0, w, tail=True)

            @block.scalar
            def _(act):
                act.preload_act_table(ACT.Exp)
                act.wait_ge(loaded, 32)
                act.wait_ge(zeroed, 4)
                act.wait_ge(kb_made, 4 if b else 1)

                def stage(c):
                    act.wait_ge(vb_made, c + 1)
                    act.activation(yw[:, :, 0:WIN].rearrange("p b (a k) -> p b a k", a=WS),
                                   strip_by_window(y[:, chunk_cols(c)]), ACT.Copy).then_inc(staged, 1)

                def expand(c, par, part_=None):
                    act.wait_ge(k_made, c + 1)
                    heads = range(HEADS) if part_ is None else range(part_ * 4, part_ * 4 + 4)
                    for h in heads:
                        a = act.activation(kexp[:, par, h, :], KP[:, 0:STRIP], ACT.Identity,
                                           bias=biask[:, h:h + 1], scale=part("headmask", h, 1))
                    if part_ != 0:
                        a.then_inc(kexp_made, 1)

                def expo(c, w):
                    n = c * NW + w
                    act.wait_ge(shifted, n + 1)
                    act.wait_ge(turned, n + 1)
                    act.activation(probs[:, w % 4, :, 0:WIN], scores[:, w % 4, :].rearrange(
                        "p (h k) -> p h k", h=HEADS), ACT.Exp).then_inc(exped, 1)

                def evacuate(c, w):
                    n = c * NW + w
                    act.wait_ge(turned, n + 5)
                    act.wait_ge(pv_made, n + 1)
                    act.activation(probsT[:, w % 2, :], T[:, w % 2, :], ACT.Copy).then_inc(turned_out, 1)

                def out(c):
                    act.wait_ge(pv_made, NW * c + NW + 2)
                    act.wait_ge(projected, c + 1)
                    act.activation(osb[:, :], OP[:, 0:STRIP], ACT.Identity, bias=part("bv")).then_inc(o_out, 1)

                def land(c):
                    act.wait_ge(projected, c + 2)
                    act.wait_ge(residual_done, c + 1)
                    act.activation(strip_by_row(landed_o[:, :]), QP[:, 0:STRIP].rearrange(
                        "p (b a k) -> p a b k", b=NW, a=WS), ACT.Identity, bias=part("bp")).then_inc(added, 1)

                def slot(c, par, w, first=False, tail=False):
                    for lag, what in ((LAG_E, expo), (LAG_T, evacuate)):
                        v = w - lag
                        if (v >= 0 and not tail) or (v < 0 and not first):
                            what(c if v >= 0 else c - 1, v % NW)
                    if w == LAG_V - 1 and not first:
                        out(c - 1)
                    if w == LAG_V + 1 and not first:
                        land(c - 1)

                def body(c0, first=False, last=False):
                    for par in range(2):
                        c = c0 + par
                        for w in range(NW):
                            slot(c, par, w, first=first and par == 0)
                            if not (last and par == 1):
                                if w == 0:
                                    stage(c + 1)
                                if w in (3, 4):
                                    expand(c + 1, 1 - par, w - 3)

                stage(0)
                expand(0, 0)
                body(0, first=True)
                with act.Fori(1, NB - 1) as m:
                    body(m * 2)
                body((NB - 1) * 2, last=True)
                for w in range(LAG_V + 3):
                    slot(CHUNKS, 0, w, tail=True)

            @block.gpsimd
            def _(pool):
                pool.memset(yw[:, :, :], 0.0).then_inc(zeroed, 1)
                pool.memset(qbd[:, :, :, :], 0.0).then_inc(zeroed, 1)
                pool.memset(vexp[:, :, :, :, :, :], 0.0).then_inc(zeroed, 1)
                pool.memset(probs[:, :, :, :], 0.0).then_inc(zeroed, 1)

                def shift(n, w):
                    tile = scores[:, w % 4, :].rearrange("p (h k) -> p h k", h=HEADS)
                    pool.wait_ge(maxed, n + 1)
                    pool.tensor_tensor(tile, tile, stat[:, w % 4, 0, :].unsqueeze(2).broadcast_to([128, HEADS, WIN]),
                                       ALU.subtract).then_inc(shifted, 1)

                def norm(n, w):
                    pool.wait_ge(inverted, n + 1)
                    pool.tensor_tensor(probs[:, w % 4, :, 0:WIN], probs[:, w % 4, :, 0:WIN],
                                       stat[:, w % 4, 2, :].unsqueeze(2).broadcast_to([128, HEADS, WIN]),
                                       ALU.mult).then_inc(normed, 1)

                for w in range(LAG_N):
                    shift(w, w)
                with pool.Fori(0, CHUNKS - 1) as c:
                    for w in range(NW):
                        shift(c * NW + w + LAG_N, w + LAG_N)
                        norm(c * NW + w, w)
                for w in range(NW):
                    if w + LAG_N < NW:
                        shift((CHUNKS - 1) * NW + w + LAG_N, w + LAG_N)
                    norm((CHUNKS - 1) * NW + w, w)

            @block.vector
            def _(dve):
                dve.wait_ge(loaded, 32)
                if b:
                    dve.wait_ge(masks_loaded, 16)
                dve.wait_ge(zeroed, 4)
                dve.tensor_scalar(biask[:, :], part("headmask"), part("bk"), None, ALU.mult).then_inc(kb_made, 1)
                if b:
                    for k in range(1, 4):
                        dve.tensor_tensor(bias[:, k, :], bias[:, 0, :], kexp[:, 0, k - 1, :], ALU.add).then_inc(kb_made, 1)
                    dve.wait_ge(kb_made, 4)
                for s, n in ((added, 1), (qbd_made, 1), (vexp_made, 1), (biased, 2), (turned_out, 2), (o_out, 1),
                             (vb_made, 1), (turned, 4), (pv_made, 2), (projected, 1),
                             (residual_done, 1)):
                    dve.sem_inc(s, n)

                def stage(c):
                    dve.wait_ge(vb_made, c + 1)
                    dve.tensor_copy(yw[:, :, C:C + WIN].rearrange("p b (a k) -> p b a k", a=WS),
                                    strip_by_window(y[:, chunk_cols(c)])).then_inc(staged, 1)

                def queries(c, par):
                    dve.wait_ge(q_made, c + 1)
                    for h in range(2):
                        rows = slice(h * C, (h + 1) * C)
                        o = dve.tensor_scalar(qbd[rows, par, :, h * C:h * C + WIN],
                                              QP[rows, 0:STRIP].rearrange("p (b k) -> p b k", b=NW),
                                              part("bq", p0=h * C, p1=h * C + C), SCALE, ALU.add, ALU.mult)
                    o.then_inc(qbd_made, 1)

                def values(c, par, h):
                    dve.wait_ge((va_made, vb_made)[h], c + 1 + h)
                    v = VP[:, :].rearrange("p (b k e d) -> p b k e d", b=NW, k=4, e=2)
                    for e in range(2):
                        rows = slice(e * C, (e + 1) * C)
                        dst = vexp[rows, par, h].rearrange("p b k (g d) -> p b (k g) d", d=HD)
                        o = dve.tensor_copy(dst[:, :, e:e + 31:10, :], v[rows, :, :, e, :])
                    o.then_inc(vexp_made, 1)

                def bias_of(w, last_strip):
                    return bias[:, (int(w == NW - 1) + 2 * int(last_strip)) if b else 0, :]

                def by_head(w):
                    return scores[:, w % 4, :].rearrange("p (h k) -> p h k", h=HEADS)

                def add_bias(n, w, last_strip):
                    dve.wait_ge(scored, n + 1)
                    dve.tensor_tensor(scores[:, w % 4, :], S[:, w % 2, 0:STRIP], bias_of(w, last_strip), ALU.add)\
                       .then_inc(biased, 1)

                def maximum(n, w):
                    dve.wait_ge(biased, n + 3)
                    dve.tensor_reduce(stat[:, w % 4, 0, :], by_head(w), AX, ALU.max).then_inc(maxed, 1)

                def total(n, w):
                    dve.wait_ge(exped, n + 1)
                    dve.tensor_reduce(stat[:, w % 4, 1, :], probs[:, w % 4, :, 0:WIN], AX, ALU.add).then_inc(summed, 1)

                def inverse(n, w):
                    dve.wait_ge(summed, n + 1)
                    dve.reciprocal(stat[:, w % 4, 2, :], stat[:, w % 4, 1, :]).then_inc(inverted, 1)

                def residual(c):
                    dve.wait_ge(added, c + 2)
                    strip = res[:, chunk_cols(c)]
                    dve.tensor_tensor(strip, landed_o[:, :], strip, ALU.add).then_inc(residual_done, 1)

                def slot(c, w, last_strip, first=False, tail=False):
                    n, before = c * NW + w, w - LAG_N
                    sums = (before >= 0 and not tail) or (before < 0 and not first)
                    if not tail:
                        add_bias(n, w, last_strip)
                    if sums:
                        total(n - LAG_N, before % NW)
                    if not tail:
                        maximum(n, w)
                    if sums:
                        inverse(n - LAG_N, before % NW)
                    if w == LAG_V + 2 and not first:
                        residual(c - 1)

                def body(c0, ends_image, first=False, last=False):
                    for par in range(2):
                        c = c0 + par
                        for w in range(NW):
                            slot(c, w, ends_image and par == 1, first=first and par == 0)
                            if not (last and par == 1):
                                if w == 0:
                                    stage(c + 1)
                                if w == 3:
                                    queries(c + 1, 1 - par)
                                if w in (5, 7):
                                    values(c + 1, 1 - par, (w - 5) // 2)

                stage(0)
                queries(0, 0)
                values(0, 0, 0)
                values(0, 0, 1)
                body(0, False, first=True)
                with dve.Fori(0, HALF_IMGS - 1) as img:
                    body(img * STRIPS + 2, False)
                    body(img * STRIPS + 4, False)
                    body(img * STRIPS + 6, True)
                    body(img * STRIPS + 8, False)
                body((HALF_IMGS - 1) * STRIPS + 2, False)
                body((HALF_IMGS - 1) * STRIPS + 4, False)
                body((NB - 1) * 2, True, last=True)
                for w in range(LAG_V + 3):
                    slot(CHUNKS, w, False, tail=True)

    def mlp(b, res, y, base):
        name = f"mlp{b}"
        with phase() as ctx:
            sem = lambda n: nc.alloc_semaphore(f"{name}_{n}")
            ctile, part = load(ctx, name, MLP)
            g = ctx.enter_context(nc.sbuf_tensor(f"{name}_g", [128, 4, STRIP], F32))
            H = ctx.enter_context(nc.psum_tensor(f"{name}_H", [128, 4, 512], F32))
            O = ctx.enter_context(nc.psum_tensor(f"{name}_O", [128, 2, 512], F32))
            loaded, hidden, gelued, used, added = (
                sem(n) for n in ("loaded", "hidden", "gelued", "used", "added"))
            block = ctx.enter_context(nc.Block())

            @block.sync
            def _(sp):
                sp.dma_start(ctile[:, :], dram["mlp"][b]).then_inc(loaded, 16)

            @block.tensor
            def _(pe):
                pe.wait_ge(loaded, 16)
                warm_up(pe, O[:, 0, :], base)
                with pe.Fori(0, CHUNKS // 2) as it:
                    for u in range(2):
                        c = it * 2 + u
                        for q in range(4):
                            pe.wait_ge(gelued, c * 4 + q + 1)
                            pe.matmul(H[:, q, 0:STRIP], part("w1", q * 128, 128), y[:, pick(c * STRIP, STRIP)],
                                      start=True, stop=True).then_inc(hidden, 1)
                        pe.wait_ge(added, c + 1)
                        for q in range(4):
                            pe.wait_ge(gelued, c * 4 + q + 5)
                            pe.matmul(O[:, u, 0:STRIP], part("w2", q * 128, 128), g[:, q, :],
                                      start=(q == 0), stop=(q == 3)).then_inc(used, 1)

            @block.scalar
            def _(act):
                act.preload_act_table(ACT.Gelu)
                act.wait_ge(loaded, 16)
                with act.Fori(0, CHUNKS) as c:
                    for q in range(4):
                        act.wait_ge(hidden, c * 4 + q + 1)
                        act.wait_ge(used, c * 4 + q + 1)
                        act.activation(g[:, q, :], H[:, q, 0:STRIP], ACT.Gelu, bias=part("b1", q, 1)).then_inc(gelued, 1)

            @block.vector
            def _(dve):
                dve.wait_ge(loaded, 16)
                dve.sem_inc(gelued, 4)
                dve.sem_inc(used, 4)
                dve.sem_inc(added, 2)
                with dve.Fori(0, CHUNKS // 2) as it:
                    for u in range(2):
                        c = it * 2 + u
                        dve.wait_ge(used, c * 4 + 8)
                        strip = res[:, pick(c * STRIP, STRIP)]
                        dve.scalar_tensor_tensor(out=strip, in0=O[:, u, 0:STRIP], scalar=part("b2"), in1=strip,
                                                 op0=ALU.add, op1=ALU.add).then_inc(added, 1)

    def image_attention(res, y, base):
        name = "att"
        with phase() as ctx:
            sb = lambda n, s, d=F32: ctx.enter_context(nc.sbuf_tensor(f"{name}_{n}", s, d))
            ps = lambda n, s: ctx.enter_context(nc.psum_tensor(f"{name}_{n}", s, F32))
            sem = lambda n: nc.alloc_semaphore(f"{name}_{n}")
            ctile, part = load(ctx, name, ATT)
            GW = KPG * QT
            HB = GW // 2
            UNITS = 2 * KG
            ys = sb("ys", [128, TOK])
            ks = sb("ks", [128, TOK])
            qs = sb("qs", [128, TOK])
            vs = sb("vs", [QT, QTILES, 128])
            qz = sb("qz", [128, 2, 2, QT])
            probs = sb("probs", [QT, 2, GW])
            probsT = sb("probsT", [QT, 2, GW])
            negmax = sb("negmax", [QT, 2, UNITS])
            sums = sb("sums", [QT, 2, UNITS])
            least = sb("least", [QT, 2, 2])
            gap = sb("gap", [QT, 2, UNITS])
            weight = sb("weight", [QT, 2, UNITS])
            wsum = sb("wsum", [QT, 2, UNITS])
            total = sb("total", [QT, 2, 2])
            inverse = sb("inverse", [QT, 2, 2])
            share = sb("share", [QT, 2, UNITS])
            scaled = sb("scaled", [QT, UNITS, C])
            joined = sb("joined", [QT, 2, 128])
            S = ps("S", [128, 4, 512])
            T = ps("T", [128, 2, 512])
            O = ps("O", [128, 2, 512])
            (loaded, staged, prepared, evac_a, evac_d, scored, maxed, exped, turned, out_a, out_d, weighed, combined,
             weights_made, o_turned, residual, q_staged, qz_blank) = (
                sem(n) for n in ("loaded", "staged", "prepared", "evac_a", "evac_d", "scored", "maxed", "exped", "turned",
                                 "out_a", "out_d", "weighed", "combined", "weights_made", "o_turned", "residual",
                                 "q_staged", "qz_blank"))
            block = ctx.enter_context(nc.Block())
            NK = TOK // STRIP
            NV = QTILES // 4
            PREP = 2 * NK + NV
            CHAIN = 8

            @block.sync
            def _(sp):
                sp.dma_start(ctile[:, :], dram["att"]).then_inc(loaded, 16)

            @block.tensor
            def _(pe):
                pe.wait_ge(loaded, 16)

                def prepare(j):
                    pe.wait_ge(staged, j + 1)
                    for u in range(PREP):
                        if u >= 4:
                            n = (u - 4) // 2 + 1
                            if u % 2 == 0:
                                pe.wait_ge(evac_a, j * ((PREP + 1) // 2) + n)
                            else:
                                pe.wait_ge(evac_d, j * (PREP // 2) + n)
                        if u < 2 * NK:
                            mm = pe.matmul(S[:, u % 4, 0:STRIP], part("wk" if u % 2 == 0 else "wq"),
                                           ys[:, (u // 2) * STRIP:(u // 2 + 1) * STRIP], start=True, stop=True)
                        else:
                            for k in range(4):
                                t = (u - 2 * NK) * 4 + k
                                mm = pe.matmul(S[0:QT, u % 4, k * 128:(k + 1) * 128], ys[:, t * QT:(t + 1) * QT],
                                               part("wv"), start=True, stop=True)
                        mm.then_inc(prepared, 1)
                    pe.wait_ge(evac_a, (j + 1) * ((PREP + 1) // 2))
                    pe.wait_ge(evac_d, (j + 1) * (PREP // 2))

                def score(tile, p, u):
                    h, g = divmod(u, KG)
                    n = tile * UNITS + u
                    if u == 0:
                        pe.wait_ge(q_staged, tile + 1)
                    pe.wait_ge(exped, n + 1)
                    for b in range(2):
                        mm = pe.matmul(S[0:QT, (u % 2) * 2 + b, 0:HB], qz[:, p, h, :],
                                       ks[:, g * GW + b * HB:g * GW + (b + 1) * HB], start=True, stop=True)
                    mm.then_inc(scored, 1)

                def turn(tile, p, u):
                    n = tile * UNITS + u
                    pe.wait_ge(exped, n + 3)
                    pe.wait_ge(out_d, n + 1)
                    pe.wait_ge(out_a, n + 1)
                    for k in range(KPG):
                        mm = pe.transpose(T[0:QT, k // 4, (k % 4) * QT:(k % 4 + 1) * QT],
                                          probs[:, u % 2, k * QT:(k + 1) * QT], base("ident", 0, QT, 0, QT))
                    mm.then_inc(turned, 1)

                def weigh(tile, p, u):
                    h, g = divmod(u, KG)
                    n = tile * UNITS + u
                    pe.wait_ge(out_d, n + 2)
                    pe.wait_ge(out_a, n + 2)
                    if u == 0:
                        pe.wait_ge(residual, tile + 1)
                    for k in range(KPG):
                        mm = pe.matmul(O[0:QT, p, u * C:(u + 1) * C], probsT[:, u % 2, k * QT:(k + 1) * QT],
                                       vs[:, g * KPG + k, h * C:(h + 1) * C], start=(k == 0), stop=(k == KPG - 1))
                    mm.then_inc(weighed, 1)

                def turn_output(tile, p):
                    pe.wait_ge(combined, (tile + 1) * CHAIN)
                    pe.transpose(O[:, p, 0:QT], joined[:, p, :], base("ident", 0, QT, 0, QT)).then_inc(o_turned, 1)

                def slots(tile, p, first, tail):
                    for u in range(UNITS):
                        if not tail:
                            score(tile, p, u)
                        for lag, what in ((1, turn), (2, weigh)):
                            if u >= lag and not tail:
                                what(tile, p, u - lag)
                            elif u < lag and not first:
                                what(tile - 1, 1 - p, u - lag + UNITS)
                        if u == 5 and not first:
                            turn_output(tile - 1, 1 - p)

                with pe.Fori(0, HALF_IMGS) as j:
                    prepare(j)
                    slots(j * QTILES, 0, True, False)
                    slots(j * QTILES + 1, 1, False, False)
                    with pe.Fori(1, QTILES // 2) as i:
                        slots(j * QTILES + i * 2, 0, False, False)
                        slots(j * QTILES + i * 2 + 1, 1, False, False)
                    slots(j * QTILES + QTILES, 0, False, True)

            @block.scalar
            def _(act):
                act.preload_act_table(ACT.Exp)

                def prepare(j):
                    for u in range(0, PREP, 2):
                        act.wait_ge(prepared, j * PREP + u + 2)
                        if u < 2 * NK:
                            a = act.activation(ks[:, (u // 2) * STRIP:(u // 2 + 1) * STRIP], S[:, u % 4, 0:STRIP], ACT.Copy)
                        else:
                            t = (u - 2 * NK) * 4
                            a = act.activation(vs[:, t:t + 4, :], S[0:QT, u % 4, :].rearrange("p (t c) -> p t c", t=4), ACT.Copy)
                        a.then_inc(evac_a, 1)

                def expo(tile, p, u):
                    n = tile * UNITS + u
                    act.wait_ge(maxed, n + 1)
                    act.wait_ge(turned, n + 1)
                    act.activation(probs[:, u % 2, :].rearrange("p (b k) -> p b k", b=2),
                                   S[0:QT, (u % 2) * 2:(u % 2) * 2 + 2, 0:HB], ACT.Exp,
                                   bias=negmax[:, p, u:u + 1], accum_out=sums[:, p, u:u + 1]).then_inc(exped, 1)

                def evacuate(tile, p, u):
                    n = tile * UNITS + u
                    act.wait_ge(turned, n + 3)
                    act.wait_ge(weighed, n + 1)
                    act.activation(probsT[:, u % 2, 4 * QT:GW], T[0:QT, 1, 0:3 * QT], ACT.Copy).then_inc(out_a, 1)

                def weights(tile, p):
                    act.wait_ge(combined, tile * CHAIN + 2)
                    act.activation(weight[:, p, :], gap[:, p, :], ACT.Exp).then_inc(weights_made, 1)

                def slots(tile, p, first, tail):
                    for u in range(UNITS):
                        if not tail:
                            expo(tile, p, u)
                        if u >= 1 and not tail:
                            evacuate(tile, p, u - 1)
                        elif u < 1 and not first:
                            evacuate(tile - 1, 1 - p, UNITS - 1)
                        if u == 3 and not first:
                            weights(tile - 1, 1 - p)

                with act.Fori(0, HALF_IMGS) as j:
                    prepare(j)
                    slots(j * QTILES, 0, True, False)
                    slots(j * QTILES + 1, 1, False, False)
                    with act.Fori(1, QTILES // 2) as i:
                        slots(j * QTILES + i * 2, 0, False, False)
                        slots(j * QTILES + i * 2 + 1, 1, False, False)
                    slots(j * QTILES + QTILES, 0, False, True)

            @block.gpsimd
            def _(pool):
                pool.memset(qz[:, :, :, :], 0.0).then_inc(qz_blank, 1)
                pool.wait_ge(qz_blank, 1)
                with pool.Fori(0, HALF_IMGS) as j:
                    with pool.Fori(0, QTILES // 2) as i:
                        for p in range(2):
                            pool.wait_ge(evac_d, (j + 1) * (PREP // 2))
                            tile = j * QTILES + i * 2 + p
                            pool.wait_ge(scored, tile * UNITS + UNITS)
                            for h in range(2):
                                rows = slice(h * C, (h + 1) * C)
                                o = pool.tensor_copy(qz[rows, p, h, :], qs[rows, pick(i * (2 * QT) + p * QT, QT)])
                            o.then_inc(q_staged, 1)

            @block.vector
            def _(dve):
                for s, n in ((exped, 2), (turned, 2), (out_a, 1), (out_d, 1), (weighed, 2), (residual, 2),
                             (scored, 2 * UNITS), (prepared, 1)):
                    dve.sem_inc(s, n)

                def prepare(j):
                    dve.wait_ge(prepared, j * PREP + 1)
                    dve.tensor_copy(ys[:, :], y[:, pick(j * TOK, TOK)]).then_inc(staged, 1)
                    for u in range(1, PREP, 2):
                        dve.wait_ge(prepared, j * PREP + u + 2)
                        if u < 2 * NK:
                            o = dve.tensor_scalar(qs[:, (u // 2) * STRIP:(u // 2 + 1) * STRIP], S[:, u % 4, 0:STRIP],
                                                  C ** -0.5, None, ALU.mult)
                        else:
                            t = (u - 2 * NK) * 4
                            o = dve.tensor_copy(vs[:, t:t + 4, :], S[0:QT, u % 4, :].rearrange("p (t c) -> p t c", t=4))
                        o.then_inc(evac_d, 1)

                def maximum(tile, p, u):
                    n = tile * UNITS + u
                    dve.wait_ge(scored, n + 1 + 2 * UNITS)
                    dve.tensor_reduce(negmax[:, p, u:u + 1], S[0:QT, (u % 2) * 2:(u % 2) * 2 + 2, 0:HB],
                                      mybir.AxisListType.XY, ALU.max, negate=True).then_inc(maxed, 1)

                def evacuate(tile, p, u):
                    n = tile * UNITS + u
                    dve.wait_ge(turned, n + 3)
                    dve.wait_ge(weighed, n + 1)
                    dve.tensor_copy(probsT[:, u % 2, 0:4 * QT], T[0:QT, 0, 0:4 * QT]).then_inc(out_d, 1)

                def by_group(ap):
                    return ap.rearrange("p (h g) -> p h g", h=2)

                def gaps(tile, p):
                    dve.wait_ge(maxed, (tile + 1) * UNITS)
                    dve.tensor_reduce(least[:, p, :], by_group(negmax[:, p, :]), AX, ALU.min).then_inc(combined, 1)
                    dve.wait_ge(combined, tile * CHAIN + 1)
                    dve.tensor_tensor(by_group(gap[:, p, :]), least[:, p, :].unsqueeze(2).broadcast_to([QT, 2, KG]),
                                      by_group(negmax[:, p, :]), ALU.subtract).then_inc(combined, 1)

                def join(tile, p):
                    dve.wait_ge(weights_made, tile + 1)
                    dve.tensor_tensor(wsum[:, p, :], weight[:, p, :], sums[:, p, :], ALU.mult).then_inc(combined, 1)
                    dve.wait_ge(combined, tile * CHAIN + 3)
                    dve.tensor_reduce(total[:, p, :], by_group(wsum[:, p, :]), AX, ALU.add).then_inc(combined, 1)
                    dve.wait_ge(combined, tile * CHAIN + 4)
                    dve.reciprocal(inverse[:, p, :], total[:, p, :]).then_inc(combined, 1)
                    dve.wait_ge(combined, tile * CHAIN + 5)
                    dve.tensor_tensor(by_group(share[:, p, :]), by_group(weight[:, p, :]),
                                      inverse[:, p, :].unsqueeze(2).broadcast_to([QT, 2, KG]), ALU.mult).then_inc(combined, 1)
                    dve.wait_ge(combined, tile * CHAIN + 6)
                    dve.wait_ge(weighed, (tile + 1) * UNITS + 2)
                    dve.tensor_tensor(scaled[:, :, :], O[0:QT, p, :].rearrange("p (u c) -> p u c", u=UNITS),
                                      share[:, p, :].unsqueeze(2).broadcast_to([QT, UNITS, C]), ALU.mult).then_inc(combined, 1)
                    dve.wait_ge(combined, tile * CHAIN + 7)
                    dve.tensor_reduce(joined[:, p, :].rearrange("p (h c) -> p h c", h=2),
                                      scaled[:, :, :].rearrange("p (h g) c -> p h c g", h=2), AX, ALU.add)\
                       .then_inc(combined, 1)

                def add(tile, i, j, p):
                    dve.wait_ge(o_turned, tile + 1)
                    cols = res[:, pick(j * TOK + i * QT, QT)]
                    dve.tensor_tensor(cols, O[:, p, 0:QT], cols, ALU.add).then_inc(residual, 1)

                def slots(j, i, p, first, tail):
                    tile = j * QTILES + i
                    for u in range(UNITS):
                        if not tail:
                            maximum(tile, p, u)
                        if u >= 1 and not tail:
                            evacuate(tile, p, u - 1)
                        elif u < 1 and not first:
                            evacuate(tile - 1, 1 - p, UNITS - 1)
                        if not first:
                            if u == 2:
                                gaps(tile - 1, 1 - p)
                            if u == 4:
                                join(tile - 1, 1 - p)
                            if u == 6:
                                add(tile - 1, i - 1, j, 1 - p)

                with dve.Fori(0, HALF_IMGS) as j:
                    prepare(j)
                    slots(j, 0, 0, True, False)
                    slots(j, 1, 1, False, False)
                    with dve.Fori(1, QTILES // 2) as i:
                        slots(j, i * 2, 0, False, False)
                        slots(j, i * 2 + 1, 1, False, False)
                    slots(j, QTILES, 0, False, True)

    def routing(y, gates, base):
        name = "gate"
        TILES = COLS // LNT
        E2 = 2 * EXPERTS
        with phase() as ctx:
            sb = lambda n, s, d=F32: ctx.enter_context(nc.sbuf_tensor(f"{name}_{n}", s, d))
            sem = lambda n: nc.alloc_semaphore(f"{name}_{n}")
            ctile, part = load(ctx, name, GATE)
            logits = sb("logits", [LNT, TILES, E2])
            work = sb("work", [LNT, TILES, E2])
            chosen = sb("chosen", [LNT, TILES, E2])
            before = sb("before", [LNT, E2, TILES])
            small = sb("small", [LNT, 3, 2 * TILES])
            lt = sb("lt", [128, 2, STRIP])
            loaded = sem("loaded")
            with ExitStack() as inner:
                L = inner.enter_context(nc.psum_tensor("gate_L", [128, 2, 512], F32))
                Z = inner.enter_context(nc.psum_tensor("gate_Z", [LNT, 2, 512], F32))
                made, copied, turned, placed = (sem(n) for n in ("made", "copied", "turned", "placed"))
                block = inner.enter_context(nc.Block())

                @block.sync
                def _(sp):
                    sp.dma_start(ctile[:, :], dram["gate"]).then_inc(loaded, 16)

                @block.tensor
                def _(pe):
                    pe.wait_ge(loaded, 16)
                    with pe.Fori(0, CHUNKS // 2) as it:
                        for u in range(2):
                            c = it * 2 + u
                            pe.wait_ge(copied, c + 1)
                            pe.matmul(L[:, u, 0:STRIP], part("gw"), y[:, pick(c * STRIP, STRIP)], start=True,
                                      stop=True).then_inc(made, 1)
                        for u in range(2):
                            c = it * 2 + u
                            pe.wait_ge(copied, c + 3)
                            pe.wait_ge(placed, c + 1)
                            for k in range(KT):
                                mm = pe.transpose(Z[:, u, k * 128:(k + 1) * 128], lt[:, u, k * LNT:(k + 1) * LNT],
                                                  base("ident"))
                            mm.then_inc(turned, 1)

                @block.scalar
                def _(act):
                    with act.Fori(0, CHUNKS // 2) as it:
                        for u in range(2):
                            c = it * 2 + u
                            act.wait_ge(made, c + 1)
                            act.wait_ge(turned, c + 1)
                            act.activation(lt[:, u, :], L[:, u, 0:STRIP], ACT.Copy).then_inc(copied, 1)

                @block.vector
                def _(dve):
                    dve.sem_inc(copied, 2)
                    dve.sem_inc(turned, 2)
                    dve.sem_inc(placed, 2)
                    dve.wait_ge(loaded, 16)
                    with dve.Fori(0, CHUNKS // 2) as it:
                        for u in range(2):
                            c = it * 2 + u
                            dve.wait_ge(turned, c + 3)
                            dve.tensor_tensor(logits[:, pick(c * KT, KT), :],
                                              Z[:, u, :].rearrange("p (t e) -> p t e", t=KT)[:, :, 0:E2],
                                              part("gb", 0, E2, 0, LNT).unsqueeze(1).broadcast_to([LNT, KT, E2]),
                                              ALU.add).then_inc(placed, 1)
            with ExitStack() as inner:
                B = 512
                NBANK = TILES * E2 // B
                INC = inner.enter_context(nc.psum_tensor("gate_inc", [LNT, NBANK, B], F32))
                TOT = inner.enter_context(nc.psum_tensor("gate_tot", [LNT, NBANK, B], F32))
                step, expd, counted = (sem(n) for n in ("step", "expd", "counted"))
                block = inner.enter_context(nc.Block())
                flat = lambda t: t[:, :, :].rearrange("p t e -> p (t e)")
                per_token = lambda t: t[:, :, :].rearrange("p t (h e) -> p (t h) e", h=2)

                @block.tensor
                def _(pe):
                    pe.wait_ge(counted, 1)
                    for k in range(NBANK):
                        pe.matmul(INC[:, k, :], part("tri", p1=LNT), flat(chosen)[:, k * B:(k + 1) * B], start=True, stop=True)
                        mm = pe.matmul(TOT[:, k, :], part("ones", p1=LNT), flat(chosen)[:, k * B:(k + 1) * B],
                                       start=True, stop=True)
                    mm.then_inc(counted, 1)

                @block.scalar
                def _(act):
                    act.preload_act_table(ACT.Exp)
                    act.wait_ge(step, 2)
                    act.activation(flat(work), flat(work), ACT.Exp).then_inc(expd, 1)

                @block.vector
                def _(dve):
                    count = [0]

                    def chained(ins):
                        count[0] += 1
                        ins.then_inc(step, 1)
                        dve.wait_ge(step, count[0])

                    biggest, total, prob = (small[:, k, :] for k in range(3))
                    wide = lambda v: v.unsqueeze(2).broadcast_to([LNT, 2 * TILES, EXPERTS])
                    chained(dve.tensor_reduce(biggest, per_token(logits), AX, ALU.max))
                    chained(dve.tensor_tensor(per_token(work), per_token(logits), wide(biggest), ALU.subtract))
                    chained(dve.tensor_tensor(per_token(chosen), per_token(logits), wide(biggest), ALU.is_equal))
                    taken = total
                    chained(dve.tensor_copy(taken, per_token(chosen)[:, :, 0]))
                    for e in range(1, EXPERTS):
                        col = per_token(chosen)[:, :, e]
                        chained(dve.tensor_tensor(col, col, taken, ALU.is_gt))
                        chained(dve.tensor_tensor(taken, taken, col, ALU.max))
                    dve.sem_inc(counted, 1)
                    dve.wait_ge(expd, 1)
                    chained(dve.tensor_reduce(total, per_token(work), AX, ALU.add))
                    chained(dve.reciprocal(prob, total))
                    dve.wait_ge(counted, 2)
                    chained(dve.tensor_copy(before[:, :, :].rearrange("p e t -> p t e"),
                                            TOT[:, :, :].rearrange("p b (t e) -> p (b t) e", e=E2)))
                    sums = logits[:, :, :].rearrange("p t e -> p (t e)").rearrange("p (e t) -> p e t", e=E2)
                    one = part("ones", 0, 1, 0, LNT)
                    for e in range(E2):
                        chained(dve.tensor_tensor_scan(sums[:, e, :], one.broadcast_to([LNT, TILES]), before[:, e, :],
                                                       0.0 if e < EXPERTS else sums[:, e - EXPERTS, TILES - 1:TILES],
                                                       ALU.mult, ALU.add))
                    chained(dve.tensor_tensor(before[:, :, :], sums, before[:, :, :], ALU.subtract))
                    for k in range(NBANK):
                        t = B // E2
                        chained(dve.tensor_tensor(work[:, k * t:(k + 1) * t, :],
                                                  INC[:, k, :].rearrange("p (t e) -> p t e", e=E2),
                                                  before[:, :, k * t:(k + 1) * t].rearrange("p e t -> p t e"), ALU.add))
                    chained(dve.scalar_tensor_tensor(out=flat(work), in0=flat(work), scalar=float(CAP), in1=flat(chosen),
                                                     op0=ALU.is_le, op1=ALU.mult))
                    chained(dve.tensor_tensor(per_token(chosen), per_token(work), wide(prob), ALU.mult))
            with ExitStack() as inner:
                G = inner.enter_context(nc.psum_tensor("gate_G", [128, 2, 512], F32))
                turned, staged, out_, blank = (sem(n) for n in ("turned2", "staged2", "out2", "blank"))
                st = inner.enter_context(nc.sbuf_tensor("gate_st", [LNT, 2, KT, 128], F32))
                block = inner.enter_context(nc.Block())

                @block.tensor
                def _(pe):
                    with pe.Fori(0, CHUNKS // 2) as it:
                        for u in range(2):
                            c = it * 2 + u
                            pe.wait_ge(staged, c + 1)
                            pe.wait_ge(out_, c + 1)
                            for k in range(KT):
                                mm = pe.transpose(G[:, u, k * LNT:(k + 1) * LNT], st[:, u, k, :],
                                                  base("ident", 0, LNT, 0, LNT))
                            mm.then_inc(turned, 1)

                @block.scalar
                def _(act):
                    with act.Fori(0, CHUNKS // 2) as it:
                        for u in range(2):
                            c = it * 2 + u
                            act.wait_ge(turned, c + 3)
                            act.activation(gates[:, pick(c * STRIP, STRIP)], G[:, u, 0:STRIP], ACT.Copy).then_inc(out_, 1)

                @block.vector
                def _(dve):
                    dve.sem_inc(out_, 2)
                    dve.sem_inc(turned, 2)
                    dve.memset(st[:, :, :, :], 0.0).then_inc(blank, 1)
                    dve.wait_ge(blank, 1)
                    with dve.Fori(0, CHUNKS // 2) as it:
                        for u in range(2):
                            c = it * 2 + u
                            dve.wait_ge(turned, c + 1)
                            dve.tensor_copy(st[:, u, :, 0:E2], chosen[:, pick(c * KT, KT), :]).then_inc(staged, 1)

    def experts(res, y, gates):
        name = "moe"
        with phase() as ctx:
            sb = lambda n, s, d=F32: ctx.enter_context(nc.sbuf_tensor(f"{name}_{n}", s, d))
            sem = lambda n: nc.alloc_semaphore(f"{name}_{n}")
            ctile, part = load(ctx, name, MOE)
            g = sb("g", [128, 4, STRIP])
            gate = sb("gate", [128, 2, STRIP])
            term = sb("term", [128, STRIP])
            total = sb("total", [128, STRIP])
            flag = sb("flag", [128, 3, STRIP], I32)
            fill = sb("fill", [128, 3, STRIP])
            spare = sb("spare", [128, 1])
            H = ctx.enter_context(nc.psum_tensor("moe_H", [128, 4, 512], F32))
            G = ctx.enter_context(nc.psum_tensor("moe_G", [128, 2, 512], F32))
            O = ctx.enter_context(nc.psum_tensor("moe_O", [128, 2, 512], F32))
            loaded, hidden, relu_a, relu_d, used, gated, gate_out, read, step, filled, bias_made, bias_read = (
                sem(n) for n in ("loaded", "hidden", "relu_a", "relu_d", "used", "gated", "gate_out", "read", "step",
                                 "filled", "bias_made", "bias_read"))
            block = ctx.enter_context(nc.Block())
            FLT_MAX = 3.4028234663852886e38

            @block.sync
            def _(sp):
                sp.dma_start(ctile[:, :], dram["moe"]).then_inc(loaded, 16)

            @block.tensor
            def _(pe):
                pe.wait_ge(loaded, 16)
                with pe.Fori(0, CHUNKS) as c:
                    for e in range(EXPERTS):
                        n = c * EXPERTS + e
                        if e == 0:
                            pe.wait_ge(bias_read, c + 1)
                        pe.wait_ge(gate_out, n + 1)
                        pe.matmul(G[:, e % 2, 0:STRIP], part("sel", e * 128, 128), gates[:, pick(c * STRIP, STRIP)],
                                  start=True, stop=True).then_inc(gated, 1)
                        for q in range(4):
                            pe.wait_ge(relu_a if q % 2 == 0 else relu_d, n * 2 + q // 2 + 1)
                            pe.matmul(H[:, q, 0:STRIP], part("w1", e * 512 + q * 128, 128), y[:, pick(c * STRIP, STRIP)],
                                      start=True, stop=True).then_inc(hidden, 1)
                        pe.wait_ge(read, n + 1)
                        for q in range(4):
                            pe.wait_ge(relu_a if q % 2 == 0 else relu_d, n * 2 + q // 2 + 3)
                            pe.matmul(O[:, e % 2, 0:STRIP], part("w2", e * 512 + q * 128, 128), g[:, q, :],
                                      start=(q == 0), stop=(q == 3)).then_inc(used, 1)
                    pe.wait_ge(gate_out, c * EXPERTS + EXPERTS + 1)
                    pe.matmul(G[:, 0, 0:STRIP], part("b2"), gates[:, pick(c * STRIP, STRIP)],
                              start=True, stop=True).then_inc(bias_made, 1)

            @block.scalar
            def _(act):
                act.wait_ge(loaded, 16)
                with act.Fori(0, CHUNKS) as c:
                    for e in range(EXPERTS):
                        n = c * EXPERTS + e
                        act.wait_ge(gated, n + 1)
                        act.wait_ge(read, n + 1)
                        act.activation(gate[:, e % 2, :], G[:, e % 2, 0:STRIP], ACT.Copy).then_inc(gate_out, 1)
                        for q in (0, 2):
                            act.wait_ge(hidden, n * 4 + q + 1)
                            act.wait_ge(used, n * 4 + q + 1)
                            act.activation(g[:, q, :], H[:, q, 0:STRIP], ACT.Relu, bias=part("b1", e * 4 + q, 1))\
                               .then_inc(relu_a, 1)

            @block.vector
            def _(dve):
                dve.wait_ge(loaded, 16)
                for s, n in ((gate_out, 2), (relu_a, 2), (relu_d, 2), (read, 2), (used, 4), (bias_read, 1)):
                    dve.sem_inc(s, n)
                for k, v in enumerate((1e4, -1e4, 0.0)):
                    o = dve.memset(fill[:, k, :], v)
                o.then_inc(filled, 1)
                dve.wait_ge(filled, 1)
                STEPS = EXPERTS + EXPERTS + 8

                def output(c, n, e, at):
                    dve.wait_ge(used, n * 4 + 8)
                    dve.wait_ge(gate_out, n + 3)
                    dst = total if e == 0 else term
                    dve.tensor_tensor(dst[:, :], O[:, e % 2, 0:STRIP], gate[:, e % 2, :], ALU.mult).then_inc(read, 1)
                    if e:
                        dve.wait_ge(read, n + 3)
                        dve.tensor_tensor(total[:, :], total[:, :], term[:, :], ALU.add).then_inc(step, 1)
                        dve.wait_ge(step, c * STEPS_C + e)

                STEPS_C = (EXPERTS - 1) + 8
                with dve.Fori(0, CHUNKS) as c:
                    for e in range(EXPERTS):
                        n = c * EXPERTS + e
                        for q in (1, 3):
                            dve.wait_ge(hidden, n * 4 + q + 1)
                            dve.wait_ge(used, n * 4 + q + 1)
                            dve.tensor_scalar(g[:, q, :], H[:, q, 0:STRIP], part("b1", e * 4 + q, 1), 0.0,
                                              ALU.add, ALU.max).then_inc(relu_d, 1)
                        output(c, n, e, 0)
                    at = c * STEPS_C + EXPERTS - 1
                    dve.wait_ge(bias_made, c + 1)
                    dve.tensor_tensor(total[:, :], total[:, :], G[:, 0, 0:STRIP], ALU.add).then_inc(step, 1)
                    dve.wait_ge(step, at + 1)
                    dve.sem_inc(bias_read, 1)
                    dve.tensor_scalar(flag[:, 0, :], total[:, :], FLT_MAX, None, ALU.is_gt).then_inc(step, 1)
                    dve.tensor_scalar(flag[:, 1, :], total[:, :], -FLT_MAX, None, ALU.is_lt).then_inc(step, 1)
                    dve.tensor_tensor(flag[:, 2, :], total[:, :], total[:, :], ALU.not_equal).then_inc(step, 1)
                    dve.wait_ge(step, at + 4)
                    dve.memset(spare[:, :], 0.0)
                    for k in range(3):
                        dve.copy_predicated(total[:, :], flag[:, k, :], fill[:, k, :]).then_inc(step, 1)
                        dve.wait_ge(step, at + 5 + k)
                        dve.memset(spare[:, :], 0.0)
                    strip = res[:, pick(c * STRIP, STRIP)]
                    dve.tensor_tensor(strip, strip, total[:, :], ALU.add).then_inc(step, 1)
                    dve.wait_ge(step, at + 8)

    def time_mix(y, z, base):
        name = "mix"
        with phase() as ctx:
            sb = lambda n, s, d=F32: ctx.enter_context(nc.sbuf_tensor(f"{name}_{n}", s, d))
            ps = lambda n, s: ctx.enter_context(nc.psum_tensor(f"{name}_{n}", s, F32))
            sem = lambda n: nc.alloc_semaphore(f"{name}_{n}")
            ctile, part = load(ctx, name, RWKV)
            two = lambda n, w=STRIP: sb(n, [128, 2, w])
            k, v, uk, er = two("k"), two("v"), two("uk"), two("er")
            top, p, q = two("top", STRIP + 1), two("p", STRIP + 1), two("q", STRIP + 1)
            m, a, e, a2, e2, ev = two("m"), two("a"), two("e"), two("a2"), two("e2"), two("ev")
            mixed = two("mixed")
            w_t, u_t = sb("w_t", [128, 1]), sb("u_t", [128, 1])
            KP, VP, RP, OP = ps("KP", [128, 2, 512]), ps("VP", [128, 2, 512]), ps("RP", [128, 2, 512]), ps("OP", [128, 2, 512])
            loaded, set_up, k_made, v_made, r_made, k_out, v_out, gaps, exps, ready, made, added, step = (
                sem(n) for n in ("loaded", "set_up", "k_made", "v_made", "r_made", "k_out", "v_out", "gaps", "exps",
                                 "ready", "made", "added", "step"))
            block = ctx.enter_context(nc.Block())

            @block.sync
            def _(sp):
                sp.dma_start(ctile[:, :], dram["rwkv"]).then_inc(loaded, 16)

            @block.tensor
            def _(pe):
                pe.wait_ge(loaded, 16)
                with pe.Fori(0, CHUNKS // 2) as it:
                    for u in range(2):
                        c = it * 2 + u
                        pe.wait_ge(added, c + 1)
                        toks = z[:, pick(c * STRIP, STRIP)]
                        for P, w, s in ((KP, "wk", k_made), (VP, "wv", v_made), (RP, "wr", r_made)):
                            pe.matmul(P[:, u, 0:STRIP], part(w), toks, start=True, stop=True).then_inc(s, 1)
                    for u in range(2):
                        c = it * 2 + u
                        pe.wait_ge(ready, c + 1)
                        pe.matmul(OP[:, u, 0:STRIP], part("wo"), mixed[:, u, :], start=True, stop=True).then_inc(made, 1)

            @block.scalar
            def _(act):
                act.preload_act_table(ACT.Exp)
                act.wait_ge(set_up, 2)
                with act.Fori(0, CHUNKS // 2) as it:
                    for u in range(2):
                        c = it * 2 + u
                        act.wait_ge(k_made, c + 1)
                        act.activation(k[:, u, :], KP[:, u, 0:STRIP], ACT.Copy).then_inc(k_out, 1)
                        act.activation(uk[:, u, :], KP[:, u, 0:STRIP], ACT.Identity, bias=u_t[:, :]).then_inc(k_out, 1)
                        act.wait_ge(v_made, c + 1)
                        act.activation(v[:, u, :], VP[:, u, 0:STRIP], ACT.Copy).then_inc(v_out, 1)
                        act.wait_ge(r_made, c + 1)
                        act.activation(er[:, u, :], RP[:, u, 0:STRIP], ACT.Exp, scale=-1.0).then_inc(v_out, 1)
                    for u in range(2):
                        c = it * 2 + u
                        for n, t in enumerate((a2, e2, a, e)):
                            act.wait_ge(gaps, c * 4 + n + 1)
                            act.activation(t[:, u, :], t[:, u, :], ACT.Exp).then_inc(exps, 1)

            @block.vector
            def _(dve):
                dve.wait_ge(loaded, 16)
                dve.sem_inc(added, 2)
                dve.tensor_scalar(w_t[:, :], part("decay"), 1.0 / TOK, None, ALU.mult).then_inc(set_up, 1)
                dve.tensor_scalar(u_t[:, :], part("first"), 1.0 / TOK, None, ALU.mult).then_inc(set_up, 1)
                dve.wait_ge(set_up, 2)
                FRONT, BACK = 4, 13

                def front(c, u, at):
                    dve.wait_ge(step, at)
                    dve.wait_ge(k_out, c * 2 + 2)
                    now, nxt = top[:, u, 0:STRIP], top[:, u, 1:STRIP + 1]
                    dve.tensor_tensor_scan(nxt, w_t[:, :].broadcast_to([128, STRIP]), k[:, u, :], top[:, u, 0:1],
                                           ALU.add, ALU.max).then_inc(step, 1)
                    dve.wait_ge(step, at + 1)
                    dve.tensor_copy(top[:, 1 - u, 0:1], top[:, u, STRIP:STRIP + 1]).then_inc(step, 1)
                    dve.scalar_tensor_tensor(out=a2[:, u, :], in0=now, scalar=w_t[:, :], in1=nxt, op0=ALU.add,
                                             op1=ALU.subtract).then_inc(gaps, 1)
                    dve.tensor_tensor(e2[:, u, :], k[:, u, :], nxt, ALU.subtract).then_inc(gaps, 1)
                    dve.tensor_tensor(m[:, u, :], now, uk[:, u, :], ALU.max).then_inc(step, 1)
                    dve.wait_ge(step, at + 3)
                    dve.tensor_tensor(a[:, u, :], now, m[:, u, :], ALU.subtract).then_inc(gaps, 1)
                    dve.tensor_tensor(e[:, u, :], uk[:, u, :], m[:, u, :], ALU.subtract).then_inc(gaps, 1)
                    dve.wait_ge(gaps, c * 4 + 4)
                    dve.sem_inc(step, 1)

                def back(c, u, at):
                    def chained(ins, n):
                        ins.then_inc(step, 1)
                        dve.wait_ge(step, at + n)
                    dve.wait_ge(v_out, c * 2 + 2)
                    dve.wait_ge(exps, c * 4 + 4)
                    chained(dve.tensor_tensor(ev[:, u, :], e2[:, u, :], v[:, u, :], ALU.mult), 1)
                    chained(dve.tensor_tensor_scan(p[:, u, 1:STRIP + 1], a2[:, u, :], ev[:, u, :], p[:, u, 0:1],
                                                   ALU.mult, ALU.add), 2)
                    chained(dve.tensor_tensor_scan(q[:, u, 1:STRIP + 1], a2[:, u, :], e2[:, u, :], q[:, u, 0:1],
                                                   ALU.mult, ALU.add), 3)
                    chained(dve.tensor_copy(p[:, 1 - u, 0:1], p[:, u, STRIP:STRIP + 1]), 4)
                    chained(dve.tensor_copy(q[:, 1 - u, 0:1], q[:, u, STRIP:STRIP + 1]), 5)
                    chained(dve.tensor_tensor(m[:, u, :], a[:, u, :], p[:, u, 0:STRIP], ALU.mult), 6)
                    chained(dve.tensor_tensor(ev[:, u, :], e[:, u, :], v[:, u, :], ALU.mult), 7)
                    chained(dve.tensor_tensor(m[:, u, :], m[:, u, :], ev[:, u, :], ALU.add), 8)
                    chained(dve.tensor_tensor(a[:, u, :], a[:, u, :], q[:, u, 0:STRIP], ALU.mult), 9)
                    chained(dve.tensor_tensor(a[:, u, :], a[:, u, :], e[:, u, :], ALU.add), 10)
                    chained(dve.scalar_tensor_tensor(out=a[:, u, :], in0=er[:, u, :], scalar=1.0, in1=a[:, u, :],
                                                     op0=ALU.add, op1=ALU.mult), 11)
                    chained(dve.reciprocal(e[:, u, :], a[:, u, :]), 12)
                    chained(dve.tensor_tensor(mixed[:, u, :], m[:, u, :], e[:, u, :], ALU.mult), 13)
                    dve.sem_inc(ready, 1)

                def add(c, u):
                    dve.wait_ge(made, c + 1)
                    strip = y[:, pick(c * STRIP, STRIP)]
                    dve.tensor_tensor(strip, OP[:, u, 0:STRIP], strip, ALU.add).then_inc(added, 1)

                PER = 2 * (FRONT + BACK)
                with dve.Fori(0, HALF_IMGS) as img:
                    start = img * (PER * (STRIPS // 2) + 3)
                    dve.memset(top[:, 0, 0:1], -1e38).then_inc(step, 1)
                    dve.memset(p[:, 0, 0:1], 0.0).then_inc(step, 1)
                    dve.memset(q[:, 0, 0:1], 0.0).then_inc(step, 1)
                    with dve.Fori(0, STRIPS // 2) as i:
                        at = start + 3 + i * PER
                        for u in range(2):
                            front(img * STRIPS + i * 2 + u, u, at + FRONT * u)
                        for u in range(2):
                            back(img * STRIPS + i * 2 + u, u, at + 2 * FRONT + BACK * u)
                        for u in range(2):
                            add(img * STRIPS + i * 2 + u, u)

    def channel_mix(res, y, z):
        name = "cmix"
        with phase() as ctx:
            sb = lambda n, s, d=F32: ctx.enter_context(nc.sbuf_tensor(f"{name}_{n}", s, d))
            sem = lambda n: nc.alloc_semaphore(f"{name}_{n}")
            ctile, part = load(ctx, name, RWKV_FFN)
            g = sb("g", [128, 4, STRIP])
            g2 = sb("g2", [128, 4, STRIP])
            sig = sb("sig", [128, 2, STRIP])
            t = sb("t", [128, 2, STRIP])
            H = ctx.enter_context(nc.psum_tensor("cmix_H", [128, 4, 512], F32))
            R = ctx.enter_context(nc.psum_tensor("cmix_R", [128, 2, 512], F32))
            O = ctx.enter_context(nc.psum_tensor("cmix_O", [128, 2, 512], F32))
            loaded, hidden, relued, squared, used, r_made, sig_made, step, done = (
                sem(n) for n in ("loaded", "hidden", "relued", "squared", "used", "r_made", "sig_made", "step", "done"))
            block = ctx.enter_context(nc.Block())

            @block.sync
            def _(sp):
                sp.dma_start(ctile[:, :], dram["rwkv_ffn"]).then_inc(loaded, 16)

            @block.tensor
            def _(pe):
                pe.wait_ge(loaded, 16)
                with pe.Fori(0, CHUNKS // 2) as it:
                    for u in range(2):
                        c = it * 2 + u
                        toks = z[:, pick(c * STRIP, STRIP)]
                        pe.wait_ge(done, c + 1)
                        pe.matmul(R[:, u, 0:STRIP], part("wr"), toks, start=True, stop=True).then_inc(r_made, 1)
                        for q in range(4):
                            pe.wait_ge(relued, c * 4 + q + 1)
                            pe.matmul(H[:, q, 0:STRIP], part("w1", q * 128, 128), toks, start=True, stop=True)\
                              .then_inc(hidden, 1)
                        for q in range(4):
                            pe.wait_ge(squared, c * 4 + q + 1)
                            pe.matmul(O[:, u, 0:STRIP], part("w2", q * 128, 128), g2[:, q, :],
                                      start=(q == 0), stop=(q == 3)).then_inc(used, 1)

            @block.scalar
            def _(act):
                act.preload_act_table(ACT.Sigmoid)
                with act.Fori(0, CHUNKS // 2) as it:
                    for u in range(2):
                        c = it * 2 + u
                        act.wait_ge(r_made, c + 1)
                        act.activation(sig[:, u, :], R[:, u, 0:STRIP], ACT.Sigmoid).then_inc(sig_made, 1)
                        for q in range(4):
                            act.wait_ge(hidden, c * 4 + q + 1)
                            act.activation(g[:, q, :], H[:, q, 0:STRIP], ACT.Relu).then_inc(relued, 1)

            @block.vector
            def _(dve):
                dve.sem_inc(relued, 4)
                dve.sem_inc(used, 4)
                dve.sem_inc(done, 2)
                with dve.Fori(0, CHUNKS // 2) as it:
                    for u in range(2):
                        c = it * 2 + u
                        for q in range(4):
                            dve.wait_ge(relued, c * 4 + q + 5)
                            dve.wait_ge(used, c * 4 + q + 1)
                            dve.tensor_tensor(g2[:, q, :], g[:, q, :], g[:, q, :], ALU.mult).then_inc(squared, 1)
                        strip = slice(None), pick(c * STRIP, STRIP)
                        dve.wait_ge(used, c * 4 + 8)
                        dve.wait_ge(sig_made, c + 1)
                        dve.tensor_tensor(t[:, u, :], O[:, u, 0:STRIP], sig[:, u, :], ALU.mult).then_inc(step, 1)
                        dve.wait_ge(step, c * 2 + 1)
                        dve.tensor_tensor(t[:, u, :], t[:, u, :], y[strip], ALU.add).then_inc(step, 1)
                        dve.wait_ge(step, c * 2 + 2)
                        dve.tensor_tensor(res[strip], res[strip], t[:, u, :], ALU.add).then_inc(done, 1)

    def routed_mlp(res, y, base):
        name = "rt"
        with phase() as ctx:
            sb = lambda n, s, d=F32: ctx.enter_context(nc.sbuf_tensor(f"{name}_{n}", s, d))
            ps = lambda n, s: ctx.enter_context(nc.psum_tensor(f"{name}_{n}", s, F32))
            sem = lambda n: nc.alloc_semaphore(f"{name}_{n}")
            ctile, part = load(ctx, name, ROUTED)
            route = sb("route", [1, 2 * CHUNKS], I32)
            wsel = sb("wsel", [128, 2, ROUTE_LAYERS, RH])
            bsel = sb("bsel", [128, 2, ROUTE_LAYERS])
            h = sb("h", [128, 2, 1 + ROUTE_LAYERS, STRIP])
            P = ps("P", [128, 2, 2, 512])
            O = ps("O", [128, 2, 512])
            loaded, shared_made, weights, made, relued, out_made, added = (
                sem(n) for n in ("loaded", "shared_made", "weights", "made", "relued", "out_made", "added"))
            block = ctx.enter_context(nc.Block())
            LAYERS = 1 + ROUTE_LAYERS

            @block.sync
            def _(sp):
                sp.dma_start(ctile[:, :], dram["routed"]).then_inc(loaded, 16)
                sp.dma_start(route[:, :], dram["route"]).then_inc(loaded, 16)

            @block.tensor
            def _(pe):
                pe.wait_ge(loaded, 32)
                with pe.Fori(0, CHUNKS // 2) as it:
                    for u in range(2):
                        c = it * 2 + u
                        pe.wait_ge(added, c + 1)
                        for l in range(LAYERS):
                            for s in range(2):
                                n = (c * LAYERS + l) * 2 + s
                                pe.wait_ge(relued, n + 1)
                                if l == 0:
                                    lhs, rhs = part("wi", s * RH, RH), y[:, pick(c * STRIP, STRIP)]
                                else:
                                    pe.wait_ge(weights, c * 4 + s * 2 + l)
                                    lhs, rhs = wsel[:, s, l - 1, :], h[:, s, l - 1, :]
                                pe.matmul(P[:, s, 0, 0:STRIP], lhs, rhs, start=True, stop=True).then_inc(made, 1)
                        for s in range(2):
                            pe.wait_ge(relued, (c * LAYERS + LAYERS) * 2 + s + 1)
                            mm = pe.matmul(O[s * C:(s + 1) * C, u, 0:STRIP], part("wo"), h[:, s, LAYERS - 1, :],
                                           start=True, stop=True)
                        mm.then_inc(out_made, 1)

            @block.scalar
            def _(act):
                act.wait_ge(loaded, 32)
                with act.Fori(0, CHUNKS) as c:
                    for l in range(LAYERS):
                        for s in range(2):
                            n = (c * LAYERS + l) * 2 + s
                            act.wait_ge(made, n + 1)
                            bias = part("bi") if l == 0 else bsel[:, s, l - 1:l]
                            act.activation(h[:, s, l, :], P[:, s, 0, 0:STRIP], ACT.Relu, bias=bias).then_inc(relued, 1)

            @block.vector
            def _(dve):
                dve.wait_ge(loaded, 32)
                dve.sem_inc(added, 2)
                dve.sem_inc(relued, 2)
                for l in range(ROUTE_LAYERS):
                    ws = part("ws", l * RH, RH)
                    dve.tensor_tensor(ws, ws, base("ident"), ALU.add).then_inc(shared_made, 1)
                dve.wait_ge(shared_made, ROUTE_LAYERS)
                at_w, at_b = ROUTED["wr"][0], ROUTED["br"][0]

                def select(c):
                    dve.wait_ge(relued, c * (2 * LAYERS) + 2)
                    for s in range(2):
                        r = dve.value_load(route[0:1, pick(c + s * CHUNKS, 1)], min_val=0, max_val=ROUTES - 1)
                        for l in range(ROUTE_LAYERS):
                            dve.tensor_tensor(bsel[:, s, l:l + 1], part("bs", l, 1),
                                              ctile[:, pick(r + (at_b + l * ROUTES), 1)], ALU.add)
                            dve.tensor_tensor(wsel[:, s, l, :], part("ws", l * RH, RH),
                                              ctile[:, pick(r * RH + (at_w + l * ROUTES * RH), RH)], ALU.add)\
                               .then_inc(weights, 1)

                with dve.Fori(0, CHUNKS // 2) as it:
                    for u in range(2):
                        c = it * 2 + u
                        select(c)
                        dve.wait_ge(out_made, c + 1)
                        strip = res[:, pick(c * STRIP, STRIP)]
                        dve.scalar_tensor_tensor(out=strip, in0=O[:, u, 0:STRIP], scalar=part("bo"), in1=strip,
                                                 op0=ALU.add, op1=ALU.add).then_inc(added, 1)

    with ExitStack() as ctx:
        base_tile, base = load(ctx, "base", BASE)
        X = ctx.enter_context(nc.sbuf_tensor("X", [128, COLS], F32))
        Y = ctx.enter_context(nc.sbuf_tensor("Y", [128, COLS], F32))
        entered = ctx.enter_context(nc.semaphore("entered"))
        stored = ctx.enter_context(nc.semaphore("stored"))
        with nc.Block() as block:
            @block.sync
            def _(sp):
                sp.dma_start(base_tile[:, :], dram["base"]).then_inc(entered, 16)
                sp.dma_start(Y[0:32, :], dram["patches"]).then_inc(entered, 16)
                sp.wait_ge(entered, 32)

        def steps():
            res, tmp = X, Y
            patch_embed(tmp, res, base)
            layernorm("ln_pe", res, res, base, base("pe_g"), base("pe_nb"))
            if STOP <= 0:
                return res
            for b in range(2):
                if b:
                    roll("roll1", res, tmp, SHIFT)
                    res, tmp = tmp, res
                layernorm(f"ln1_{b}", res, tmp, base, base("n1g", b, 1), base("n1b", b, 1))
                window_attention(b, res, tmp, base)
                if STOP <= 1:
                    return res
                layernorm(f"ln2_{b}", res, tmp, base, base("n2g", b, 1), base("n2b", b, 1))
                mlp(b, res, tmp, base)
                if STOP <= 2:
                    return res
            roll("roll2", res, tmp, SIDE - SHIFT)
            res, tmp = tmp, res
            if STOP <= 3:
                return res
            layernorm("ln_att", res, tmp, base)
            image_attention(res, tmp, base)
            if STOP <= 4:
                return res
            layernorm("ln_moe", res, tmp, base)
            with nc.sbuf_tensor("gates", [128, COLS], F32) as gates:
                routing(tmp, gates, base)
                experts(res, tmp, gates)
            if STOP <= 5:
                return res
            layernorm("ln_rwkv", res, tmp, base)
            with nc.sbuf_tensor("Z", [128, COLS], F32) as Z:
                layernorm("ln_mix", tmp, Z, base, base("rg1"), base("rb1"))
                time_mix(tmp, Z, base)
                layernorm("ln_cmix", tmp, Z, base, base("rg2"), base("rb2"))
                channel_mix(res, tmp, Z)
            if STOP <= 6:
                return res
            layernorm("ln_rt", res, tmp, base)
            routed_mlp(res, tmp, base)
            return res

        res = steps()
        with nc.Block() as block:
            @block.sync
            def _(sp):
                sp.dma_start(out, res[:, :]).then_inc(stored, 16)
                sp.wait_ge(stored, 16)


def halves(v):
    return np.concatenate([v, v])


def diagonal(w):
    a, b = w.shape
    o = np.zeros((128, 2 * b), np.float32)
    o[0:a, 0:b] = w
    o[64:64 + a, b:] = w
    return o


def groups_of_hidden(w1, w2):
    up = np.concatenate([diagonal(w1[:, q * 64:(q + 1) * 64]) for q in range(4)], 1)
    down = np.concatenate([diagonal(w2[q * 64:(q + 1) * 64]) for q in range(4)], 1)
    return up, down


def pack(cols, **parts):
    o = np.zeros((128, cols["_"][1]), np.float32)
    for name, v in parts.items():
        at, w = cols[name]
        v = np.asarray(v, np.float32)
        v = v[:, None] if v.ndim == 1 else v
        assert v.shape[1] == w, (name, v.shape, w)
        o[:v.shape[0], at:at + w] = v
    return o


def lay_out(i):
    i = {k: np.asarray(v) for k, v in i.items()}
    p = i["x"].reshape(2, HALF_IMGS, SIDE, 4, SIDE, 4).transpose(0, 3, 5, 1, 2, 4).reshape(32, COLS)
    mean = np.kron(np.eye(2), np.full((C, C), 1.0 / C))
    bd = diagonal
    two = lambda v: np.stack([halves(v[0]), halves(v[1])], 1)
    pe = np.zeros((32, 128), np.float32)
    w16 = i["L0_tok_pe_w"].reshape(C, 16).T
    pe[0:16, 0:64] = w16
    pe[16:32, 64:128] = w16
    base = pack(BASE, ident=np.eye(128), center=np.eye(128) - mean, mean=mean, eps=np.full(128, EPS),
                pe_w=pe, pe_b=halves(i["L0_tok_pe_b"]), pe_g=halves(i["L0_tok_pe_ng"]), pe_nb=halves(i["L0_tok_pe_nb"]),
                n1g=two(i["L0_tok_n1g"]), n1b=two(i["L0_tok_n1b"]), n2g=two(i["L0_tok_n2g"]), n2b=two(i["L0_tok_n2b"]),
                rg1=halves(i["L1_attn_g1"]), rb1=halves(i["L1_attn_b1"]), rg2=halves(i["L1_attn_g2"]), rb2=halves(i["L1_attn_b2"]))
    swin, mlps, rpbs = [], [], []
    yx = np.stack(np.meshgrid(np.arange(WS), np.arange(WS), indexing="ij")).reshape(2, -1)
    rel = (yx[:, :, None] - yx[:, None, :]) + WS - 1
    rpi = rel[0] * (2 * WS - 1) + rel[1]
    headmask = np.zeros((128, HEADS), np.float32)
    for k in range(128):
        headmask[k, (k % 64) // HD] = 1.0
    for b in range(2):
        wq, wk, wv = (i["L0_tok_qkv_w"][b, n * C:(n + 1) * C].T for n in range(3))
        bq, bk, bv = (halves(i["L0_tok_qkv_b"][b, n * C:(n + 1) * C]) for n in range(3))
        swin.append(pack(SWIN, wq=bd(wq), wk=bd(wk), wv=np.concatenate([wv, wv]), wp=bd(i["L0_tok_proj_w"][b].T),
                         bq=bq, bk=bk, bv=bv, bp=halves(i["L0_tok_proj_b"][b]), headmask=headmask))
        up, down = groups_of_hidden(i["L0_tok_w1"][b].T, i["L0_tok_w2"][b].T)
        b1 = i["L0_tok_b1"][b].reshape(4, 64)
        mlps.append(pack(MLP, w1=up, w2=down, b1=np.concatenate([b1.T, b1.T]), b2=halves(i["L0_tok_b2"][b])))
        t = i["L0_tok_rpb"][b][rpi].transpose(0, 2, 1).reshape(WIN, HEADS * WIN)
        r = np.zeros((128, HEADS * WIN), np.float32)
        r[0:WIN] = t
        r[64:64 + WIN] = t
        rpbs.append(r)
    region = np.zeros((SIDE, SIDE), np.int32)
    n = 0
    for a in (slice(0, -WS), slice(-WS, -SHIFT), slice(-SHIFT, None)):
        for c in (slice(0, -WS), slice(-WS, -SHIFT), slice(-SHIFT, None)):
            n += 1
            region[a, c] = n
    mw = region.reshape(NW, WS, NW, WS).transpose(0, 2, 1, 3).reshape(NW, NW, WIN)
    masks = np.zeros((128, 3, HEADS, WIN), np.float32)
    for k, (a, c) in enumerate(((0, NW - 1), (NW - 1, 0), (NW - 1, NW - 1))):
        m = np.where(mw[a, c][None, :] != mw[a, c][:, None], -100.0, 0.0).astype(np.float32)
        masks[0:WIN, k] = m[:, None, :]
        masks[64:64 + WIN, k] = m[:, None, :]
    wide = lambda a: np.concatenate([a, np.zeros((128, 112), np.float32)], 1)
    att = pack(ATT, wq=bd(i["L0_attn_Wq"]), wk=bd(i["L0_attn_Wk"]), wv=bd(i["L0_attn_Wv"]))
    gate = pack(GATE, gw=wide(bd(i["L0_ffn_gate_w"])), gb=wide(np.tile(i["L0_ffn_gate_b"], (128, 2))),
                tri=np.triu(np.ones((LNT, LNT))), ones=np.ones((LNT, LNT)))
    ups, downs, b1s, sel = [], [], [], np.zeros((16, EXPERTS, 128), np.float32)
    b2 = np.zeros((16, 128), np.float32)
    for e in range(EXPERTS):
        up, down = groups_of_hidden(i["L0_ffn_w1"][e], i["L0_ffn_w2"][e])
        ups.append(up)
        downs.append(down)
        b = i["L0_ffn_b1"][e].reshape(4, 64).T
        b1s.append(np.concatenate([b, b]))
        for h in range(2):
            sel[8 * h + e, e, 64 * h:64 * h + 64] = 1.0
            b2[8 * h + e, 64 * h:64 * h + 64] = i["L0_ffn_b2"][e]
    moe = pack(MOE, w1=np.concatenate(ups, 1), w2=np.concatenate(downs, 1), b1=np.concatenate(b1s, 1), b2=b2,
               sel=sel.reshape(16, -1))
    rwkv = pack(RWKV, wk=bd(i["L1_attn_Wk"]), wv=bd(i["L1_attn_Wv"]), wr=bd(i["L1_attn_Wr"]), wo=bd(i["L1_attn_Wo"]),
                decay=halves(i["L1_attn_spatial_decay"]), first=halves(i["L1_attn_spatial_first"]))
    up, down = groups_of_hidden(i["L1_attn_Wk_ffn"], i["L1_attn_Wv_ffn"])
    rwkv_ffn = pack(RWKV_FFN, wr=bd(i["L1_attn_Wr_ffn"]), w1=up, w2=down)
    wi = np.zeros((128, 2 * RH), np.float32)
    wi[0:64, 0:RH] = i["L1_ffn_Wi"].T
    wi[64:128, RH:] = i["L1_ffn_Wi"].T
    routed = pack(ROUTED, wi=wi, bi=i["L1_ffn_bi"], wr=i["L1_ffn_Wr"].transpose(3, 0, 1, 2).reshape(128, -1),
                  br=i["L1_ffn_br"].transpose(2, 0, 1).reshape(128, -1),
                  ws=i["L1_ffn_Ws"][:, 0].transpose(2, 0, 1).reshape(128, -1), bs=i["L1_ffn_bs"][:, 0].T,
                  wo=i["L1_ffn_Wo"].T, bo=halves(i["L1_ffn_bo"]))
    return {"att": att, "gate": gate, "moe": moe, "rwkv": rwkv, "rwkv_ffn": rwkv_ffn, "routed": routed,
            "route": i["L1_ffn_route_id"].reshape(1, -1), "patches": p, "base": base, "swin": np.stack(swin), "mlp": np.stack(mlps), "rpb": np.stack(rpbs),
            "masks": masks.reshape(128, 3, HEADS * WIN)}


def kernel(**inputs):
    import concourse.bacc as _bacc
    from concourse import mybir as _mybir
    from concourse.bass_utils import run_bass_kernel_spmd as _run

    nc = _bacc.Bacc("TRN2", target_bir_lowering=False, num_devices=1)
    arrays = {f"in_{k}": np.ascontiguousarray(v) for k, v in lay_out(inputs).items()}
    dram = {k[3:]: nc.dram_tensor(k, a.shape, _mybir.dt.from_np(a.dtype), kind="ExternalInput").ap()
            for k, a in arrays.items()}
    out = nc.dram_tensor("out", [128, COLS], _mybir.dt.float32, kind="ExternalOutput").ap()
    build(nc, dram, out)
    r = _run(nc, [arrays], core_ids=[0])
    got = np.asarray(r.results[0]["out"])
    return got.reshape(2, C, HALF_IMGS, TOK).transpose(0, 2, 3, 1).reshape(IMGS, TOK, C)
```

```python
import numpy as np

C = 64
IMGS, SIDE = 8, 56
HALF_IMGS = IMGS // 2
TOK = SIDE * SIDE
COLS = HALF_IMGS * TOK
WS = 7
WIN = WS * WS
STRIP = WS * SIDE
STRIPS = SIDE // WS
CHUNKS = COLS // STRIP
NW = SIDE // WS
HEADS, HD = 8, 8
SHIFT = WS // 2
HID = 256
EPS = 1e-5
UN = 4
LNT = 98
KT = STRIP // LNT
EXPERTS = 8
CAP = 3920
QT = 112
QTILES = TOK // QT
KG = 4
KPG = QTILES // KG
ROUTES = 16
ROUTE_LAYERS = 2
RH = 128
STOP = 99

def table(*items):
    at, out = 0, {}
    for name, width in items:
        out[name] = (at, width)
        at += width
    out["_"] = (0, at)
    return out


BASE = table(("ident", 128), ("center", 128), ("mean", 128), ("eps", 1), ("pe_w", HALF_IMGS * 128), ("pe_b", 1),
             ("pe_g", 1), ("pe_nb", 1), ("n1g", 2), ("n1b", 2), ("n2g", 2), ("n2b", 2),
             ("rg1", 1), ("rb1", 1), ("rg2", 1), ("rb2", 1))
SWIN = table(("wq", 128), ("wk", 128), ("wv", 64), ("wp", 128), ("bq", 1), ("bk", 1), ("bv", 1), ("bp", 1),
             ("headmask", HEADS))
MLP = table(("w1", 4 * 128), ("w2", 4 * 128), ("b1", 4), ("b2", 1))
ATT = table(("wq", 256), ("wk", 256), ("wv", 128))
GATE = table(("gw", 128), ("gb", 128), ("tri", LNT), ("ones", LNT))
MOE = table(("w1", EXPERTS * 512), ("w2", EXPERTS * 512), ("b1", EXPERTS * 4), ("b2", EXPERTS),
            ("sel", EXPERTS * 128))
RWKV = table(("wk", 128), ("wv", 128), ("wr", 128), ("wo", 128), ("decay", 1), ("first", 1))
RWKV_FFN = table(("wr", 128), ("w1", 512), ("w2", 512))
ROUTED = table(("wi", 2 * RH), ("bi", 1), ("wr", ROUTE_LAYERS * ROUTES * RH), ("br", ROUTE_LAYERS * ROUTES),
               ("ws", ROUTE_LAYERS * RH), ("bs", ROUTE_LAYERS), ("wo", C), ("bo", 1))


def build(nc, dram, out):
    from contextlib import ExitStack, contextmanager

    import concourse.bass as bass
    from concourse import mybir

    F32 = mybir.dt.float32
    BF16 = mybir.dt.bfloat16
    I32 = mybir.dt.int32
    ALU = mybir.AluOpType
    ACT = mybir.ActivationFunctionType
    AX = mybir.AxisListType.X
    pick = bass.ds

    def strip_by_row(ap):
        return ap.rearrange("p (a b k) -> p a b k", a=WS, b=NW)

    def strip_by_window(ap):
        return ap.rearrange("p (a b k) -> p b a k", a=WS, b=NW)

    @contextmanager
    def phase():
        with nc.cleanup_on_exit(), ExitStack() as ctx:
            yield ctx

    def load(ctx, name, cols):
        width = cols["_"][1]
        tile = ctx.enter_context(nc.sbuf_tensor(f"c_{name}", [128, width], F32))

        def part(key, a=0, n=None, p0=0, p1=128):
            at, w = cols[key]
            n = w - a if n is None else n
            return tile[p0:p1, at + a:at + a + n]
        return tile, part

    def warm_up(pe, bank, base):
        for _ in range(9):
            pe.matmul(bank[:, 0:256], base("center"), base("ident", 0, 256), start=True, stop=True)

    def layernorm(name, src, dst, base, gamma=None, beta=None):
        affine = gamma is not None
        with phase() as ctx:
            sb = lambda n, s, d=F32: ctx.enter_context(nc.sbuf_tensor(f"{name}_{n}", s, d))
            sem = lambda n: nc.alloc_semaphore(f"{name}_{n}")
            xs = sb("xs", [128, UN, STRIP])
            r = sb("r", [128, UN, STRIP])
            t = sb("t", [128, UN, STRIP]) if affine else None
            A = ctx.enter_context(nc.psum_tensor(f"{name}_A", [128, UN, 512], F32))
            V = ctx.enter_context(nc.psum_tensor(f"{name}_V", [128, UN, 512], F32))
            centered, copied, squared, averaged, logged, inverted, scaled, done = (
                sem(n) for n in ("centered", "copied", "squared", "averaged", "logged", "inverted", "scaled", "done"))
            block = ctx.enter_context(nc.Block())

            def cols(c):
                return pick(c * STRIP, STRIP)

            def after(eng, s, c):
                eng.wait_ge(s, c + 1)

            def passed(eng, s, c):
                eng.wait_ge(s, c + 1 + UN)

            def pipeline(eng, *stages):
                def turn(c0, first=False, tail=False):
                    for u in range(max(lag for lag, _ in stages) if tail else UN):
                        for lag, stage in stages:
                            v = u - lag
                            if (v >= 0 and not tail) or (v < 0 and not first):
                                stage(c0 + v, v % UN)
                turn(0, first=True)
                with eng.Fori(1, CHUNKS // UN) as it:
                    turn(it * UN)
                turn(CHUNKS, tail=True)

            @block.tensor
            def _(pe):
                def center(c, u):
                    after(pe, copied, c)
                    pe.matmul(A[:, u, 0:STRIP], base("center"), src[:, cols(c)], start=True, stop=True)\
                      .then_inc(centered, 1)

                def average(c, u):
                    after(pe, logged, c)
                    pe.wait_ge(squared, c + 1)
                    pe.matmul(V[:, u, 0:STRIP], base("mean"), r[:, u, :], start=True, stop=True).then_inc(averaged, 1)

                pipeline(pe, (0, center), (1, average))

            @block.scalar
            def _(act):
                act.preload_act_table_set("natural_log_exp_and_others")

                def square(c, u):
                    after(act, scaled, c)
                    passed(act, copied, c)
                    act.activation(r[:, u, :], xs[:, u, :], ACT.Square).then_inc(squared, 1)

                def log(c, u):
                    act.wait_ge(averaged, c + 1)
                    act.activation(r[:, u, :], V[:, u, 0:STRIP], ACT.Ln, bias=base("eps")).then_inc(logged, 1)

                def invert(c, u):
                    passed(act, logged, c)
                    act.activation(r[:, u, :], r[:, u, :], ACT.Exp, scale=-0.5).then_inc(inverted, 1)

                pipeline(act, (0, square), (1, log), (1, invert))

            @block.vector
            def _(dve):
                def copy(c, u):
                    dve.wait_ge(centered, c + 1)
                    after(dve, scaled, c)
                    dve.tensor_copy(xs[:, u, :], A[:, u, 0:STRIP]).then_inc(copied, 1)

                def scale(c, u):
                    dve.wait_ge(inverted, c + 1)
                    if affine:
                        after(dve, done, c)
                    dve.tensor_tensor(t[:, u, :] if affine else dst[:, cols(c)], xs[:, u, :], r[:, u, :],
                                      ALU.mult).then_inc(scaled, 1)

                def transform(c, u):
                    passed(dve, scaled, c)
                    dve.tensor_scalar(dst[:, cols(c)], t[:, u, :], gamma, beta, ALU.mult, ALU.add).then_inc(done, 1)

                for s in (copied, scaled, logged, done):
                    dve.sem_inc(s, UN)
                if affine:
                    pipeline(dve, (0, copy), (2, scale), (2, transform))
                else:
                    pipeline(dve, (0, copy), (2, scale))

    def patch_embed(patches, dst, base):
        with phase() as ctx:
            P = ctx.enter_context(nc.psum_tensor("pe_P", [128, UN, 512], F32))
            made = nc.alloc_semaphore("pe_made")
            done = nc.alloc_semaphore("pe_done")
            block = ctx.enter_context(nc.Block())

            @block.tensor
            def _(pe):
                for j in range(HALF_IMGS):
                    with pe.Fori(0, STRIPS // UN) as it:
                        for u in range(UN):
                            pe.wait_ge(done, it * UN + (j * STRIPS + u + 1))
                            pe.matmul(P[:, u, 0:STRIP], base("pe_w", j * 128, 128),
                                      patches[:, pick(it * (UN * STRIP) + u * STRIP, STRIP)],
                                      start=True, stop=True).then_inc(made, 1)

            @block.vector
            def _(dve):
                dve.sem_inc(done, UN)
                with dve.Fori(0, CHUNKS // UN) as it:
                    for u in range(UN):
                        dve.wait_ge(made, it * UN + u + 1)
                        dve.tensor_scalar(dst[:, pick(it * (UN * STRIP) + u * STRIP, STRIP)], P[:, u, 0:STRIP],
                                          base("pe_b"), None, ALU.add).then_inc(done, 1)

    def roll(name, src, dst, shift):
        s = src[:, :].rearrange("p (i y x) -> p i y x", i=HALF_IMGS, y=SIDE)
        d = dst[:, :].rearrange("p (i y x) -> p i y x", i=HALF_IMGS, y=SIDE)
        cut = SIDE - shift
        spans = ((0, cut, shift), (cut, SIDE, -cut))
        with phase() as ctx:
            block = ctx.enter_context(nc.Block())

            def copies(eng, images):
                for i in images:
                    for y0, y1, dy in spans:
                        for x0, x1, dx in spans:
                            yield d[:, i, y0:y1, x0:x1], s[:, i, y0 + dy:y1 + dy, x0 + dx:x1 + dx]

            @block.vector
            def _(dve):
                for o, i in copies(dve, (0, 1, 2)):
                    dve.tensor_copy(o, i)

            @block.scalar
            def _(act):
                for o, i in copies(act, (3,)):
                    act.activation(o, i, ACT.Copy)

    def window_attention(b, res, y, base):
        name = f"wa{b}"
        with phase() as ctx:
            sb = lambda n, s, d=F32: ctx.enter_context(nc.sbuf_tensor(f"{name}_{n}", s, d))
            ps = lambda n, s: ctx.enter_context(nc.psum_tensor(f"{name}_{n}", s, F32))
            sem = lambda n: nc.alloc_semaphore(f"{name}_{n}")
            ctile, part = load(ctx, name, SWIN)
            yw = sb("yw", [128, NW, 128])
            kexp = sb("kexp", [128, 2, HEADS, STRIP])
            qbd = sb("qbd", [128, 2, NW, 128])
            vexp = sb("vexp", [128, 2, 2, NW, 4, C])
            bias = sb("bias", [128, 4, HEADS * WIN])
            biask = sb("biask", [128, HEADS])
            scores = sb("scores", [128, 4, HEADS * WIN])
            probs = sb("probs", [128, 4, HEADS, C])
            probsT = sb("probsT", [128, 2, 512])
            stat = sb("stat", [128, 4, 3, HEADS])
            osb = sb("osb", [128, STRIP])
            landed_o = sb("landed_o", [128, STRIP])
            KP, QP, OP, VP = ps("KP", [128, 512]), ps("QP", [128, 512]), ps("OP", [128, 512]), ps("VP", [128, 512])
            S = ps("S", [128, 2, 512])
            T = ps("T", [128, 2, 512])
            (loaded, masks_loaded, zeroed, staged, k_made, q_made, va_made, vb_made, kexp_made, qbd_made, vexp_made, scored,
             biased, maxed, shifted, exped, summed, inverted, normed, turned, turned_out, pv_made, o_out,
             projected, added, kb_made, residual_done) = (
                sem(n) for n in ("loaded", "masks_loaded", "zeroed", "staged", "k_made", "q_made", "va_made", "vb_made", "kexp_made",
                                 "qbd_made", "vexp_made", "scored", "biased", "maxed", "shifted", "exped", "summed",
                                 "inverted", "normed", "turned", "turned_out", "pv_made", "o_out", "projected",
                                 "added", "kb_made", "residual_done"))
            block = ctx.enter_context(nc.Block())
            NB = CHUNKS // 2
            LAG_E, LAG_N, LAG_T, LAG_V = 1, 2, 4, 5
            SCALE = HD ** -0.5

            def chunk_cols(c):
                return pick(c * STRIP, STRIP)

            @block.sync
            def _(sp):
                sp.dma_start(ctile[:, :], dram["swin"][b]).then_inc(loaded, 16)
                sp.dma_start(bias[:, 0, :], dram["rpb"][b]).then_inc(loaded, 16)
                if b:
                    sp.dma_start(kexp[:, 0, 0:3, :], dram["masks"][:, :, :]).then_inc(masks_loaded, 16)

            @block.tensor
            def _(pe):
                pe.wait_ge(loaded, 32)
                pe.wait_ge(zeroed, 4)

                def keys_queries(c):
                    toks = yw[:, :, 0:WIN]
                    pe.wait_ge(staged, 2 * c + 2)
                    if not isinstance(c, int) or c:
                        pe.wait_ge(kexp_made, c)
                    pe.matmul(KP[:, 0:STRIP], part("wk"), toks, start=True, stop=True).then_inc(k_made, 1)
                    pe.wait_ge(qbd_made, c + 1)
                    if not isinstance(c, int) or c > 1:
                        pe.wait_ge(added, c - 1)
                    pe.matmul(QP[:, 0:STRIP], part("wq"), toks, start=True, stop=True).then_inc(q_made, 1)

                def values(c, h):
                    pe.wait_ge(vexp_made, 2 * c + 1 + h)
                    for w in range(NW):
                        mm = pe.matmul(VP[:, w * C:(w + 1) * C], yw[h * C:(h + 1) * C, w, :],
                                       part("wv", p0=h * C, p1=(h + 1) * C), start=True, stop=True)
                    mm.then_inc((va_made, vb_made)[h], 1)

                def score(c, par, w):
                    if w == 0:
                        pe.wait_ge(kexp_made, c + 1)
                        pe.wait_ge(qbd_made, c + 2)
                    pe.wait_ge(biased, c * NW + w + 1)
                    pe.matmul(S[:, w % 2, 0:STRIP], qbd[:, par, w, :],
                              kexp[:, par, :, w * WIN:(w + 1) * WIN], start=True, stop=True).then_inc(scored, 1)

                def turn(c, w):
                    n = c * NW + w
                    pe.wait_ge(normed, n + 1)
                    pe.wait_ge(turned_out, n + 1)
                    for k in range(4):
                        mm = pe.transpose(T[:, w % 2, k * 128:(k + 1) * 128],
                                          probs[:, w % 4, 2 * k:2 * k + 2, :].rearrange("p h k -> p (h k)"), base("ident"))
                    mm.then_inc(turned, 1)

                def weigh(c, par, w):
                    n = c * NW + w
                    if w == 0:
                        pe.wait_ge(vexp_made, 2 * c + 3)
                        pe.wait_ge(o_out, c + 1)
                    pe.wait_ge(turned_out, n + 3)
                    for h in range(2):
                        for k in range(4):
                            mm = pe.matmul(OP[h * C:(h + 1) * C, w * WIN:(w + 1) * WIN], vexp[:, par, h, w, k, :],
                                           probsT[:, w % 2, k * 128 + h * C:k * 128 + h * C + WIN],
                                           start=(k == 0), stop=(k == 3))
                    mm.then_inc(pv_made, 1)

                def project(c):
                    pe.wait_ge(o_out, c + 2)
                    pe.wait_ge(qbd_made, min(c + 4, CHUNKS + 1) if isinstance(c, int) else c + 4)
                    pe.matmul(QP[:, 0:STRIP], part("wp"), osb[:, :], start=True, stop=True).then_inc(projected, 1)

                def slot(c, par, w, first=False, tail=False):
                    if not tail:
                        score(c, par, w)
                    for lag, kind in ((LAG_T, 0), (LAG_V, 1)):
                        v = w - lag
                        cc, pp = (c, par) if v >= 0 else (c - 1, 1 - par)
                        if first and v < 0:
                            continue
                        if tail and v >= 0:
                            continue
                        if kind == 0:
                            turn(cc, v % NW)
                        else:
                            weigh(cc, pp, v % NW)
                    if w == LAG_V and not first:
                        project(c - 1)

                def body(c0, first=False, last=False):
                    for par in range(2):
                        c = c0 + par
                        for w in range(NW):
                            slot(c, par, w, first=first and par == 0)
                            if not (last and par == 1):
                                if w == 2:
                                    keys_queries(c + 1)
                                if w == 4:
                                    values(c + 1, 0)
                                if w == 6:
                                    values(c + 1, 1)

                warm_up(pe, OP, base)
                keys_queries(0)
                values(0, 0)
                values(0, 1)
                warm_up(pe, OP, base)
                body(0, first=True)
                with pe.Fori(1, NB - 1) as m:
                    body(m * 2)
                body((NB - 1) * 2, last=True)
                for w in range(LAG_V + 3):
                    slot(CHUNKS, 0, w, tail=True)

            @block.scalar
            def _(act):
                act.preload_act_table(ACT.Exp)
                act.wait_ge(loaded, 32)
                act.wait_ge(zeroed, 4)
                act.wait_ge(kb_made, 4 if b else 1)

                def stage(c):
                    act.wait_ge(vb_made, c + 1)
                    act.activation(yw[:, :, 0:WIN].rearrange("p b (a k) -> p b a k", a=WS),
                                   strip_by_window(y[:, chunk_cols(c)]), ACT.Copy).then_inc(staged, 1)

                def expand(c, par, part_=None):
                    act.wait_ge(k_made, c + 1)
                    heads = range(HEADS) if part_ is None else range(part_ * 4, part_ * 4 + 4)
                    for h in heads:
                        a = act.activation(kexp[:, par, h, :], KP[:, 0:STRIP], ACT.Identity,
                                           bias=biask[:, h:h + 1], scale=part("headmask", h, 1))
                    if part_ != 0:
                        a.then_inc(kexp_made, 1)

                def expo(c, w):
                    n = c * NW + w
                    act.wait_ge(shifted, n + 1)
                    act.wait_ge(turned, n + 1)
                    act.activation(probs[:, w % 4, :, 0:WIN], scores[:, w % 4, :].rearrange(
                        "p (h k) -> p h k", h=HEADS), ACT.Exp).then_inc(exped, 1)

                def evacuate(c, w):
                    n = c * NW + w
                    act.wait_ge(turned, n + 5)
                    act.wait_ge(pv_made, n + 1)
                    act.activation(probsT[:, w % 2, :], T[:, w % 2, :], ACT.Copy).then_inc(turned_out, 1)

                def out(c):
                    act.wait_ge(pv_made, NW * c + NW + 2)
                    act.wait_ge(projected, c + 1)
                    act.activation(osb[:, :], OP[:, 0:STRIP], ACT.Identity, bias=part("bv")).then_inc(o_out, 1)

                def land(c):
                    act.wait_ge(projected, c + 2)
                    act.wait_ge(residual_done, c + 1)
                    act.activation(strip_by_row(landed_o[:, :]), QP[:, 0:STRIP].rearrange(
                        "p (b a k) -> p a b k", b=NW, a=WS), ACT.Identity, bias=part("bp")).then_inc(added, 1)

                def slot(c, par, w, first=False, tail=False):
                    for lag, what in ((LAG_E, expo), (LAG_T, evacuate)):
                        v = w - lag
                        if (v >= 0 and not tail) or (v < 0 and not first):
                            what(c if v >= 0 else c - 1, v % NW)
                    if w == LAG_V - 1 and not first:
                        out(c - 1)
                    if w == LAG_V + 1 and not first:
                        land(c - 1)

                def body(c0, first=False, last=False):
                    for par in range(2):
                        c = c0 + par
                        for w in range(NW):
                            slot(c, par, w, first=first and par == 0)
                            if not (last and par == 1):
                                if w == 0:
                                    stage(c + 1)
                                if w in (3, 4):
                                    expand(c + 1, 1 - par, w - 3)

                stage(0)
                expand(0, 0)
                body(0, first=True)
                with act.Fori(1, NB - 1) as m:
                    body(m * 2)
                body((NB - 1) * 2, last=True)
                for w in range(LAG_V + 3):
                    slot(CHUNKS, 0, w, tail=True)

            @block.gpsimd
            def _(pool):
                pool.memset(yw[:, :, :], 0.0).then_inc(zeroed, 1)
                pool.memset(qbd[:, :, :, :], 0.0).then_inc(zeroed, 1)
                pool.memset(probs[:, :, :, :], 0.0).then_inc(zeroed, 1)

                def shift(n, w):
                    tile = scores[:, w % 4, :].rearrange("p (h k) -> p h k", h=HEADS)
                    pool.wait_ge(maxed, n + 1)
                    pool.tensor_tensor(tile, tile, stat[:, w % 4, 0, :].unsqueeze(2).broadcast_to([128, HEADS, WIN]),
                                       ALU.subtract).then_inc(shifted, 1)

                def norm(n, w):
                    pool.wait_ge(inverted, n + 1)
                    pool.tensor_tensor(probs[:, w % 4, :, 0:WIN], probs[:, w % 4, :, 0:WIN],
                                       stat[:, w % 4, 2, :].unsqueeze(2).broadcast_to([128, HEADS, WIN]),
                                       ALU.mult).then_inc(normed, 1)

                for w in range(LAG_N):
                    shift(w, w)
                with pool.Fori(0, CHUNKS - 1) as c:
                    for w in range(NW):
                        shift(c * NW + w + LAG_N, w + LAG_N)
                        norm(c * NW + w, w)
                for w in range(NW):
                    if w + LAG_N < NW:
                        shift((CHUNKS - 1) * NW + w + LAG_N, w + LAG_N)
                    norm((CHUNKS - 1) * NW + w, w)

            @block.vector
            def _(dve):
                dve.memset(vexp[:, :, :, :, :, :], 0.0).then_inc(zeroed, 1)
                dve.wait_ge(loaded, 32)
                if b:
                    dve.wait_ge(masks_loaded, 16)
                dve.wait_ge(zeroed, 4)
                dve.tensor_scalar(biask[:, :], part("headmask"), part("bk"), None, ALU.mult).then_inc(kb_made, 1)
                if b:
                    for k in range(1, 4):
                        dve.tensor_tensor(bias[:, k, :], bias[:, 0, :], kexp[:, 0, k - 1, :], ALU.add).then_inc(kb_made, 1)
                    dve.wait_ge(kb_made, 4)
                for s, n in ((added, 1), (qbd_made, 1), (vexp_made, 1), (biased, 2), (turned_out, 2), (o_out, 1),
                             (vb_made, 1), (turned, 4), (pv_made, 2), (projected, 1),
                             (residual_done, 1)):
                    dve.sem_inc(s, n)

                def stage(c):
                    dve.wait_ge(vb_made, c + 1)
                    dve.tensor_copy(yw[:, :, C:C + WIN].rearrange("p b (a k) -> p b a k", a=WS),
                                    strip_by_window(y[:, chunk_cols(c)])).then_inc(staged, 1)

                def queries(c, par):
                    dve.wait_ge(q_made, c + 1)
                    for h in range(2):
                        rows = slice(h * C, (h + 1) * C)
                        o = dve.tensor_scalar(qbd[rows, par, :, h * C:h * C + WIN],
                                              QP[rows, 0:STRIP].rearrange("p (b k) -> p b k", b=NW),
                                              part("bq", p0=h * C, p1=h * C + C), SCALE, ALU.add, ALU.mult)
                    o.then_inc(qbd_made, 1)

                def values(c, par, h):
                    dve.wait_ge((va_made, vb_made)[h], c + 1 + h)
                    v = VP[:, :].rearrange("p (b k e d) -> p b k e d", b=NW, k=4, e=2)
                    for e in range(2):
                        rows = slice(e * C, (e + 1) * C)
                        dst = vexp[rows, par, h].rearrange("p b k (g d) -> p b (k g) d", d=HD)
                        o = dve.tensor_copy(dst[:, :, e:e + 31:10, :], v[rows, :, :, e, :])
                    o.then_inc(vexp_made, 1)

                def bias_of(w, last_strip):
                    return bias[:, (int(w == NW - 1) + 2 * int(last_strip)) if b else 0, :]

                def by_head(w):
                    return scores[:, w % 4, :].rearrange("p (h k) -> p h k", h=HEADS)

                def add_bias(n, w, last_strip):
                    dve.wait_ge(scored, n + 1)
                    dve.tensor_tensor(scores[:, w % 4, :], S[:, w % 2, 0:STRIP], bias_of(w, last_strip), ALU.add)\
                       .then_inc(biased, 1)

                def maximum(n, w):
                    dve.wait_ge(biased, n + 3)
                    dve.tensor_reduce(stat[:, w % 4, 0, :], by_head(w), AX, ALU.max).then_inc(maxed, 1)

                def total(n, w):
                    dve.wait_ge(exped, n + 1)
                    dve.tensor_reduce(stat[:, w % 4, 1, :], probs[:, w % 4, :, 0:WIN], AX, ALU.add).then_inc(summed, 1)

                def inverse(n, w):
                    dve.wait_ge(summed, n + 1)
                    dve.reciprocal(stat[:, w % 4, 2, :], stat[:, w % 4, 1, :]).then_inc(inverted, 1)

                def residual(c):
                    dve.wait_ge(added, c + 2)
                    strip = res[:, chunk_cols(c)]
                    dve.tensor_tensor(strip, landed_o[:, :], strip, ALU.add).then_inc(residual_done, 1)

                def slot(c, w, last_strip, first=False, tail=False):
                    n, before = c * NW + w, w - LAG_N
                    sums = (before >= 0 and not tail) or (before < 0 and not first)
                    if not tail:
                        add_bias(n, w, last_strip)
                    if sums:
                        total(n - LAG_N, before % NW)
                    if not tail:
                        maximum(n, w)
                    if sums:
                        inverse(n - LAG_N, before % NW)
                    if w == LAG_V + 2 and not first:
                        residual(c - 1)

                def body(c0, ends_image, first=False, last=False):
                    for par in range(2):
                        c = c0 + par
                        for w in range(NW):
                            slot(c, w, ends_image and par == 1, first=first and par == 0)
                            if not (last and par == 1):
                                if w == 0:
                                    stage(c + 1)
                                if w == 3:
                                    queries(c + 1, 1 - par)
                                if w in (5, 7):
                                    values(c + 1, 1 - par, (w - 5) // 2)

                stage(0)
                queries(0, 0)
                values(0, 0, 0)
                values(0, 0, 1)
                body(0, False, first=True)
                with dve.Fori(0, HALF_IMGS - 1) as img:
                    body(img * STRIPS + 2, False)
                    body(img * STRIPS + 4, False)
                    body(img * STRIPS + 6, True)
                    body(img * STRIPS + 8, False)
                body((HALF_IMGS - 1) * STRIPS + 2, False)
                body((HALF_IMGS - 1) * STRIPS + 4, False)
                body((NB - 1) * 2, True, last=True)
                for w in range(LAG_V + 3):
                    slot(CHUNKS, w, False, tail=True)

    def mlp(b, res, y, base):
        name = f"mlp{b}"
        with phase() as ctx:
            sem = lambda n: nc.alloc_semaphore(f"{name}_{n}")
            ctile, part = load(ctx, name, MLP)
            g = ctx.enter_context(nc.sbuf_tensor(f"{name}_g", [128, 4, STRIP], F32))
            H = ctx.enter_context(nc.psum_tensor(f"{name}_H", [128, 4, 512], F32))
            O = ctx.enter_context(nc.psum_tensor(f"{name}_O", [128, 2, 512], F32))
            loaded, hidden, gelued, used, added = (
                sem(n) for n in ("loaded", "hidden", "gelued", "used", "added"))
            block = ctx.enter_context(nc.Block())

            @block.sync
            def _(sp):
                sp.dma_start(ctile[:, :], dram["mlp"][b]).then_inc(loaded, 16)

            @block.tensor
            def _(pe):
                pe.wait_ge(loaded, 16)
                with pe.Fori(0, CHUNKS // 2) as it:
                    for u in range(2):
                        c = it * 2 + u
                        for q in range(4):
                            pe.wait_ge(gelued, c * 4 + q + 1)
                            pe.matmul(H[:, q, 0:STRIP], part("w1", q * 128, 128), y[:, pick(c * STRIP, STRIP)],
                                      start=True, stop=True).then_inc(hidden, 1)
                        pe.wait_ge(added, c + 1)
                        for q in range(4):
                            pe.wait_ge(gelued, c * 4 + q + 5)
                            pe.matmul(O[:, u, 0:STRIP], part("w2", q * 128, 128), g[:, q, :],
                                      start=(q == 0), stop=(q == 3)).then_inc(used, 1)

            @block.scalar
            def _(act):
                act.preload_act_table(ACT.Gelu)
                act.wait_ge(loaded, 16)
                with act.Fori(0, CHUNKS) as c:
                    for q in range(4):
                        act.wait_ge(hidden, c * 4 + q + 1)
                        act.wait_ge(used, c * 4 + q + 1)
                        act.activation(g[:, q, :], H[:, q, 0:STRIP], ACT.Gelu, bias=part("b1", q, 1)).then_inc(gelued, 1)

            @block.vector
            def _(dve):
                dve.wait_ge(loaded, 16)
                dve.sem_inc(gelued, 4)
                dve.sem_inc(used, 4)
                dve.sem_inc(added, 2)
                with dve.Fori(0, CHUNKS // 2) as it:
                    for u in range(2):
                        c = it * 2 + u
                        dve.wait_ge(used, c * 4 + 8)
                        strip = res[:, pick(c * STRIP, STRIP)]
                        dve.scalar_tensor_tensor(out=strip, in0=O[:, u, 0:STRIP], scalar=part("b2"), in1=strip,
                                                 op0=ALU.add, op1=ALU.add).then_inc(added, 1)

    def image_attention(res, y, base):
        name = "att"
        with phase() as ctx:
            sb = lambda n, s, d=F32: ctx.enter_context(nc.sbuf_tensor(f"{name}_{n}", s, d))
            ps = lambda n, s: ctx.enter_context(nc.psum_tensor(f"{name}_{n}", s, F32))
            sem = lambda n: nc.alloc_semaphore(f"{name}_{n}")
            ctile, part = load(ctx, name, ATT)
            GW = KPG * QT
            HB = GW // 2
            UNITS = 2 * KG
            ks = sb("ks", [128, 2, 3, TOK], BF16)
            qs = sb("qs", [128, 2, TOK])
            vs = sb("vs", [QT, QTILES, 128])
            qz = sb("qz", [128, 2, 2, 2, QT], BF16)
            qt = sb("qt", [128, 2, QT])
            left = sb("left", [128, 2, QT])
            probs_rows = sb("probs", [128, 2, GW])
            probs = probs_rows[0:QT]
            krest = probs_rows[:, :, 0:STRIP]
            probsT_rows = sb("probsT", [128, 2, GW])
            probsT = probsT_rows[0:QT]
            ys = probsT_rows[:, :, 0:4 * QT]
            negmax = sb("negmax", [QT, 2, UNITS])
            sums = sb("sums", [QT, 2, UNITS])
            least = sb("least", [QT, 2, 2])
            gap = sb("gap", [QT, 2, UNITS])
            weight = sb("weight", [QT, 2, UNITS])
            wsum = sb("wsum", [QT, 2, UNITS])
            total = sb("total", [QT, 2, 2])
            inverse = sb("inverse", [QT, 2, 2])
            share = sb("share", [QT, 2, UNITS])
            scaled = sb("scaled", [QT, UNITS, C])
            joined = sb("joined", [QT, 2, 128])
            S = ps("S", [128, 4, 512])
            T = ps("T", [128, 2, 512])
            O = ps("O", [128, 2, 512])
            (loaded, staged, prepared, evac_a, evac_d, scored, maxed, exped, turned, out_a, out_d, weighed, combined,
             weights_made, o_turned, residual, q_staged, k_first, k_rest, k_second, k_split, q_kept, q_step) = (
                sem(n) for n in ("loaded", "staged", "prepared", "evac_a", "evac_d", "scored", "maxed", "exped", "turned",
                                 "out_a", "out_d", "weighed", "combined", "weights_made", "o_turned", "residual",
                                 "q_staged", "k_first", "k_rest", "k_second", "k_split", "q_kept", "q_step"))
            block = ctx.enter_context(nc.Block())
            NK = 2 * (TOK // STRIP)
            NV = QTILES // 4
            NV_A, NV_D = (NV + 1) // 2, NV // 2
            PREP = 2 * NK + NV
            KSTEPS = 4
            CHAIN = 8

            @block.sync
            def _(sp):
                sp.dma_start(ctile[:, :], dram["att"]).then_inc(loaded, 16)

            @block.tensor
            def _(pe):
                pe.wait_ge(loaded, 16)

                def prepare(j):
                    for n in range(NK):
                        i, h = divmod(n, 2)
                        for bank, w, kept in ((0, "wk", k_rest), (1, "wq", q_kept)):
                            if n >= 2:
                                pe.wait_ge(kept, j * NK + n - 1)
                            pe.matmul(S[:, n % 2 * 2 + bank, 0:STRIP], part(w, h * 128, 128),
                                      y[:, pick(j * TOK + i * STRIP, STRIP)], start=True, stop=True)\
                              .then_inc(prepared, 1)
                    for v in range(NV):
                        if v < 4:
                            pe.wait_ge((k_rest, q_kept)[v % 2], j * NK + NK - 1 + v // 2)
                        else:
                            pe.wait_ge((evac_a, evac_d)[v % 2], j * (NV_A, NV_D)[v % 2] + v // 2 - 1)
                        pe.wait_ge(staged, j * NV + v + 1)
                        for k in range(4):
                            mm = pe.matmul(S[0:QT, v % 4, k * 128:(k + 1) * 128], ys[:, v % 2, k * QT:(k + 1) * QT],
                                           part("wv"), start=True, stop=True)
                        mm.then_inc(prepared, 1)
                    pe.wait_ge(evac_a, (j + 1) * NV_A)
                    pe.wait_ge(evac_d, (j + 1) * NV_D)
                    pe.wait_ge(k_split, (j + 1) * (NK * KSTEPS))

                def score(tile, p, u):
                    h, g = divmod(u, KG)
                    n = tile * UNITS + u
                    if u == 0:
                        pe.wait_ge(q_staged, tile + 2)
                    pe.wait_ge(exped, n + 1)
                    for which, part_ in ((0, 0), (0, 1), (1, 2)):
                        for b in range(2):
                            mm = pe.matmul(S[0:QT, (u % 2) * 2 + b, 0:HB], qz[:, p, h, which, :],
                                           ks[:, h, part_, g * GW + b * HB:g * GW + (b + 1) * HB],
                                           start=(part_ == 0), stop=(part_ == 2))
                    mm.then_inc(scored, 1)

                def turn(tile, p, u):
                    n = tile * UNITS + u
                    pe.wait_ge(exped, n + 3)
                    pe.wait_ge(out_d, n + 1)
                    pe.wait_ge(out_a, n + 1)
                    for k in range(KPG):
                        mm = pe.transpose(T[0:QT, k // 4, (k % 4) * QT:(k % 4 + 1) * QT],
                                          probs[:, u % 2, k * QT:(k + 1) * QT], base("ident", 0, QT, 0, QT))
                    mm.then_inc(turned, 1)

                def weigh(tile, p, u):
                    h, g = divmod(u, KG)
                    n = tile * UNITS + u
                    pe.wait_ge(out_d, n + 2)
                    pe.wait_ge(out_a, n + 2)
                    if u == 0:
                        pe.wait_ge(residual, tile + 1)
                    for k in range(KPG):
                        mm = pe.matmul(O[0:QT, p, u * C:(u + 1) * C], probsT[:, u % 2, k * QT:(k + 1) * QT],
                                       vs[:, g * KPG + k, h * C:(h + 1) * C], start=(k == 0), stop=(k == KPG - 1))
                    mm.then_inc(weighed, 1)

                def turn_output(tile, p):
                    pe.wait_ge(combined, (tile + 1) * CHAIN)
                    pe.transpose(O[:, p, 0:QT], joined[:, p, :], base("ident", 0, QT, 0, QT)).then_inc(o_turned, 1)

                def slots(tile, p, first, tail):
                    for u in range(UNITS):
                        if not tail:
                            score(tile, p, u)
                        if u == 7 and not first:
                            turn_output(tile - 1, 1 - p)
                        for lag, what in ((1, turn), (2, weigh)):
                            if u >= lag and not tail:
                                what(tile, p, u - lag)
                            elif u < lag and not first:
                                what(tile - 1, 1 - p, u - lag + UNITS)

                with pe.Fori(0, HALF_IMGS) as j:
                    prepare(j)
                    slots(j * QTILES, 0, True, False)
                    slots(j * QTILES + 1, 1, False, False)
                    with pe.Fori(1, QTILES // 2) as i:
                        slots(j * QTILES + i * 2, 0, False, False)
                        slots(j * QTILES + i * 2 + 1, 1, False, False)
                    slots(j * QTILES + QTILES, 0, False, True)

            @block.scalar
            def _(act):
                act.preload_act_table(ACT.Exp)

                def prepare(j):
                    def second(n):
                        i, h = divmod(n, 2)
                        act.wait_ge(k_rest, j * NK + n + 1)
                        act.activation(ks[:, h, 1, i * STRIP:(i + 1) * STRIP], krest[:, n % 2, :], ACT.Copy)\
                           .then_inc(k_second, 1)

                    for n in range(NK):
                        i, h = divmod(n, 2)
                        act.wait_ge(prepared, j * PREP + 2 * n + 1)
                        act.activation(ks[:, h, 2, i * STRIP:(i + 1) * STRIP], S[:, n % 2 * 2, 0:STRIP], ACT.Copy)\
                           .then_inc(k_first, 1)
                        act.wait_ge(prepared, j * PREP + 2 * n + 2)
                        act.activation(qs[:, h, i * STRIP:(i + 1) * STRIP], S[:, n % 2 * 2 + 1, 0:STRIP], ACT.Copy,
                                       scale=C ** -0.5).then_inc(q_kept, 1)
                        second(n)
                    for v in range(0, NV, 2):
                        act.wait_ge(prepared, j * PREP + 2 * NK + v + 1)
                        act.activation(vs[:, v * 4:v * 4 + 4, :], S[0:QT, v % 4, :].rearrange("p (t c) -> p t c", t=4),
                                       ACT.Copy).then_inc(evac_a, 1)

                def expo(tile, p, u):
                    n = tile * UNITS + u
                    act.wait_ge(maxed, n + 1)
                    act.wait_ge(turned, n + 1)
                    act.activation(probs[:, u % 2, :].rearrange("p (b k) -> p b k", b=2),
                                   S[0:QT, (u % 2) * 2:(u % 2) * 2 + 2, 0:HB], ACT.Exp,
                                   bias=negmax[:, p, u:u + 1], accum_out=sums[:, p, u:u + 1]).then_inc(exped, 1)

                def evacuate(tile, p, u):
                    n = tile * UNITS + u
                    act.wait_ge(turned, n + 3)
                    act.wait_ge(weighed, n + 1)
                    act.activation(probsT[:, u % 2, 4 * QT:GW], T[0:QT, 1, 0:3 * QT], ACT.Copy).then_inc(out_a, 1)

                def weights(tile, p):
                    act.wait_ge(combined, tile * CHAIN + 2)
                    act.activation(weight[:, p, :], gap[:, p, :], ACT.Exp).then_inc(weights_made, 1)

                def slots(tile, p, first, tail):
                    for u in range(UNITS):
                        if not tail:
                            expo(tile, p, u)
                        if u >= 1 and not tail:
                            evacuate(tile, p, u - 1)
                        elif u < 1 and not first:
                            evacuate(tile - 1, 1 - p, UNITS - 1)
                        if u == 3 and not first:
                            weights(tile - 1, 1 - p)

                with act.Fori(0, HALF_IMGS) as j:
                    prepare(j)
                    slots(j * QTILES, 0, True, False)
                    slots(j * QTILES + 1, 1, False, False)
                    with act.Fori(1, QTILES // 2) as i:
                        slots(j * QTILES + i * 2, 0, False, False)
                        slots(j * QTILES + i * 2 + 1, 1, False, False)
                    slots(j * QTILES + QTILES, 0, False, True)

            @block.gpsimd
            def _(pool):
                QSTEPS = 5
                low, high = slice(0, C), slice(C, 128)
                with pool.Fori(0, HALF_IMGS) as j:
                    with pool.Fori(0, QTILES // 2) as i:
                        for p in range(2):
                            pool.wait_ge(q_kept, (j + 1) * NK)
                            tile = j * QTILES + i * 2 + p
                            pool.wait_ge(scored, tile * UNITS + UNITS)
                            pool.wait_ge(q_staged, tile + 1)
                            cols = pick(i * (2 * QT) + p * QT, QT)
                            pool.tensor_copy(qt[:, :, :], qs[:, :, cols]).then_inc(q_step, 1)
                            pool.tensor_copy(qz[:, p, :, 1, :], qs[:, :, cols]).then_inc(q_step, 1)
                            pool.wait_ge(q_step, tile * QSTEPS + 2)
                            pool.tensor_tensor(left[:, :, :], qt[:, :, :], qz[:, p, :, 1, :], ALU.subtract)\
                                .then_inc(q_step, 1)
                            pool.tensor_tensor(qz[:, p, :, 0, :], qt[:, :, :], qz[:, p, :, 1, :],
                                               ALU.subtract).then_inc(q_step, 1)
                            pool.wait_ge(q_step, tile * QSTEPS + 4)
                            pool.tensor_tensor(qz[high, p, :, 1, :], left[high, :, :], qz[high, p, :, 0, :],
                                               ALU.subtract).then_inc(q_step, 1)
                            pool.wait_ge(q_step, tile * QSTEPS + 5)
                            pool.tensor_tensor(qz[low, p, :, 0, :], qt[low, :, :], left[low, :, :],
                                               ALU.subtract).then_inc(q_staged, 1)

            @block.vector
            def _(dve):
                for s, n in ((exped, 2), (turned, 2), (out_a, 1), (out_d, 1), (weighed, 2), (residual, 2),
                             (scored, 2 * UNITS), (q_staged, 1)):
                    dve.sem_inc(s, n)

                def prepare(j):
                    def stage(v):
                        dve.wait_ge(prepared, j * PREP + (1 if v < 2 else 2 * NK + v - 1))
                        dve.tensor_copy(ys[:, v % 2, :], y[:, pick(j * TOK + v * 4 * QT, 4 * QT)]).then_inc(staged, 1)

                    def rest(n):
                        i, h = divmod(n, 2)
                        dve.wait_ge(k_first, j * NK + n + 1)
                        if n >= 2:
                            dve.wait_ge(k_split, (j * NK + n - 1) * KSTEPS)
                        dve.tensor_tensor(krest[:, n % 2, :], S[:, n % 2 * 2, 0:STRIP],
                                          ks[:, h, 2, i * STRIP:(i + 1) * STRIP], ALU.subtract).then_inc(k_rest, 1)

                    def order(n):
                        i, h = divmod(n, 2)
                        a, b, c = (ks[:, h, k, i * STRIP:(i + 1) * STRIP] for k in range(3))
                        at = (j * NK + n) * KSTEPS
                        dve.tensor_copy(a[0:C], c[0:C]).then_inc(k_split, 1)
                        dve.wait_ge(k_second, j * NK + n + 1)
                        dve.tensor_copy(a[C:128], b[C:128]).then_inc(k_split, 1)
                        dve.wait_ge(k_split, at + 2)
                        dve.tensor_tensor(c[0:C], krest[0:C, n % 2, :], b[0:C], ALU.subtract).then_inc(k_split, 1)
                        dve.tensor_copy(b[C:128], c[C:128]).then_inc(k_split, 1)

                    for n in range(NK):
                        rest(n)
                        if n:
                            order(n - 1)
                        if 2 <= n < 4:
                            stage(n - 2)
                    order(NK - 1)
                    for v in range(2, NV):
                        stage(v)
                    for v in range(1, NV, 2):
                        dve.wait_ge(prepared, j * PREP + 2 * NK + v + 1)
                        dve.tensor_copy(vs[:, v * 4:v * 4 + 4, :], S[0:QT, v % 4, :].rearrange("p (t c) -> p t c", t=4))\
                           .then_inc(evac_d, 1)

                def maximum(tile, p, u):
                    n = tile * UNITS + u
                    dve.wait_ge(scored, n + 1 + 2 * UNITS)
                    dve.tensor_reduce(negmax[:, p, u:u + 1], S[0:QT, (u % 2) * 2:(u % 2) * 2 + 2, 0:HB],
                                      mybir.AxisListType.XY, ALU.max, negate=True).then_inc(maxed, 1)

                def evacuate(tile, p, u):
                    n = tile * UNITS + u
                    dve.wait_ge(turned, n + 3)
                    dve.wait_ge(weighed, n + 1)
                    dve.tensor_copy(probsT[:, u % 2, 0:4 * QT], T[0:QT, 0, 0:4 * QT]).then_inc(out_d, 1)

                def by_group(ap):
                    return ap.rearrange("p (h g) -> p h g", h=2)

                def gaps(tile, p):
                    dve.wait_ge(maxed, (tile + 1) * UNITS)
                    dve.tensor_reduce(least[:, p, :], by_group(negmax[:, p, :]), AX, ALU.min).then_inc(combined, 1)
                    dve.wait_ge(combined, tile * CHAIN + 1)
                    dve.tensor_tensor(by_group(gap[:, p, :]), least[:, p, :].unsqueeze(2).broadcast_to([QT, 2, KG]),
                                      by_group(negmax[:, p, :]), ALU.subtract).then_inc(combined, 1)

                def shares(tile, p):
                    dve.wait_ge(weights_made, tile + 1)
                    dve.tensor_tensor(wsum[:, p, :], weight[:, p, :], sums[:, p, :], ALU.mult).then_inc(combined, 1)
                    dve.wait_ge(combined, tile * CHAIN + 3)
                    dve.tensor_reduce(total[:, p, :], by_group(wsum[:, p, :]), AX, ALU.add).then_inc(combined, 1)
                    dve.wait_ge(combined, tile * CHAIN + 4)
                    dve.reciprocal(inverse[:, p, :], total[:, p, :]).then_inc(combined, 1)
                    dve.wait_ge(combined, tile * CHAIN + 5)
                    dve.tensor_tensor(by_group(share[:, p, :]), by_group(weight[:, p, :]),
                                      inverse[:, p, :].unsqueeze(2).broadcast_to([QT, 2, KG]), ALU.mult).then_inc(combined, 1)

                def share_out(tile, p):
                    dve.wait_ge(combined, tile * CHAIN + 6)
                    dve.wait_ge(weighed, (tile + 1) * UNITS + 2)
                    dve.tensor_tensor(scaled[:, :, :], O[0:QT, p, :].rearrange("p (u c) -> p u c", u=UNITS),
                                      share[:, p, :].unsqueeze(2).broadcast_to([QT, UNITS, C]), ALU.mult).then_inc(combined, 1)

                def join(tile, p):
                    dve.wait_ge(combined, tile * CHAIN + 7)
                    dve.tensor_reduce(joined[:, p, :].rearrange("p (h c) -> p h c", h=2),
                                      scaled[:, :, :].rearrange("p (h g) c -> p h c g", h=2), AX, ALU.add)\
                       .then_inc(combined, 1)

                def add(tile, i, j, p):
                    dve.wait_ge(o_turned, tile + 1)
                    cols = res[:, pick(j * TOK + i * QT, QT)]
                    dve.tensor_tensor(cols, O[:, p, 0:QT], cols, ALU.add).then_inc(residual, 1)

                def slots(j, i, p, first, tail):
                    tile = j * QTILES + i
                    for u in range(UNITS):
                        if not tail:
                            maximum(tile, p, u)
                        if u >= 1 and not tail:
                            evacuate(tile, p, u - 1)
                        elif u < 1 and not first:
                            evacuate(tile - 1, 1 - p, UNITS - 1)
                        if not first:
                            if u == 2:
                                gaps(tile - 1, 1 - p)
                            if u == 4:
                                shares(tile - 1, 1 - p)
                            if u == 5:
                                share_out(tile - 1, 1 - p)
                            if u == 6:
                                join(tile - 1, 1 - p)
                            if u == 7:
                                add(tile - 1, i - 1, j, 1 - p)

                with dve.Fori(0, HALF_IMGS) as j:
                    prepare(j)
                    slots(j, 0, 0, True, False)
                    slots(j, 1, 1, False, False)
                    with dve.Fori(1, QTILES // 2) as i:
                        slots(j, i * 2, 0, False, False)
                        slots(j, i * 2 + 1, 1, False, False)
                    slots(j, QTILES, 0, False, True)

    def routing(y, gates, base):
        name = "gate"
        TILES = COLS // LNT
        E2 = 2 * EXPERTS
        with phase() as ctx:
            sb = lambda n, s, d=F32: ctx.enter_context(nc.sbuf_tensor(f"{name}_{n}", s, d))
            sem = lambda n: nc.alloc_semaphore(f"{name}_{n}")
            ctile, part = load(ctx, name, GATE)
            logits = sb("logits", [LNT, TILES, E2])
            work = sb("work", [LNT, TILES, E2])
            chosen = sb("chosen", [LNT, TILES, E2])
            before = sb("before", [LNT, E2, TILES])
            parts = sb("parts", [LNT, 3, TILES, E2], BF16)
            small = sb("small", [LNT, 3, 2 * TILES])
            lt = sb("lt", [128, 2, STRIP])
            loaded = sem("loaded")
            with ExitStack() as inner:
                L = inner.enter_context(nc.psum_tensor("gate_L", [128, 2, 512], F32))
                Z = inner.enter_context(nc.psum_tensor("gate_Z", [LNT, 2, 512], F32))
                made, copied, turned, placed = (sem(n) for n in ("made", "copied", "turned", "placed"))
                block = inner.enter_context(nc.Block())

                @block.sync
                def _(sp):
                    sp.dma_start(ctile[:, :], dram["gate"]).then_inc(loaded, 16)

                @block.tensor
                def _(pe):
                    pe.wait_ge(loaded, 16)
                    with pe.Fori(0, CHUNKS // 2) as it:
                        for u in range(2):
                            c = it * 2 + u
                            pe.wait_ge(copied, c + 1)
                            pe.matmul(L[:, u, 0:STRIP], part("gw"), y[:, pick(c * STRIP, STRIP)], start=True,
                                      stop=True).then_inc(made, 1)
                        for u in range(2):
                            c = it * 2 + u
                            pe.wait_ge(copied, c + 3)
                            pe.wait_ge(placed, c + 1)
                            for k in range(KT):
                                mm = pe.transpose(Z[:, u, k * 128:(k + 1) * 128], lt[:, u, k * LNT:(k + 1) * LNT],
                                                  base("ident"))
                            mm.then_inc(turned, 1)

                @block.scalar
                def _(act):
                    with act.Fori(0, CHUNKS // 2) as it:
                        for u in range(2):
                            c = it * 2 + u
                            act.wait_ge(made, c + 1)
                            act.wait_ge(turned, c + 1)
                            act.activation(lt[:, u, :], L[:, u, 0:STRIP], ACT.Copy).then_inc(copied, 1)

                @block.vector
                def _(dve):
                    dve.sem_inc(copied, 2)
                    dve.sem_inc(turned, 2)
                    dve.sem_inc(placed, 2)
                    dve.wait_ge(loaded, 16)
                    with dve.Fori(0, CHUNKS // 2) as it:
                        for u in range(2):
                            c = it * 2 + u
                            dve.wait_ge(turned, c + 3)
                            dve.tensor_tensor(logits[:, pick(c * KT, KT), :],
                                              Z[:, u, :].rearrange("p (t e) -> p t e", t=KT)[:, :, 0:E2],
                                              part("gb", 0, E2, 0, LNT).unsqueeze(1).broadcast_to([LNT, KT, E2]),
                                              ALU.add).then_inc(placed, 1)
            with ExitStack() as inner:
                B = 512
                NBANK = TILES * E2 // B
                INC = inner.enter_context(nc.psum_tensor("gate_inc", [LNT, NBANK, B], F32))
                TOT = inner.enter_context(nc.psum_tensor("gate_tot", [LNT, NBANK, B], F32))
                step, expd, counted = (sem(n) for n in ("step", "expd", "counted"))
                block = inner.enter_context(nc.Block())
                flat = lambda t: t[:, :, :].rearrange("p t e -> p (t e)")
                per_token = lambda t: t[:, :, :].rearrange("p t (h e) -> p (t h) e", h=2)

                @block.tensor
                def _(pe):
                    pe.wait_ge(counted, 1)
                    for k in range(NBANK):
                        pe.matmul(INC[:, k, :], part("tri", p1=LNT), flat(chosen)[:, k * B:(k + 1) * B], start=True, stop=True)
                        mm = pe.matmul(TOT[:, k, :], part("ones", p1=LNT), flat(chosen)[:, k * B:(k + 1) * B],
                                       start=True, stop=True)
                    mm.then_inc(counted, 1)

                @block.scalar
                def _(act):
                    act.preload_act_table(ACT.Exp)
                    act.wait_ge(step, 2)
                    act.activation(flat(work), flat(work), ACT.Exp).then_inc(expd, 1)

                @block.vector
                def _(dve):
                    count = [0]

                    def chained(ins):
                        count[0] += 1
                        ins.then_inc(step, 1)
                        dve.wait_ge(step, count[0])

                    biggest, total, prob = (small[:, k, :] for k in range(3))
                    wide = lambda v: v.unsqueeze(2).broadcast_to([LNT, 2 * TILES, EXPERTS])
                    chained(dve.tensor_reduce(biggest, per_token(logits), AX, ALU.max))
                    chained(dve.tensor_tensor(per_token(work), per_token(logits), wide(biggest), ALU.subtract))
                    chained(dve.tensor_tensor(per_token(chosen), per_token(logits), wide(biggest), ALU.is_equal))
                    taken = total
                    chained(dve.tensor_copy(taken, per_token(chosen)[:, :, 0]))
                    for e in range(1, EXPERTS):
                        col = per_token(chosen)[:, :, e]
                        chained(dve.tensor_tensor(col, col, taken, ALU.is_gt))
                        chained(dve.tensor_tensor(taken, taken, col, ALU.max))
                    dve.sem_inc(counted, 1)
                    dve.wait_ge(expd, 1)
                    chained(dve.tensor_reduce(total, per_token(work), AX, ALU.add))
                    chained(dve.reciprocal(prob, total))
                    dve.wait_ge(counted, 2)
                    chained(dve.tensor_copy(before[:, :, :].rearrange("p e t -> p t e"),
                                            TOT[:, :, :].rearrange("p b (t e) -> p (b t) e", e=E2)))
                    sums = logits[:, :, :].rearrange("p t e -> p (t e)").rearrange("p (e t) -> p e t", e=E2)
                    one = part("ones", 0, 1, 0, LNT)
                    for e in range(E2):
                        chained(dve.tensor_tensor_scan(sums[:, e, :], one.broadcast_to([LNT, TILES]), before[:, e, :],
                                                       0.0 if e < EXPERTS else sums[:, e - EXPERTS, TILES - 1:TILES],
                                                       ALU.mult, ALU.add))
                    chained(dve.tensor_tensor(before[:, :, :], sums, before[:, :, :], ALU.subtract))
                    for k in range(NBANK):
                        t = B // E2
                        chained(dve.tensor_tensor(work[:, k * t:(k + 1) * t, :],
                                                  INC[:, k, :].rearrange("p (t e) -> p t e", e=E2),
                                                  before[:, :, k * t:(k + 1) * t].rearrange("p e t -> p t e"), ALU.add))
                    chained(dve.scalar_tensor_tensor(out=flat(work), in0=flat(work), scalar=float(CAP), in1=flat(chosen),
                                                     op0=ALU.is_le, op1=ALU.mult))
                    chained(dve.tensor_tensor(per_token(chosen), per_token(work), wide(prob), ALU.mult))
                    left = chosen
                    for k in range(3):
                        chained(dve.tensor_copy(parts[:, k], left[:, :, :]))
                        if k < 2:
                            chained(dve.tensor_tensor(work[:, :, :], left[:, :, :], parts[:, k], ALU.subtract))
                        left = work
            with ExitStack() as inner:
                G = inner.enter_context(nc.psum_tensor("gate_G", [128, 2, 512], F32))
                turned, staged, out_, blank = (sem(n) for n in ("turned2", "staged2", "out2", "blank"))
                st = inner.enter_context(nc.sbuf_tensor("gate_st", [LNT, 2, KT, 128], F32))
                block = inner.enter_context(nc.Block())

                @block.tensor
                def _(pe):
                    with pe.Fori(0, CHUNKS // 2) as it:
                        for u in range(2):
                            c = it * 2 + u
                            pe.wait_ge(staged, c + 1)
                            pe.wait_ge(out_, c + 1)
                            for k in range(KT):
                                mm = pe.transpose(G[:, u, k * LNT:(k + 1) * LNT], st[:, u, k, :],
                                                  base("ident", 0, LNT, 0, LNT))
                            mm.then_inc(turned, 1)

                @block.scalar
                def _(act):
                    with act.Fori(0, CHUNKS // 2) as it:
                        for u in range(2):
                            c = it * 2 + u
                            act.wait_ge(turned, c + 3)
                            act.activation(gates[:, pick(c * STRIP, STRIP)], G[:, u, 0:STRIP], ACT.Copy).then_inc(out_, 1)

                @block.vector
                def _(dve):
                    dve.sem_inc(out_, 2)
                    dve.sem_inc(turned, 2)
                    dve.memset(st[:, :, :, :], 0.0).then_inc(blank, 1)
                    dve.wait_ge(blank, 1)
                    with dve.Fori(0, CHUNKS // 2) as it:
                        for u in range(2):
                            c = it * 2 + u
                            dve.wait_ge(turned, c + 1)
                            dve.tensor_copy(st[:, u, :, 0:3 * E2].rearrange("p k (s e) -> p k s e", s=3),
                                            parts[:, :, pick(c * KT, KT), :].rearrange("p s k e -> p k s e"))\
                               .then_inc(staged, 1)

    def experts(res, y, gates):
        name = "moe"
        with phase() as ctx:
            sb = lambda n, s, d=F32: ctx.enter_context(nc.sbuf_tensor(f"{name}_{n}", s, d))
            sem = lambda n: nc.alloc_semaphore(f"{name}_{n}")
            ctile, part = load(ctx, name, MOE)
            g = sb("g", [128, 4, STRIP])
            gate = sb("gate", [128, 2, STRIP])
            term = sb("term", [128, STRIP])
            total = sb("total", [128, 2, STRIP])
            flag = sb("flag", [128, 3, STRIP], I32)
            fill = sb("fill", [128, 3, STRIP])
            spare = sb("spare", [128, 1])
            sel = sb("sel", [128, EXPERTS * 128], BF16)
            H = ctx.enter_context(nc.psum_tensor("moe_H", [128, 4, 512], F32))
            G = ctx.enter_context(nc.psum_tensor("moe_G", [128, 2, 512], F32))
            O = ctx.enter_context(nc.psum_tensor("moe_O", [128, 2, 512], F32))
            loaded, hidden, relu_a, relu_d, used, gated, gate_out, read, summed, finished, filled, sel_made = (
                sem(n) for n in ("loaded", "hidden", "relu_a", "relu_d", "used", "gated", "gate_out", "read", "summed",
                                 "finished", "filled", "sel_made"))
            block = ctx.enter_context(nc.Block())
            FLT_MAX = 3.4028234663852886e38

            @block.sync
            def _(sp):
                sp.dma_start(ctile[:, :], dram["moe"]).then_inc(loaded, 16)

            @block.tensor
            def _(pe):
                pe.wait_ge(loaded, 16)
                pe.wait_ge(sel_made, 1)
                with pe.Fori(0, CHUNKS) as c:
                    for e in range(EXPERTS):
                        n = c * EXPERTS + e
                        pe.wait_ge(gate_out, n + 1)
                        pe.matmul(G[:, e % 2, 0:STRIP], sel[:, e * 128:(e + 1) * 128], gates[:, pick(c * STRIP, STRIP)],
                                  start=True, stop=True).then_inc(gated, 1)
                        for q in range(4):
                            pe.wait_ge(relu_a if q % 2 == 0 else relu_d, n * 2 + q // 2 + 1)
                            pe.matmul(H[:, q, 0:STRIP], part("w1", e * 512 + q * 128, 128), y[:, pick(c * STRIP, STRIP)],
                                      start=True, stop=True).then_inc(hidden, 1)
                        pe.wait_ge(read, n + 1)
                        for q in range(4):
                            pe.wait_ge(relu_a if q % 2 == 0 else relu_d, n * 2 + q // 2 + 3)
                            pe.matmul(O[:, e % 2, 0:STRIP], part("w2", e * 512 + q * 128, 128), g[:, q, :],
                                      start=(q == 0), stop=(q == 3)).then_inc(used, 1)

            @block.scalar
            def _(act):
                act.wait_ge(loaded, 16)
                with act.Fori(0, CHUNKS) as c:
                    for e in range(EXPERTS):
                        n = c * EXPERTS + e
                        act.wait_ge(gated, n + 1)
                        act.wait_ge(read, n + 1)
                        act.activation(gate[:, e % 2, :], G[:, e % 2, 0:STRIP], ACT.Copy).then_inc(gate_out, 1)
                        for q in (0, 2):
                            act.wait_ge(hidden, n * 4 + q + 1)
                            act.wait_ge(used, n * 4 + q + 1)
                            act.activation(g[:, q, :], H[:, q, 0:STRIP], ACT.Relu, bias=part("b1", e * 4 + q, 1))\
                               .then_inc(relu_a, 1)

            @block.vector
            def _(dve):
                dve.wait_ge(loaded, 16)
                for s, n in ((gate_out, 2), (relu_a, 2), (relu_d, 2), (read, 2), (used, 4)):
                    dve.sem_inc(s, n)
                dve.tensor_copy(sel[:, :], part("sel")).then_inc(sel_made, 1)
                for k, v in enumerate((1e4, -1e4, 0.0)):
                    o = dve.memset(fill[:, k, :], v)
                o.then_inc(filled, 1)
                dve.wait_ge(filled, 1)
                SUMS = EXPERTS - 1
                GUARD = 7

                def relu(n, e, q):
                    dve.wait_ge(hidden, n * 4 + q + 1)
                    dve.wait_ge(used, n * 4 + q + 1)
                    dve.tensor_scalar(g[:, q, :], H[:, q, 0:STRIP], part("b1", e * 4 + q, 1), 0.0,
                                      ALU.add, ALU.max).then_inc(relu_d, 1)

                def output(c, p, e):
                    n = c * EXPERTS + e
                    dve.wait_ge(used, n * 4 + 8)
                    dve.wait_ge(gate_out, n + 3)
                    if e == 0:
                        dve.wait_ge(finished, c * GUARD + GUARD)
                    dst = total[:, p, :] if e == 0 else term[:, :]
                    dve.scalar_tensor_tensor(out=dst, in0=O[:, e % 2, 0:STRIP], scalar=part("b2", e, 1),
                                             in1=gate[:, e % 2, :], op0=ALU.add, op1=ALU.mult).then_inc(read, 1)
                    if e:
                        dve.wait_ge(read, n + 3)
                        if e > 1:
                            dve.wait_ge(summed, c * SUMS + e - 1)
                        dve.tensor_tensor(total[:, p, :], total[:, p, :], term[:, :], ALU.add).then_inc(summed, 1)
                        dve.wait_ge(summed, c * SUMS + e)

                def finish(c, p, k):
                    t = total[:, p, :]
                    at = (c + 2) * GUARD
                    if k == 0:
                        dve.tensor_scalar(flag[:, 0, :], t, FLT_MAX, None, ALU.is_gt).then_inc(finished, 1)
                        dve.tensor_scalar(flag[:, 1, :], t, -FLT_MAX, None, ALU.is_lt).then_inc(finished, 1)
                        dve.tensor_tensor(flag[:, 2, :], t, t, ALU.not_equal).then_inc(finished, 1)
                    elif k < 4:
                        dve.wait_ge(finished, at + k + 2)
                        dve.memset(spare[:, :], 0.0)
                        dve.copy_predicated(t, flag[:, k - 1, :], fill[:, k - 1, :]).then_inc(finished, 1)
                    else:
                        dve.wait_ge(finished, at + 6)
                        strip = res[:, pick(c * STRIP, STRIP)]
                        dve.tensor_tensor(strip, strip, t, ALU.add).then_inc(finished, 1)

                def body(c0, first=False):
                    for p in range(2):
                        c = c0 + p
                        for e in range(EXPERTS):
                            n = c * EXPERTS + e
                            relu(n, e, 1)
                            if e or p or not first:
                                output(*((c, p, e - 1) if e else (c - 1, 1 - p, EXPERTS - 1)))
                            relu(n, e, 3)
                            if 1 <= e < 6 and (p or not first):
                                finish(c - 1, 1 - p, e - 1)

                dve.sem_inc(finished, 2 * GUARD)
                body(0, first=True)
                with dve.Fori(1, CHUNKS // 2) as m:
                    body(m * 2)
                output(CHUNKS - 1, 1, EXPERTS - 1)
                for k in range(5):
                    finish(CHUNKS - 1, 1, k)

    def time_mix(y, z, base):
        name = "mix"
        with phase() as ctx:
            sb = lambda n, s, d=F32: ctx.enter_context(nc.sbuf_tensor(f"{name}_{n}", s, d))
            ps = lambda n, s: ctx.enter_context(nc.psum_tensor(f"{name}_{n}", s, F32))
            sem = lambda n: nc.alloc_semaphore(f"{name}_{n}")
            ctile, part = load(ctx, name, RWKV)
            two = lambda n, w=STRIP: sb(n, [128, 2, w])
            k, v, uk, er = two("k"), two("v"), two("uk"), two("er")
            top, p, q = two("top", STRIP + 1), two("p", STRIP + 1), two("q", STRIP + 1)
            m, a, e, a2, e2, ev = two("m"), two("a"), two("e"), two("a2"), two("e2"), two("ev")
            bonus, mixed = two("bonus"), two("mixed")
            w_t, u_t = sb("w_t", [128, 1]), sb("u_t", [128, 1])
            KP, VP, RP, OP = ps("KP", [128, 2, 512]), ps("VP", [128, 2, 512]), ps("RP", [128, 2, 512]), ps("OP", [128, 2, 512])
            (loaded, set_up, k_made, v_made, r_made, k_out, v_out, gaps, exps, valued, scanned, weighted, summed, ready,
             made, added, step) = (
                sem(n) for n in ("loaded", "set_up", "k_made", "v_made", "r_made", "k_out", "v_out", "gaps", "exps",
                                 "valued", "scanned", "weighted", "summed", "ready", "made", "added", "step"))
            block = ctx.enter_context(nc.Block())

            @block.sync
            def _(sp):
                sp.dma_start(ctile[:, :], dram["rwkv"]).then_inc(loaded, 16)

            @block.tensor
            def _(pe):
                pe.wait_ge(loaded, 16)

                def inward(c, u):
                    toks = z[:, pick(c * STRIP, STRIP)]
                    pe.wait_ge(k_out, c * 2 + 2)
                    pe.matmul(KP[:, u, 0:STRIP], part("wk"), toks, start=True, stop=True).then_inc(k_made, 1)
                    pe.wait_ge(v_out, c * 2 + 2)
                    pe.matmul(VP[:, u, 0:STRIP], part("wv"), toks, start=True, stop=True).then_inc(v_made, 1)
                    pe.matmul(RP[:, u, 0:STRIP], part("wr"), toks, start=True, stop=True).then_inc(r_made, 1)

                def outward(c, u):
                    pe.wait_ge(ready, c + 3)
                    pe.wait_ge(added, c + 1)
                    pe.matmul(OP[:, u, 0:STRIP], part("wo"), mixed[:, u, :], start=True, stop=True).then_inc(made, 1)

                for u in range(2):
                    inward(u, u)
                with pe.Fori(1, CHUNKS // 2) as it:
                    for u in range(2):
                        inward(it * 2 + u, u)
                    for u in range(2):
                        outward(it * 2 - 2 + u, u)
                for u in range(2):
                    outward(CHUNKS - 2 + u, u)

            @block.scalar
            def _(act):
                act.preload_act_table(ACT.Exp)
                act.wait_ge(set_up, 2)
                with act.Fori(0, CHUNKS // 2) as it:
                    for u in range(2):
                        c = it * 2 + u
                        act.wait_ge(k_made, c + 1)
                        act.wait_ge(gaps, c * 4 + 4)
                        act.activation(k[:, u, :], KP[:, u, 0:STRIP], ACT.Copy).then_inc(k_out, 1)
                        act.activation(uk[:, u, :], KP[:, u, 0:STRIP], ACT.Identity, bias=u_t[:, :]).then_inc(k_out, 1)
                    for u in range(2):
                        c = it * 2 + u
                        act.wait_ge(ready, c + 1)
                        act.wait_ge(v_made, c + 1)
                        act.activation(v[:, u, :], VP[:, u, 0:STRIP], ACT.Copy).then_inc(v_out, 1)
                        act.wait_ge(r_made, c + 1)
                        act.activation(er[:, u, :], RP[:, u, 0:STRIP], ACT.Exp, scale=-1.0).then_inc(v_out, 1)
                    for u in range(2):
                        c = it * 2 + u
                        for n, t in enumerate((a2, e2, a, e)):
                            act.wait_ge(gaps, c * 4 + n + 9)
                            act.activation(t[:, u, :], t[:, u, :], ACT.Exp).then_inc(exps, 1)

            @block.gpsimd
            def _(pool):
                with pool.Fori(0, CHUNKS // 2) as it:
                    for u in range(2):
                        c = it * 2 + u
                        pool.wait_ge(v_out, c * 2 + 6)
                        pool.wait_ge(exps, c * 4 + 4)
                        pool.tensor_tensor(ev[:, u, :], e2[:, u, :], v[:, u, :], ALU.mult).then_inc(valued, 1)
                        pool.wait_ge(summed, c + 1)
                        pool.tensor_tensor(bonus[:, u, :], e[:, u, :], v[:, u, :], ALU.mult).then_inc(weighted, 1)
                    for u in range(2):
                        c = it * 2 + u
                        pool.wait_ge(scanned, c + 1)
                        pool.tensor_tensor(m[:, u, :], a[:, u, :], p[:, u, 0:STRIP], ALU.mult).then_inc(weighted, 1)
                        pool.wait_ge(weighted, it * 4 + 3 + u)
                        pool.tensor_tensor(m[:, u, :], m[:, u, :], bonus[:, u, :], ALU.add).then_inc(summed, 1)

            @block.vector
            def _(dve):
                dve.wait_ge(loaded, 16)
                for s, n in ((added, 2), (ready, 2), (summed, 2), (k_out, 4), (v_out, 4), (gaps, 8)):
                    dve.sem_inc(s, n)
                dve.tensor_scalar(w_t[:, :], part("decay"), 1.0 / TOK, None, ALU.mult).then_inc(set_up, 1)
                dve.tensor_scalar(u_t[:, :], part("first"), 1.0 / TOK, None, ALU.mult).then_inc(set_up, 1)
                dve.wait_ge(set_up, 2)
                FRONT, BACK = 4, 9

                def front(c, u, at):
                    dve.wait_ge(step, at)
                    dve.wait_ge(k_out, c * 2 + 6)
                    now, nxt = top[:, u, 0:STRIP], top[:, u, 1:STRIP + 1]
                    dve.tensor_tensor_scan(nxt, w_t[:, :].broadcast_to([128, STRIP]), k[:, u, :], top[:, u, 0:1],
                                           ALU.add, ALU.max).then_inc(step, 1)
                    dve.wait_ge(step, at + 1)
                    dve.tensor_copy(top[:, 1 - u, 0:1], top[:, u, STRIP:STRIP + 1]).then_inc(step, 1)
                    dve.scalar_tensor_tensor(out=a2[:, u, :], in0=now, scalar=w_t[:, :], in1=nxt, op0=ALU.add,
                                             op1=ALU.subtract).then_inc(gaps, 1)
                    dve.tensor_tensor(e2[:, u, :], k[:, u, :], nxt, ALU.subtract).then_inc(gaps, 1)
                    dve.tensor_tensor(m[:, u, :], now, uk[:, u, :], ALU.max).then_inc(step, 1)
                    dve.wait_ge(step, at + 3)
                    dve.tensor_tensor(a[:, u, :], now, m[:, u, :], ALU.subtract).then_inc(gaps, 1)
                    dve.tensor_tensor(e[:, u, :], uk[:, u, :], m[:, u, :], ALU.subtract).then_inc(gaps, 1)
                    dve.wait_ge(gaps, c * 4 + 12)
                    dve.sem_inc(step, 1)

                def back(c, u, at):
                    def chained(ins, n):
                        ins.then_inc(step, 1)
                        dve.wait_ge(step, at + n)
                    dve.wait_ge(v_out, c * 2 + 6)
                    dve.wait_ge(exps, c * 4 + 4)
                    chained(dve.tensor_tensor_scan(q[:, u, 1:STRIP + 1], a2[:, u, :], e2[:, u, :], q[:, u, 0:1],
                                                   ALU.mult, ALU.add), 1)
                    dve.wait_ge(valued, c + 1)
                    dve.tensor_tensor_scan(p[:, u, 1:STRIP + 1], a2[:, u, :], ev[:, u, :], p[:, u, 0:1],
                                           ALU.mult, ALU.add).then_inc(scanned, 1)
                    dve.tensor_copy(q[:, 1 - u, 0:1], q[:, u, STRIP:STRIP + 1]).then_inc(step, 1)
                    dve.wait_ge(scanned, c + 1)
                    dve.tensor_copy(p[:, 1 - u, 0:1], p[:, u, STRIP:STRIP + 1]).then_inc(step, 1)
                    chained(dve.tensor_tensor(a2[:, u, :], a[:, u, :], q[:, u, 0:STRIP], ALU.mult), 4)
                    chained(dve.tensor_tensor(a2[:, u, :], a2[:, u, :], e[:, u, :], ALU.add), 5)
                    chained(dve.scalar_tensor_tensor(out=a2[:, u, :], in0=er[:, u, :], scalar=1.0, in1=a2[:, u, :],
                                                     op0=ALU.add, op1=ALU.mult), 6)
                    chained(dve.reciprocal(e2[:, u, :], a2[:, u, :]), 7)
                    dve.wait_ge(summed, c + 3)
                    chained(dve.tensor_tensor(mixed[:, u, :], m[:, u, :], e2[:, u, :], ALU.mult), 8)
                    dve.sem_inc(step, 1)
                    dve.sem_inc(ready, 1)

                def add(c, u):
                    dve.wait_ge(made, c + 1)
                    strip = y[:, pick(c * STRIP, STRIP)]
                    dve.tensor_tensor(strip, OP[:, u, 0:STRIP], strip, ALU.add).then_inc(added, 1)

                PER = 2 * (FRONT + BACK)
                with dve.Fori(0, HALF_IMGS) as img:
                    start = img * (PER * (STRIPS // 2) + 3)
                    dve.memset(top[:, 0, 0:1], -1e38).then_inc(step, 1)
                    dve.memset(p[:, 0, 0:1], 0.0).then_inc(step, 1)
                    dve.memset(q[:, 0, 0:1], 0.0).then_inc(step, 1)
                    with dve.Fori(0, STRIPS // 2) as i:
                        at = start + 3 + i * PER
                        for u in range(2):
                            front(img * STRIPS + i * 2 + u, u, at + FRONT * u)
                        for u in range(2):
                            back(img * STRIPS + i * 2 + u, u, at + 2 * FRONT + BACK * u)
                        for u in range(2):
                            add(img * STRIPS + i * 2 + u, u)

    def channel_mix(res, y, z):
        name = "cmix"
        with phase() as ctx:
            sb = lambda n, s, d=F32: ctx.enter_context(nc.sbuf_tensor(f"{name}_{n}", s, d))
            sem = lambda n: nc.alloc_semaphore(f"{name}_{n}")
            ctile, part = load(ctx, name, RWKV_FFN)
            g = sb("g", [128, 4, STRIP])
            g2 = sb("g2", [128, 4, STRIP])
            sig = sb("sig", [128, 2, STRIP])
            t = sb("t", [128, 2, STRIP])
            H = ctx.enter_context(nc.psum_tensor("cmix_H", [128, 4, 512], F32))
            R = ctx.enter_context(nc.psum_tensor("cmix_R", [128, 2, 512], F32))
            O = ctx.enter_context(nc.psum_tensor("cmix_O", [128, 2, 512], F32))
            loaded, hidden, relued, squared, used, r_made, sig_made, step, done = (
                sem(n) for n in ("loaded", "hidden", "relued", "squared", "used", "r_made", "sig_made", "step", "done"))
            block = ctx.enter_context(nc.Block())

            @block.sync
            def _(sp):
                sp.dma_start(ctile[:, :], dram["rwkv_ffn"]).then_inc(loaded, 16)

            @block.tensor
            def _(pe):
                pe.wait_ge(loaded, 16)
                with pe.Fori(0, CHUNKS // 2) as it:
                    for u in range(2):
                        c = it * 2 + u
                        toks = z[:, pick(c * STRIP, STRIP)]
                        pe.wait_ge(done, c + 1)
                        pe.matmul(R[:, u, 0:STRIP], part("wr"), toks, start=True, stop=True).then_inc(r_made, 1)
                        for q in range(4):
                            pe.wait_ge(relued, c * 4 + q + 1)
                            pe.matmul(H[:, q, 0:STRIP], part("w1", q * 128, 128), toks, start=True, stop=True)\
                              .then_inc(hidden, 1)
                        for q in range(4):
                            pe.wait_ge(squared, c * 4 + q + 1)
                            pe.matmul(O[:, u, 0:STRIP], part("w2", q * 128, 128), g2[:, q, :],
                                      start=(q == 0), stop=(q == 3)).then_inc(used, 1)

            @block.scalar
            def _(act):
                act.preload_act_table(ACT.Sigmoid)
                with act.Fori(0, CHUNKS // 2) as it:
                    for u in range(2):
                        c = it * 2 + u
                        act.wait_ge(r_made, c + 1)
                        act.activation(sig[:, u, :], R[:, u, 0:STRIP], ACT.Sigmoid).then_inc(sig_made, 1)
                        for q in range(4):
                            act.wait_ge(hidden, c * 4 + q + 1)
                            act.activation(g[:, q, :], H[:, q, 0:STRIP], ACT.Relu).then_inc(relued, 1)

            @block.vector
            def _(dve):
                dve.sem_inc(relued, 4)
                dve.sem_inc(used, 4)
                dve.sem_inc(done, 2)
                with dve.Fori(0, CHUNKS // 2) as it:
                    for u in range(2):
                        c = it * 2 + u
                        for q in range(4):
                            dve.wait_ge(relued, c * 4 + q + 5)
                            dve.wait_ge(used, c * 4 + q + 1)
                            dve.tensor_tensor(g2[:, q, :], g[:, q, :], g[:, q, :], ALU.mult).then_inc(squared, 1)
                        strip = slice(None), pick(c * STRIP, STRIP)
                        dve.wait_ge(used, c * 4 + 8)
                        dve.wait_ge(sig_made, c + 1)
                        dve.tensor_tensor(t[:, u, :], O[:, u, 0:STRIP], sig[:, u, :], ALU.mult).then_inc(step, 1)
                        dve.wait_ge(step, c * 2 + 1)
                        dve.tensor_tensor(t[:, u, :], t[:, u, :], y[strip], ALU.add).then_inc(step, 1)
                        dve.wait_ge(step, c * 2 + 2)
                        dve.tensor_tensor(res[strip], res[strip], t[:, u, :], ALU.add).then_inc(done, 1)

    def routed_mlp(res, y, base):
        name = "rt"
        with phase() as ctx:
            sb = lambda n, s, d=F32: ctx.enter_context(nc.sbuf_tensor(f"{name}_{n}", s, d))
            ps = lambda n, s: ctx.enter_context(nc.psum_tensor(f"{name}_{n}", s, F32))
            sem = lambda n: nc.alloc_semaphore(f"{name}_{n}")
            ctile, part = load(ctx, name, ROUTED)
            route = sb("route", [1, 2 * CHUNKS], I32)
            wsel = sb("wsel", [128, 2, 2, ROUTE_LAYERS, RH])
            bsel = sb("bsel", [128, 2, 2, ROUTE_LAYERS])
            h = sb("h", [128, 2, 2, 1 + ROUTE_LAYERS, STRIP])
            P = ps("P", [128, 2, 2, 512])
            O = ps("O", [128, 2, 512])
            loaded, shared_made, weights, made, relued, out_made, added = (
                sem(n) for n in ("loaded", "shared_made", "weights", "made", "relued", "out_made", "added"))
            block = ctx.enter_context(nc.Block())
            LAYERS = 1 + ROUTE_LAYERS

            @block.sync
            def _(sp):
                sp.dma_start(ctile[:, :], dram["routed"]).then_inc(loaded, 16)
                sp.dma_start(route[:, :], dram["route"]).then_inc(loaded, 16)

            @block.tensor
            def _(pe):
                pe.wait_ge(loaded, 32)
                with pe.Fori(0, CHUNKS // 2) as it:
                    for l in range(LAYERS):
                        for u in range(2):
                            c = it * 2 + u
                            if l == 0:
                                pe.wait_ge(added, c + 1)
                            for s in range(2):
                                pe.wait_ge(relued, ((it * LAYERS + l) * 2 + u) * 2 + s + 1)
                                if l == 0:
                                    lhs, rhs = part("wi", s * RH, RH), y[:, pick(c * STRIP, STRIP)]
                                else:
                                    pe.wait_ge(weights, c * 4 + s * 2 + l)
                                    lhs, rhs = wsel[:, u, s, l - 1, :], h[:, u, s, l - 1, :]
                                pe.matmul(P[:, s, u, 0:STRIP], lhs, rhs, start=True, stop=True).then_inc(made, 1)
                    for u in range(2):
                        for s in range(2):
                            pe.wait_ge(relued, (it * LAYERS + LAYERS) * 4 + u * 2 + s + 1)
                            mm = pe.matmul(O[s * C:(s + 1) * C, u, 0:STRIP], part("wo"), h[:, u, s, LAYERS - 1, :],
                                           start=True, stop=True)
                        mm.then_inc(out_made, 1)

            @block.scalar
            def _(act):
                act.wait_ge(loaded, 32)
                with act.Fori(0, CHUNKS // 2) as it:
                    for l in range(LAYERS):
                        for u in range(2):
                            for s in range(2):
                                act.wait_ge(made, ((it * LAYERS + l) * 2 + u) * 2 + s + 1)
                                bias = part("bi") if l == 0 else bsel[:, u, s, l - 1:l]
                                act.activation(h[:, u, s, l, :], P[:, s, u, 0:STRIP], ACT.Relu, bias=bias)\
                                   .then_inc(relued, 1)

            @block.vector
            def _(dve):
                dve.wait_ge(loaded, 32)
                dve.sem_inc(added, 2)
                dve.sem_inc(relued, 4)
                for l in range(ROUTE_LAYERS):
                    ws = part("ws", l * RH, RH)
                    dve.tensor_tensor(ws, ws, base("ident"), ALU.add).then_inc(shared_made, 1)
                dve.wait_ge(shared_made, ROUTE_LAYERS)
                at_w, at_b = ROUTED["wr"][0], ROUTED["br"][0]

                def select(c, u):
                    for s in range(2):
                        r = dve.value_load(route[0:1, pick(c + s * CHUNKS, 1)], min_val=0, max_val=ROUTES - 1)
                        for l in range(ROUTE_LAYERS):
                            dve.tensor_tensor(bsel[:, u, s, l:l + 1], part("bs", l, 1),
                                              ctile[:, pick(r + (at_b + l * ROUTES), 1)], ALU.add)
                            dve.tensor_tensor(wsel[:, u, s, l, :], part("ws", l * RH, RH),
                                              ctile[:, pick(r * RH + (at_w + l * ROUTES * RH), RH)], ALU.add)\
                               .then_inc(weights, 1)

                with dve.Fori(0, CHUNKS // 2) as it:
                    for u in range(2):
                        select(it * 2 + u, u)
                    for u in range(2):
                        c = it * 2 + u
                        dve.wait_ge(out_made, c + 1)
                        strip = res[:, pick(c * STRIP, STRIP)]
                        dve.scalar_tensor_tensor(out=strip, in0=O[:, u, 0:STRIP], scalar=part("bo"), in1=strip,
                                                 op0=ALU.add, op1=ALU.add).then_inc(added, 1)

    with ExitStack() as ctx:
        base_tile, base = load(ctx, "base", BASE)
        X = ctx.enter_context(nc.sbuf_tensor("X", [128, COLS], F32))
        Y = ctx.enter_context(nc.sbuf_tensor("Y", [128, COLS], F32))
        entered = ctx.enter_context(nc.semaphore("entered"))
        stored = ctx.enter_context(nc.semaphore("stored"))
        with nc.Block() as block:
            @block.sync
            def _(sp):
                sp.dma_start(base_tile[:, :], dram["base"]).then_inc(entered, 16)
                sp.dma_start(Y[:, 0:TOK], dram["patches"]).then_inc(entered, 16)
                sp.wait_ge(entered, 32)

        def steps():
            res, tmp = X, Y
            patch_embed(tmp, res, base)
            layernorm("ln_pe", res, res, base, base("pe_g"), base("pe_nb"))
            if STOP <= 0:
                return res
            for b in range(2):
                if b:
                    roll("roll1", res, tmp, SHIFT)
                    res, tmp = tmp, res
                layernorm(f"ln1_{b}", res, tmp, base, base("n1g", b, 1), base("n1b", b, 1))
                window_attention(b, res, tmp, base)
                if STOP <= 1:
                    return res
                layernorm(f"ln2_{b}", res, tmp, base, base("n2g", b, 1), base("n2b", b, 1))
                mlp(b, res, tmp, base)
                if STOP <= 2:
                    return res
            roll("roll2", res, tmp, SIDE - SHIFT)
            res, tmp = tmp, res
            if STOP <= 3:
                return res
            layernorm("ln_att", res, tmp, base)
            image_attention(res, tmp, base)
            if STOP <= 4:
                return res
            layernorm("ln_moe", res, tmp, base)
            with nc.sbuf_tensor("gates", [128, COLS], BF16) as gates:
                routing(tmp, gates, base)
                experts(res, tmp, gates)
            if STOP <= 5:
                return res
            layernorm("ln_rwkv", res, tmp, base)
            with nc.sbuf_tensor("Z", [128, COLS], F32) as Z:
                layernorm("ln_mix", tmp, Z, base, base("rg1"), base("rb1"))
                time_mix(tmp, Z, base)
                layernorm("ln_cmix", tmp, Z, base, base("rg2"), base("rb2"))
                channel_mix(res, tmp, Z)
            if STOP <= 6:
                return res
            layernorm("ln_rt", res, tmp, base)
            routed_mlp(res, tmp, base)
            return res

        res = steps()
        with nc.Block() as block:
            @block.sync
            def _(sp):
                sp.dma_start(out, res[:, :]).then_inc(stored, 16)
                sp.wait_ge(stored, 16)


def halves(v):
    return np.concatenate([v, v])


def diagonal(w):
    a, b = w.shape
    o = np.zeros((128, 2 * b), np.float32)
    o[0:a, 0:b] = w
    o[64:64 + a, b:] = w
    return o


def groups_of_hidden(w1, w2):
    up = np.concatenate([diagonal(w1[:, q * 64:(q + 1) * 64]) for q in range(4)], 1)
    down = np.concatenate([diagonal(w2[q * 64:(q + 1) * 64]) for q in range(4)], 1)
    return up, down


def pack(cols, **parts):
    o = np.zeros((128, cols["_"][1]), np.float32)
    for name, v in parts.items():
        at, w = cols[name]
        v = np.asarray(v, np.float32)
        v = v[:, None] if v.ndim == 1 else v
        assert v.shape[1] == w, (name, v.shape, w)
        o[:v.shape[0], at:at + w] = v
    return o


def lay_out(i):
    i = {k: np.asarray(v) for k, v in i.items()}
    p = i["x"].reshape(2, HALF_IMGS, SIDE, 4, SIDE, 4).transpose(1, 0, 3, 5, 2, 4).reshape(128, TOK)
    mean = np.kron(np.eye(2), np.full((C, C), 1.0 / C))
    bd = diagonal
    two = lambda v: np.stack([halves(v[0]), halves(v[1])], 1)
    w16 = i["L0_tok_pe_w"].reshape(C, 16).T
    pe = np.zeros((2 * HALF_IMGS, 16, 2 * HALF_IMGS, C), np.float32)
    for k in range(2 * HALF_IMGS):
        pe[k, :, k] = w16
    base = pack(BASE, ident=np.eye(128), center=np.eye(128) - mean, mean=mean, eps=np.full(128, EPS),
                pe_w=pe.reshape(128, -1), pe_b=halves(i["L0_tok_pe_b"]), pe_g=halves(i["L0_tok_pe_ng"]), pe_nb=halves(i["L0_tok_pe_nb"]),
                n1g=two(i["L0_tok_n1g"]), n1b=two(i["L0_tok_n1b"]), n2g=two(i["L0_tok_n2g"]), n2b=two(i["L0_tok_n2b"]),
                rg1=halves(i["L1_attn_g1"]), rb1=halves(i["L1_attn_b1"]), rg2=halves(i["L1_attn_g2"]), rb2=halves(i["L1_attn_b2"]))
    swin, mlps, rpbs = [], [], []
    yx = np.stack(np.meshgrid(np.arange(WS), np.arange(WS), indexing="ij")).reshape(2, -1)
    rel = (yx[:, :, None] - yx[:, None, :]) + WS - 1
    rpi = rel[0] * (2 * WS - 1) + rel[1]
    headmask = np.zeros((128, HEADS), np.float32)
    for k in range(128):
        headmask[k, (k % 64) // HD] = 1.0
    for b in range(2):
        wq, wk, wv = (i["L0_tok_qkv_w"][b, n * C:(n + 1) * C].T for n in range(3))
        bq, bk, bv = (halves(i["L0_tok_qkv_b"][b, n * C:(n + 1) * C]) for n in range(3))
        swin.append(pack(SWIN, wq=bd(wq), wk=bd(wk), wv=np.concatenate([wv, wv]), wp=bd(i["L0_tok_proj_w"][b].T),
                         bq=bq, bk=bk, bv=bv, bp=halves(i["L0_tok_proj_b"][b]), headmask=headmask))
        up, down = groups_of_hidden(i["L0_tok_w1"][b].T, i["L0_tok_w2"][b].T)
        b1 = i["L0_tok_b1"][b].reshape(4, 64)
        mlps.append(pack(MLP, w1=up, w2=down, b1=np.concatenate([b1.T, b1.T]), b2=halves(i["L0_tok_b2"][b])))
        t = i["L0_tok_rpb"][b][rpi].transpose(0, 2, 1).reshape(WIN, HEADS * WIN)
        r = np.zeros((128, HEADS * WIN), np.float32)
        r[0:WIN] = t
        r[64:64 + WIN] = t
        rpbs.append(r)
    region = np.zeros((SIDE, SIDE), np.int32)
    n = 0
    for a in (slice(0, -WS), slice(-WS, -SHIFT), slice(-SHIFT, None)):
        for c in (slice(0, -WS), slice(-WS, -SHIFT), slice(-SHIFT, None)):
            n += 1
            region[a, c] = n
    mw = region.reshape(NW, WS, NW, WS).transpose(0, 2, 1, 3).reshape(NW, NW, WIN)
    masks = np.zeros((128, 3, HEADS, WIN), np.float32)
    for k, (a, c) in enumerate(((0, NW - 1), (NW - 1, 0), (NW - 1, NW - 1))):
        m = np.where(mw[a, c][None, :] != mw[a, c][:, None], -100.0, 0.0).astype(np.float32)
        masks[0:WIN, k] = m[:, None, :]
        masks[64:64 + WIN, k] = m[:, None, :]
    wide = lambda a: np.concatenate([a, np.zeros((128, 112), np.float32)], 1)
    twice = lambda w: diagonal(np.concatenate([w, w], 1))
    att = pack(ATT, wq=twice(i["L0_attn_Wq"]), wk=twice(i["L0_attn_Wk"]), wv=bd(i["L0_attn_Wv"]))
    gate = pack(GATE, gw=wide(bd(i["L0_ffn_gate_w"])), gb=wide(np.tile(i["L0_ffn_gate_b"], (128, 2))),
                tri=np.triu(np.ones((LNT, LNT))), ones=np.ones((LNT, LNT)))
    ups, downs, b1s, sel = [], [], [], np.zeros((3, 16, EXPERTS, 128), np.float32)
    for e in range(EXPERTS):
        up, down = groups_of_hidden(i["L0_ffn_w1"][e], i["L0_ffn_w2"][e])
        ups.append(up)
        downs.append(down)
        b = i["L0_ffn_b1"][e].reshape(4, 64).T
        b1s.append(np.concatenate([b, b]))
        for h in range(2):
            sel[:, 8 * h + e, e, 64 * h:64 * h + 64] = 1.0
    moe = pack(MOE, w1=np.concatenate(ups, 1), w2=np.concatenate(downs, 1), b1=np.concatenate(b1s, 1),
               b2=np.stack([halves(v) for v in i["L0_ffn_b2"]], 1), sel=sel.reshape(48, -1))
    rwkv = pack(RWKV, wk=bd(i["L1_attn_Wk"]), wv=bd(i["L1_attn_Wv"]), wr=bd(i["L1_attn_Wr"]), wo=bd(i["L1_attn_Wo"]),
                decay=halves(i["L1_attn_spatial_decay"]), first=halves(i["L1_attn_spatial_first"]))
    up, down = groups_of_hidden(i["L1_attn_Wk_ffn"], i["L1_attn_Wv_ffn"])
    rwkv_ffn = pack(RWKV_FFN, wr=bd(i["L1_attn_Wr_ffn"]), w1=up, w2=down)
    wi = np.zeros((128, 2 * RH), np.float32)
    wi[0:64, 0:RH] = i["L1_ffn_Wi"].T
    wi[64:128, RH:] = i["L1_ffn_Wi"].T
    routed = pack(ROUTED, wi=wi, bi=i["L1_ffn_bi"], wr=i["L1_ffn_Wr"].transpose(3, 0, 1, 2).reshape(128, -1),
                  br=i["L1_ffn_br"].transpose(2, 0, 1).reshape(128, -1),
                  ws=i["L1_ffn_Ws"][:, 0].transpose(2, 0, 1).reshape(128, -1), bs=i["L1_ffn_bs"][:, 0].T,
                  wo=i["L1_ffn_Wo"].T, bo=halves(i["L1_ffn_bo"]))
    return {"att": att, "gate": gate, "moe": moe, "rwkv": rwkv, "rwkv_ffn": rwkv_ffn, "routed": routed,
            "route": i["L1_ffn_route_id"].reshape(1, -1), "patches": p, "base": base, "swin": np.stack(swin), "mlp": np.stack(mlps), "rpb": np.stack(rpbs),
            "masks": masks.reshape(128, 3, HEADS * WIN)}


def kernel(**inputs):
    import concourse.bacc as _bacc
    from concourse import mybir as _mybir
    from concourse.bass_utils import run_bass_kernel_spmd as _run

    nc = _bacc.Bacc("TRN2", target_bir_lowering=False, num_devices=1)
    arrays = {f"in_{k}": np.ascontiguousarray(v) for k, v in lay_out(inputs).items()}
    dram = {k[3:]: nc.dram_tensor(k, a.shape, _mybir.dt.from_np(a.dtype), kind="ExternalInput").ap()
            for k, a in arrays.items()}
    out = nc.dram_tensor("out", [128, COLS], _mybir.dt.float32, kind="ExternalOutput").ap()
    build(nc, dram, out)
    r = _run(nc, [arrays], core_ids=[0])
    got = np.asarray(r.results[0]["out"])
    return got.reshape(2, C, HALF_IMGS, TOK).transpose(0, 2, 3, 1).reshape(IMGS, TOK, C)
```
